# Optimizing a Trainium2 kernel written in Bass

```python
import numpy as np
import jax
import jax.numpy as jnp

def _softmax(x, axis=-1):
    return jax.nn.softmax(x, axis=axis)

def _gelu(x):
    return jax.nn.gelu(x, approximate=True)

def _silu(x):
    return jax.nn.silu(x)

def _sigmoid(x):
    return jax.nn.sigmoid(x)

def _layernorm(x, axis=-1, eps=1e-05):
    m = jnp.mean(x, axis=axis, keepdims=True)
    v = jnp.var(x, axis=axis, keepdims=True)
    return (x - m) / jnp.sqrt(v + eps)

def _scatter_add(tgt, idx, src, axis=0):
    return tgt.at[idx].add(src)

def _segment_sum(src, seg, n):
    return jax.ops.segment_sum(src, seg, n)
kernel_name = 'mk_metaformer_d4_conv_nhwc768_r4_90e6b5'

def setup_inputs(seed: int=0):
    np.random.seed(seed)
    _w = jnp.asarray

    def _rec_inputs():
        import jax
        import jax.numpy as jnp
        _gk = jax.random.key(seed)
        x = -0.0005963 + 1.001 * jax.random.normal(jax.random.fold_in(_gk, 1), (1, 16, 16, 192), jnp.float32)
        return x
    x = _rec_inputs()

    def _L0_conv_setup():
        import jax, jax.numpy as jnp
        import numpy as np

        def get_rel_pos(q_size, k_size, rel_pos):
            q_coords = jnp.arange(q_size)[:, None]
            k_coords = jnp.arange(k_size)[None, :]
            rel = q_coords - k_coords + (k_size - 1)
            return rel_pos[rel]
        key = jax.random.key(seed)
        ks = jax.random.split(key, 11)
        B, H, W, C = (1, 16, 16, 192)
        nH, hd = (12, 16)
        s = 0.02
        return {'x': jax.random.normal(ks[0], (B, H, W, C), jnp.float32), 'wq': jax.random.normal(ks[1], (nH, hd, C), jnp.float32) * s, 'bq': jax.random.normal(ks[2], (nH, hd), jnp.float32) * s, 'wk': jax.random.normal(ks[3], (nH, hd, C), jnp.float32) * s, 'bk': jax.random.normal(ks[4], (nH, hd), jnp.float32) * s, 'wv': jax.random.normal(ks[5], (nH, hd, C), jnp.float32) * s, 'bv': jax.random.normal(ks[6], (nH, hd), jnp.float32) * s, 'rel_pos_h': jax.random.normal(ks[7], (2 * H - 1, hd), jnp.float32) * s, 'rel_pos_w': jax.random.normal(ks[8], (2 * W - 1, hd), jnp.float32) * s, 'proj_w': jax.random.normal(ks[9], (nH * hd, nH * hd), jnp.float32) * s, 'proj_b': jax.random.normal(ks[10], (nH * hd,), jnp.float32) * s}
    _L0_conv_all = _L0_conv_setup()
    _L0_conv_in = {k: v for k, v in _L0_conv_all.items() if k in ('wq', 'bq', 'wk', 'bk', 'wv', 'bv', 'rel_pos_h', 'rel_pos_w', 'proj_w', 'proj_b')}
    del _L0_conv_all

    def _L0_ffn_setup():
        import jax, jax.numpy as jnp
        import numpy as np
        TOP_K = 2
        key = jax.random.key(seed)
        ks = jax.random.split(key, 5)
        B, T, C, H, E = (4, 256, 192, 768, 8)
        x = jax.random.normal(ks[0], (B, T, C), dtype=jnp.float32)
        Wg = jax.random.normal(ks[1], (C, E), dtype=jnp.float32) * 0.02
        W1 = jax.random.normal(ks[2], (E, C, H), dtype=jnp.float32) * (1.0 / np.sqrt(C))
        b1 = jnp.zeros((E, H), dtype=jnp.float32)
        W2 = jax.random.normal(ks[3], (E, H, C), dtype=jnp.float32) * (1.0 / np.sqrt(H))
        b2 = jnp.zeros((E, C), dtype=jnp.float32)
        return {'x': x, 'Wg': Wg, 'W1': W1, 'b1': b1, 'W2': W2, 'b2': b2}
    _L0_ffn_all = _L0_ffn_setup()
    _L0_ffn_in = {k: v for k, v in _L0_ffn_all.items() if k in ('Wg', 'W1', 'b1', 'W2', 'b2')}
    del _L0_ffn_all

    def _L1_conv_setup():
        import jax, jax.numpy as jnp
        import numpy as np
        B, H, W, DIM = (8, 32, 32, 192)
        NUM_HEADS = 12
        HEAD_DIM = DIM // NUM_HEADS
        key = jax.random.key(seed)
        ks = jax.random.split(key, 7)
        x = jax.random.normal(ks[0], (B, H, W, DIM), dtype=jnp.float32)
        qkv_w = jax.random.normal(ks[1], (DIM, 3 * DIM), dtype=jnp.float32) * 0.02
        qkv_b = jnp.zeros((3 * DIM,), dtype=jnp.float32)
        proj_w = jax.random.normal(ks[2], (DIM, DIM), dtype=jnp.float32) * 0.02
        proj_b = jnp.zeros((DIM,), dtype=jnp.float32)
        rel_pos_h = jax.random.normal(ks[3], (2 * H - 1, HEAD_DIM), dtype=jnp.float32) * 0.02
        rel_pos_w = jax.random.normal(ks[4], (2 * W - 1, HEAD_DIM), dtype=jnp.float32) * 0.02
        return {'x': x, 'qkv_w': qkv_w, 'qkv_b': qkv_b, 'proj_w': proj_w, 'proj_b': proj_b, 'rel_pos_h': rel_pos_h, 'rel_pos_w': rel_pos_w}
    _L1_conv_all = _L1_conv_setup()
    _L1_conv_in = {k: v for k, v in _L1_conv_all.items() if k in ('qkv_w', 'qkv_b', 'proj_w', 'proj_b', 'rel_pos_h', 'rel_pos_w')}
    del _L1_conv_all

    def _L1_ffn_setup():
        import jax, jax.numpy as jnp
        import numpy as np
        N_EXPERTS = 8
        TOPK = 2
        B, S, H, F = (8, 512, 192, 768)
        key = jax.random.key(seed)
        ks = jax.random.split(key, 4)
        return {'hidden_states': jax.random.normal(ks[0], (B, S, H), dtype=jnp.float32), 'Wr': jax.random.normal(ks[1], (H, N_EXPERTS), dtype=jnp.float32) * 0.02, 'br': jnp.zeros((N_EXPERTS,), dtype=jnp.float32), 'Wfc': jax.random.normal(ks[2], (N_EXPERTS, H, F), dtype=jnp.float32) * 0.02, 'bfc': jnp.zeros((N_EXPERTS, F), dtype=jnp.float32), 'Wproj': jax.random.normal(ks[3], (N_EXPERTS, F, H), dtype=jnp.float32) * 0.02, 'bproj': jnp.zeros((N_EXPERTS, H), dtype=jnp.float32)}
    _L1_ffn_all = _L1_ffn_setup()
    _L1_ffn_in = {k: v for k, v in _L1_ffn_all.items() if k in ('Wr', 'br', 'Wfc', 'bfc', 'Wproj', 'bproj')}
    del _L1_ffn_all

    def _L2_conv_setup():
        import jax, jax.numpy as jnp
        import numpy as np
        NUM_HEADS = 12

        def _rel_pos_table(size, rel_pos):
            coords = jnp.arange(size)[:, None] - jnp.arange(size)[None, :] + (size - 1)
            return rel_pos[coords]
        key = jax.random.key(seed)
        ks = jax.random.split(key, 5)
        B, H, W, C = (8, 32, 32, 192)
        hd = C // NUM_HEADS
        x = jax.random.normal(ks[0], (B, H, W, C), dtype=jnp.float32)
        qkv_w = jax.random.normal(ks[1], (C, 3 * C), dtype=jnp.float32) * 0.02
        qkv_b = jnp.zeros((3 * C,), dtype=jnp.float32)
        proj_w = jax.random.normal(ks[2], (C, C), dtype=jnp.float32) * 0.02
        proj_b = jnp.zeros((C,), dtype=jnp.float32)
        rel_pos_h = jax.random.normal(ks[3], (2 * H - 1, hd), dtype=jnp.float32) * 0.02
        rel_pos_w = jax.random.normal(ks[4], (2 * W - 1, hd), dtype=jnp.float32) * 0.02
        return {'x': x, 'qkv_w': qkv_w, 'qkv_b': qkv_b, 'proj_w': proj_w, 'proj_b': proj_b, 'rel_pos_h': rel_pos_h, 'rel_pos_w': rel_pos_w}
    _L2_conv_all = _L2_conv_setup()
    _L2_conv_in = {k: v for k, v in _L2_conv_all.items() if k in ('qkv_w', 'qkv_b', 'proj_w', 'proj_b', 'rel_pos_h', 'rel_pos_w')}
    del _L2_conv_all

    def _L2_ffn_setup():
        import jax, jax.numpy as jnp
        import numpy as np
        import math
        N_HEAD = 12
        N_EXP = 8
        TOP_K = 2
        EVAL_CAPACITY = 1.0
        MIN_CAPACITY = 4
        EPS = 1e-05

        def layer_norm(x, w):
            mu = jnp.mean(x, axis=-1, keepdims=True)
            var = jnp.var(x, axis=-1, keepdims=True)
            return (x - mu) / jnp.sqrt(var + EPS) * w

        def attention(x, c_attn_w, c_proj_w):
            B, T, C = x.shape
            H, D = (N_HEAD, C // N_HEAD)
            qkv = x @ c_attn_w.T
            q, k, v = jnp.split(qkv, 3, axis=-1)
            q = q.reshape(B, T, H, D).transpose(0, 2, 1, 3)
            k = k.reshape(B, T, H, D).transpose(0, 2, 1, 3)
            v = v.reshape(B, T, H, D).transpose(0, 2, 1, 3)
            scores = jnp.einsum('bhqd,bhkd->bhqk', q, k) * (1.0 / math.sqrt(D))
            causal = jnp.tril(jnp.ones((T, T), dtype=bool))
            scores = jnp.where(causal, scores, -jnp.inf)
            att = jax.nn.softmax(scores, axis=-1)
            y = jnp.einsum('bhqk,bhkd->bhqd', att, v)
            y = y.transpose(0, 2, 1, 3).reshape(B, T, C)
            return y @ c_proj_w.T

        def get_capacity(num_tokens):
            cap = int(math.floor(TOP_K * EVAL_CAPACITY * num_tokens / N_EXP))
            cap += cap % 2
            return max(cap, MIN_CAPACITY)

        def moe(x_flat, w_g, c_fc, c_proj_e):
            n_tok, C = x_flat.shape
            logits = x_flat @ w_g.T
            top_vals, top_idx = jax.lax.top_k(logits, TOP_K)
            rows = jnp.arange(n_tok)[:, None]
            masked = jnp.full_like(logits, -jnp.inf).at[rows, top_idx].set(top_vals)
            probs = jax.nn.softmax(masked, axis=-1)
            cap = get_capacity(n_tok)
            flat_e = top_idx.reshape(-1)
            onehot = jax.nn.one_hot(flat_e, N_EXP, dtype=jnp.int32)
            pos = jnp.cumsum(onehot, axis=0) - onehot
            slot = jnp.take_along_axis(pos, flat_e[:, None], axis=1)[:, 0]
            valid = slot < cap
            tok = jnp.repeat(jnp.arange(n_tok), TOP_K)
            slot_c = jnp.where(valid, slot, cap)
            sec = jnp.zeros((n_tok, N_EXP, cap + 1), dtype=x_flat.dtype)
            sec = sec.at[tok, flat_e, slot_c].set(1.0)[:, :, :cap]
            w_tok = probs[tok, flat_e]
            cb = jnp.zeros((n_tok, N_EXP, cap + 1), dtype=x_flat.dtype)
            cb = cb.at[tok, flat_e, slot_c].set(w_tok)[:, :, :cap]
            dispatched = jnp.einsum('tec,td->ecd', sec, x_flat)
            h = jax.nn.gelu(jnp.einsum('ecd,edh->ech', dispatched, c_fc), approximate=False)
            out = jnp.einsum('ech,ehd->ecd', h, c_proj_e)
            return jnp.einsum('tec,ecd->td', cb, out)
        key = jax.random.key(seed)
        ks = jax.random.split(key, 7)
        B, T, C = (2, 512, 192)
        std = 0.02
        return {'x': jax.random.normal(ks[0], (B, T, C), dtype=jnp.float32), 'ln1_w': jnp.ones((C,), dtype=jnp.float32), 'ln2_w': jnp.ones((C,), dtype=jnp.float32), 'c_attn_w': jax.random.normal(ks[1], (3 * C, C), dtype=jnp.float32) * std, 'c_proj_w': jax.random.normal(ks[2], (C, C), dtype=jnp.float32) * std, 'w_g': jax.random.normal(ks[3], (N_EXP, C), dtype=jnp.float32) * std, 'c_fc': jax.random.normal(ks[4], (N_EXP, C, 4 * C), dtype=jnp.float32) * std, 'c_proj_e': jax.random.normal(ks[5], (N_EXP, 4 * C, C), dtype=jnp.float32) * std}
    _L2_ffn_all = _L2_ffn_setup()
    _L2_ffn_in = {k: v for k, v in _L2_ffn_all.items() if k in ('ln1_w', 'ln2_w', 'c_attn_w', 'c_proj_w', 'w_g', 'c_fc', 'c_proj_e')}
    del _L2_ffn_all

    def _L3_conv_setup():
        import jax, jax.numpy as jnp
        import numpy as np
        E = 8
        TOPK = 2
        D = 192
        F = 768

        def _gelu(v):
            return jax.nn.gelu(v, approximate=False)
        key = jax.random.key(seed)
        ks = jax.random.split(key, 11)
        s = 0.02
        return {'x': jax.random.normal(ks[0], (2, 16, 16, D), dtype=jnp.float32), 'gate_w': jax.random.normal(ks[1], (E, D), dtype=jnp.float32), 'w1': jax.random.normal(ks[2], (E, F, D), dtype=jnp.float32) * s, 'b1': jax.random.normal(ks[3], (E, F), dtype=jnp.float32) * s, 'w2': jax.random.normal(ks[4], (E, D, F), dtype=jnp.float32) * s, 'b2': jax.random.normal(ks[5], (E, D), dtype=jnp.float32) * s, 'ws1': jax.random.normal(ks[6], (F, D), dtype=jnp.float32) * s, 'bs1': jax.random.normal(ks[7], (F,), dtype=jnp.float32) * s, 'ws2': jax.random.normal(ks[8], (D, F), dtype=jnp.float32) * s, 'bs2': jax.random.normal(ks[9], (D,), dtype=jnp.float32) * s}
    _L3_conv_all = _L3_conv_setup()
    _L3_conv_in = {k: v for k, v in _L3_conv_all.items() if k in ('gate_w', 'w1', 'b1', 'w2', 'b2', 'ws1', 'bs1', 'ws2', 'bs2')}
    del _L3_conv_all

    def _L3_ffn_setup():
        import jax, jax.numpy as jnp
        import numpy as np
        K_ACTIVE = 2
        key = jax.random.key(seed)
        ks = jax.random.split(key, 9)
        B, S, D, F, E, NS = (2, 512, 192, 384, 8, 1)
        sd = 1.0 / np.sqrt(D)
        sf = 1.0 / np.sqrt(F)
        return {'x': jax.random.normal(ks[0], (B, S, D), jnp.float32), 'Wg_s': jax.random.normal(ks[1], (NS, D, F), jnp.float32) * sd, 'Wu_s': jax.random.normal(ks[2], (NS, D, F), jnp.float32) * sd, 'Wd_s': jax.random.normal(ks[3], (NS, F, D), jnp.float32) * sf, 'Wg_r': jax.random.normal(ks[4], (E, D, F), jnp.float32) * sd, 'Wu_r': jax.random.normal(ks[5], (E, D, F), jnp.float32) * sd, 'Wd_r': jax.random.normal(ks[6], (E, F, D), jnp.float32) * sf, 'W_router': jax.random.normal(ks[7], (D, E), jnp.float32) * sd, 'expert_bias': jnp.zeros((E,), jnp.float32)}
    _L3_ffn_all = _L3_ffn_setup()
    _L3_ffn_in = {k: v for k, v in _L3_ffn_all.items() if k in ('Wg_s', 'Wu_s', 'Wd_s', 'Wg_r', 'Wu_r', 'Wd_r', 'W_router', 'expert_bias')}
    del _L3_ffn_all
    return {'x': x, 'L0_conv_wq': _L0_conv_in['wq'], 'L0_conv_bq': _L0_conv_in['bq'], 'L0_conv_wk': _L0_conv_in['wk'], 'L0_conv_bk': _L0_conv_in['bk'], 'L0_conv_wv': _L0_conv_in['wv'], 'L0_conv_bv': _L0_conv_in['bv'], 'L0_conv_rel_pos_h': _L0_conv_in['rel_pos_h'], 'L0_conv_rel_pos_w': _L0_conv_in['rel_pos_w'], 'L0_conv_proj_w': _L0_conv_in['proj_w'], 'L0_conv_proj_b': _L0_conv_in['proj_b'], 'L0_ffn_Wg': _L0_ffn_in['Wg'], 'L0_ffn_W1': _L0_ffn_in['W1'], 'L0_ffn_b1': _L0_ffn_in['b1'], 'L0_ffn_W2': _L0_ffn_in['W2'], 'L0_ffn_b2': _L0_ffn_in['b2'], 'L1_conv_qkv_w': _L1_conv_in['qkv_w'], 'L1_conv_qkv_b': _L1_conv_in['qkv_b'], 'L1_conv_proj_w': _L1_conv_in['proj_w'], 'L1_conv_proj_b': _L1_conv_in['proj_b'], 'L1_conv_rel_pos_h': _L1_conv_in['rel_pos_h'], 'L1_conv_rel_pos_w': _L1_conv_in['rel_pos_w'], 'L1_ffn_Wr': _L1_ffn_in['Wr'], 'L1_ffn_br': _L1_ffn_in['br'], 'L1_ffn_Wfc': _L1_ffn_in['Wfc'], 'L1_ffn_bfc': _L1_ffn_in['bfc'], 'L1_ffn_Wproj': _L1_ffn_in['Wproj'], 'L1_ffn_bproj': _L1_ffn_in['bproj'], 'L2_conv_qkv_w': _L2_conv_in['qkv_w'], 'L2_conv_qkv_b': _L2_conv_in['qkv_b'], 'L2_conv_proj_w': _L2_conv_in['proj_w'], 'L2_conv_proj_b': _L2_conv_in['proj_b'], 'L2_conv_rel_pos_h': _L2_conv_in['rel_pos_h'], 'L2_conv_rel_pos_w': _L2_conv_in['rel_pos_w'], 'L2_ffn_ln1_w': _L2_ffn_in['ln1_w'], 'L2_ffn_ln2_w': _L2_ffn_in['ln2_w'], 'L2_ffn_c_attn_w': _L2_ffn_in['c_attn_w'], 'L2_ffn_c_proj_w': _L2_ffn_in['c_proj_w'], 'L2_ffn_w_g': _L2_ffn_in['w_g'], 'L2_ffn_c_fc': _L2_ffn_in['c_fc'], 'L2_ffn_c_proj_e': _L2_ffn_in['c_proj_e'], 'L3_conv_gate_w': _L3_conv_in['gate_w'], 'L3_conv_w1': _L3_conv_in['w1'], 'L3_conv_b1': _L3_conv_in['b1'], 'L3_conv_w2': _L3_conv_in['w2'], 'L3_conv_b2': _L3_conv_in['b2'], 'L3_conv_ws1': _L3_conv_in['ws1'], 'L3_conv_bs1': _L3_conv_in['bs1'], 'L3_conv_ws2': _L3_conv_in['ws2'], 'L3_conv_bs2': _L3_conv_in['bs2'], 'L3_ffn_Wg_s': _L3_ffn_in['Wg_s'], 'L3_ffn_Wu_s': _L3_ffn_in['Wu_s'], 'L3_ffn_Wd_s': _L3_ffn_in['Wd_s'], 'L3_ffn_Wg_r': _L3_ffn_in['Wg_r'], 'L3_ffn_Wu_r': _L3_ffn_in['Wu_r'], 'L3_ffn_Wd_r': _L3_ffn_in['Wd_r'], 'L3_ffn_W_router': _L3_ffn_in['W_router'], 'L3_ffn_expert_bias': _L3_ffn_in['expert_bias']}

def reference(x, L0_conv_wq, L0_conv_bq, L0_conv_wk, L0_conv_bk, L0_conv_wv, L0_conv_bv, L0_conv_rel_pos_h, L0_conv_rel_pos_w, L0_conv_proj_w, L0_conv_proj_b, L0_ffn_Wg, L0_ffn_W1, L0_ffn_b1, L0_ffn_W2, L0_ffn_b2, L1_conv_qkv_w, L1_conv_qkv_b, L1_conv_proj_w, L1_conv_proj_b, L1_conv_rel_pos_h, L1_conv_rel_pos_w, L1_ffn_Wr, L1_ffn_br, L1_ffn_Wfc, L1_ffn_bfc, L1_ffn_Wproj, L1_ffn_bproj, L2_conv_qkv_w, L2_conv_qkv_b, L2_conv_proj_w, L2_conv_proj_b, L2_conv_rel_pos_h, L2_conv_rel_pos_w, L2_ffn_ln1_w, L2_ffn_ln2_w, L2_ffn_c_attn_w, L2_ffn_c_proj_w, L2_ffn_w_g, L2_ffn_c_fc, L2_ffn_c_proj_e, L3_conv_gate_w, L3_conv_w1, L3_conv_b1, L3_conv_w2, L3_conv_b2, L3_conv_ws1, L3_conv_bs1, L3_conv_ws2, L3_conv_bs2, L3_ffn_Wg_s, L3_ffn_Wu_s, L3_ffn_Wd_s, L3_ffn_Wg_r, L3_ffn_Wu_r, L3_ffn_Wd_r, L3_ffn_W_router, L3_ffn_expert_bias):
    import jax
    import jax.numpy as jnp

    def _L0_conv_ref(x, wq, bq, wk, bk, wv, bv, rel_pos_h, rel_pos_w, proj_w, proj_b):
        import jax, jax.numpy as jnp
        import numpy as np

        def get_rel_pos(q_size, k_size, rel_pos):
            q_coords = jnp.arange(q_size)[:, None]
            k_coords = jnp.arange(k_size)[None, :]
            rel = q_coords - k_coords + (k_size - 1)
            return rel_pos[rel]
        B, H, W, C = x.shape
        nH, hd, _ = wq.shape
        scale = hd ** (-0.5)
        q = jnp.einsum('bhwc,ndc->bnhwd', x, wq) + bq[None, :, None, None, :]
        k = jnp.einsum('bhwc,ndc->bnhwd', x, wk) + bk[None, :, None, None, :]
        v = jnp.einsum('bhwc,ndc->bnhwd', x, wv) + bv[None, :, None, None, :]
        qf = q.reshape(B, nH, H * W, hd)
        kf = k.reshape(B, nH, H * W, hd)
        vf = v.reshape(B, nH, H * W, hd)
        attn = jnp.einsum('bnqd,bnkd->bnqk', qf * scale, kf)
        Rh = get_rel_pos(H, H, rel_pos_h)
        Rw = get_rel_pos(W, W, rel_pos_w)
        rel_h = jnp.einsum('bnhwc,hkc->bnhwk', q, Rh)
        rel_w = jnp.einsum('bnhwc,wkc->bnhwk', q, Rw)
        attn = (attn.reshape(B, nH, H, W, H, W) + rel_h[:, :, :, :, :, None] + rel_w[:, :, :, None, :]).reshape(B, nH, H * W, H * W)
        attn = jax.nn.softmax(attn, axis=-1)
        out = jnp.einsum('bnqk,bnkd->bnqd', attn, vf)
        out = out.transpose(0, 2, 1, 3).reshape(B, H, W, nH * hd)
        return jnp.einsum('bhwc,oc->bhwo', out, proj_w) + proj_b

    def _L0_ffn_ref(x, Wg, W1, b1, W2, b2):
        import jax, jax.numpy as jnp
        import numpy as np
        TOP_K = 2
        E = Wg.shape[-1]
        logits = jnp.einsum('btc,ce->bte', x, Wg)
        probs = jax.nn.softmax(logits, axis=-1)
        top_vals, top_idx = jax.lax.top_k(probs, TOP_K)
        gates = (jax.nn.one_hot(top_idx, E, dtype=probs.dtype) * top_vals[..., None]).sum(-2)
        h = jax.nn.relu(jnp.einsum('btc,ech->bteh', x, W1) + b1)
        y = jnp.einsum('bteh,ehc->btec', h, W2) + b2
        out = jnp.einsum('bte,btec->btc', gates, y)
        return out

    def _L1_conv_ref(x, qkv_w, qkv_b, proj_w, proj_b, rel_pos_h, rel_pos_w):
        import jax, jax.numpy as jnp
        import numpy as np
        B, H, W, DIM = (8, 32, 32, 192)
        NUM_HEADS = 12
        HEAD_DIM = DIM // NUM_HEADS
        b, h, w, dim = x.shape
        nH, hd = (NUM_HEADS, dim // NUM_HEADS)
        scale = hd ** (-0.5)
        hw = h * w
        qkv = x.reshape(b, hw, dim) @ qkv_w + qkv_b
        qkv = qkv.reshape(b, hw, 3, nH, hd).transpose(2, 0, 3, 1, 4)
        qkv = qkv.reshape(3, b * nH, hw, hd)
        q, k, v = (qkv[0], qkv[1], qkv[2])
        idx_h = jnp.arange(h)[:, None] - jnp.arange(h)[None, :] + (h - 1)
        idx_w = jnp.arange(w)[:, None] - jnp.arange(w)[None, :] + (w - 1)
        Rh = rel_pos_h[idx_h]
        Rw = rel_pos_w[idx_w]
        r_q = q.reshape(b * nH, h, w, hd)
        rel_h = jnp.einsum('bhwc,hkc->bhwk', r_q, Rh)
        rel_w = jnp.einsum('bhwc,wkc->bhwk', r_q, Rw)
        attn_bias = (rel_h[:, :, :, :, None] + rel_w[:, :, :, None, :]).reshape(b * nH, hw, hw)
        attn = jnp.einsum('bqd,bkd->bqk', q, k) * scale + attn_bias
        attn = jax.nn.softmax(attn, axis=-1)
        out = jnp.einsum('bqk,bkd->bqd', attn, v)
        out = out.reshape(b, nH, h, w, hd).transpose(0, 2, 3, 1, 4).reshape(b, h, w, dim)
        return out @ proj_w + proj_b

    def _L1_ffn_ref(hidden_states, Wr, br, Wfc, bfc, Wproj, bproj):
        import jax, jax.numpy as jnp
        import numpy as np
        N_EXPERTS = 8
        TOPK = 2
        B, S, H, F = (8, 512, 192, 768)
        b, s, h = hidden_states.shape
        x = hidden_states.reshape(-1, h)
        logits = x @ Wr + br
        probs = jax.nn.softmax(logits, axis=-1)
        topk_w, topk_i = jax.lax.top_k(probs, TOPK)
        topk_w = topk_w / jnp.sum(topk_w, axis=-1, keepdims=True)
        out = jnp.zeros_like(x)
        for e in range(N_EXPERTS):
            w = jnp.sum(jnp.where(topk_i == e, topk_w, 0.0), axis=-1)
            he = jax.nn.gelu(x @ Wfc[e] + bfc[e], approximate=True) @ Wproj[e] + bproj[e]
            out = out + w[:, None] * he
        return out.reshape(b, s, h)

    def _L2_conv_ref(x, qkv_w, qkv_b, proj_w, proj_b, rel_pos_h, rel_pos_w):
        import jax, jax.numpy as jnp
        import numpy as np
        NUM_HEADS = 12

        def _rel_pos_table(size, rel_pos):
            coords = jnp.arange(size)[:, None] - jnp.arange(size)[None, :] + (size - 1)
            return rel_pos[coords]
        B, H, W, C = x.shape
        nh = NUM_HEADS
        hd = C // nh
        scale = hd ** (-0.5)
        L = H * W
        qkv = x.reshape(B, L, C) @ qkv_w + qkv_b
        qkv = qkv.reshape(B, L, 3, nh, hd).transpose(2, 0, 3, 1, 4)
        q, k, v = (qkv[0], qkv[1], qkv[2])
        attn = jnp.einsum('bhqd,bhkd->bhqk', q * scale, k)
        Rh = _rel_pos_table(H, rel_pos_h)
        Rw = _rel_pos_table(W, rel_pos_w)
        rq = q.reshape(B, nh, H, W, hd)
        rel_h = jnp.einsum('bnhwd,hkd->bnhwk', rq, Rh)
        rel_w = jnp.einsum('bnhwd,wkd->bnhwk', rq, Rw)
        attn = (attn.reshape(B, nh, H, W, H, W) + rel_h[..., :, None] + rel_w[..., None, :]).reshape(B, nh, L, L)
        attn = jax.nn.softmax(attn, axis=-1)
        out = jnp.einsum('bhqk,bhkd->bhqd', attn, v)
        out = out.reshape(B, nh, H, W, hd).transpose(0, 2, 3, 1, 4).reshape(B, H, W, C)
        return out @ proj_w + proj_b

    def _L2_ffn_ref(x, ln1_w, ln2_w, c_attn_w, c_proj_w, w_g, c_fc, c_proj_e):
        import jax, jax.numpy as jnp
        import numpy as np
        import math
        N_HEAD = 12
        N_EXP = 8
        TOP_K = 2
        EVAL_CAPACITY = 1.0
        MIN_CAPACITY = 4
        EPS = 1e-05

        def layer_norm(x, w):
            mu = jnp.mean(x, axis=-1, keepdims=True)
            var = jnp.var(x, axis=-1, keepdims=True)
            return (x - mu) / jnp.sqrt(var + EPS) * w

        def attention(x, c_attn_w, c_proj_w):
            B, T, C = x.shape
            H, D = (N_HEAD, C // N_HEAD)
            qkv = x @ c_attn_w.T
            q, k, v = jnp.split(qkv, 3, axis=-1)
            q = q.reshape(B, T, H, D).transpose(0, 2, 1, 3)
            k = k.reshape(B, T, H, D).transpose(0, 2, 1, 3)
            v = v.reshape(B, T, H, D).transpose(0, 2, 1, 3)
            scores = jnp.einsum('bhqd,bhkd->bhqk', q, k) * (1.0 / math.sqrt(D))
            causal = jnp.tril(jnp.ones((T, T), dtype=bool))
            scores = jnp.where(causal, scores, -jnp.inf)
            att = jax.nn.softmax(scores, axis=-1)
            y = jnp.einsum('bhqk,bhkd->bhqd', att, v)
            y = y.transpose(0, 2, 1, 3).reshape(B, T, C)
            return y @ c_proj_w.T

        def get_capacity(num_tokens):
            cap = int(math.floor(TOP_K * EVAL_CAPACITY * num_tokens / N_EXP))
            cap += cap % 2
            return max(cap, MIN_CAPACITY)

        def moe(x_flat, w_g, c_fc, c_proj_e):
            n_tok, C = x_flat.shape
            logits = x_flat @ w_g.T
            top_vals, top_idx = jax.lax.top_k(logits, TOP_K)
            rows = jnp.arange(n_tok)[:, None]
            masked = jnp.full_like(logits, -jnp.inf).at[rows, top_idx].set(top_vals)
            probs = jax.nn.softmax(masked, axis=-1)
            cap = get_capacity(n_tok)
            flat_e = top_idx.reshape(-1)
            onehot = jax.nn.one_hot(flat_e, N_EXP, dtype=jnp.int32)
            pos = jnp.cumsum(onehot, axis=0) - onehot
            slot = jnp.take_along_axis(pos, flat_e[:, None], axis=1)[:, 0]
            valid = slot < cap
            tok = jnp.repeat(jnp.arange(n_tok), TOP_K)
            slot_c = jnp.where(valid, slot, cap)
            sec = jnp.zeros((n_tok, N_EXP, cap + 1), dtype=x_flat.dtype)
            sec = sec.at[tok, flat_e, slot_c].set(1.0)[:, :, :cap]
            w_tok = probs[tok, flat_e]
            cb = jnp.zeros((n_tok, N_EXP, cap + 1), dtype=x_flat.dtype)
            cb = cb.at[tok, flat_e, slot_c].set(w_tok)[:, :, :cap]
            dispatched = jnp.einsum('tec,td->ecd', sec, x_flat)
            h = jax.nn.gelu(jnp.einsum('ecd,edh->ech', dispatched, c_fc), approximate=False)
            out = jnp.einsum('ech,ehd->ecd', h, c_proj_e)
            return jnp.einsum('tec,ecd->td', cb, out)
        x = x + attention(layer_norm(x, ln1_w), c_attn_w, c_proj_w)
        B, T, C = x.shape
        x_ln = layer_norm(x, ln2_w)
        moe_out = moe(x_ln.reshape(B * T, C), w_g, c_fc, c_proj_e)
        return x + moe_out.reshape(B, T, C)

    def _L3_conv_ref(x, gate_w, w1, b1, w2, b2, ws1, bs1, ws2, bs2):
        import jax, jax.numpy as jnp
        import numpy as np
        E = 8
        TOPK = 2
        D = 192
        F = 768

        def _gelu(v):
            return jax.nn.gelu(v, approximate=False)
        B, H, W, Dh = x.shape
        xf = x.reshape(-1, Dh)
        T = xf.shape[0]
        scores = jax.nn.softmax(xf @ gate_w.T, axis=-1)
        vals, idx = jax.lax.top_k(scores, TOPK)
        vals = vals / jnp.sum(vals, axis=-1, keepdims=True)
        cw = jnp.zeros((T, E), dtype=xf.dtype).at[jnp.arange(T)[:, None], idx].add(vals)
        out = jnp.zeros_like(xf)
        for e in range(E):
            h = _gelu(xf @ w1[e].T + b1[e])
            y = h @ w2[e].T + b2[e]
            out = out + y * cw[:, e:e + 1]
        shared = _gelu(xf @ ws1.T + bs1) @ ws2.T + bs2
        return (out + shared).reshape(B, H, W, Dh)

    def _L3_ffn_ref(x, Wg_s, Wu_s, Wd_s, Wg_r, Wu_r, Wd_r, W_router, expert_bias):
        import jax, jax.numpy as jnp
        import numpy as np
        K_ACTIVE = 2
        B, S, D = x.shape
        E = Wg_r.shape[0]
        xf = x.reshape(-1, D)
        T = xf.shape[0]
        g_s = jax.nn.silu(jnp.einsum('td,edf->etf', xf, Wg_s))
        u_s = jnp.einsum('td,edf->etf', xf, Wu_s)
        shared_out = jnp.einsum('etf,efd->td', g_s * u_s, Wd_s)
        logits = xf @ W_router + expert_bias
        top_vals, top_idx = jax.lax.top_k(logits, K_ACTIVE)
        rw = jax.nn.softmax(top_vals, axis=-1)
        combine = jnp.zeros((T, E), xf.dtype).at[jnp.arange(T)[:, None], top_idx].set(rw)
        g_r = jax.nn.silu(jnp.einsum('td,edf->etf', xf, Wg_r))
        u_r = jnp.einsum('td,edf->etf', xf, Wu_r)
        out_e = jnp.einsum('etf,efd->etd', g_r * u_r, Wd_r)
        routed_out = jnp.einsum('etd,te->td', out_e, combine)
        return (shared_out + routed_out).reshape(B, S, D)

    def _gn(v, G=32, eps=1e-05):
        B_, H_, W_, C_ = v.shape
        g = v.reshape(B_, H_, W_, G, C_ // G)
        m = jnp.mean(g, axis=(1, 2, 4), keepdims=True)
        s = jnp.var(g, axis=(1, 2, 4), keepdims=True)
        return ((g - m) / jnp.sqrt(s + eps)).reshape(v.shape)

    def _ln_c(v, eps=1e-06):
        m = jnp.mean(v, axis=-1, keepdims=True)
        s = jnp.var(v, axis=-1, keepdims=True)
        return (v - m) / jnp.sqrt(s + eps)

    def _ln_t(v, eps=1e-05):
        m = jnp.mean(v, axis=-1, keepdims=True)
        s = jnp.var(v, axis=-1, keepdims=True)
        return (v - m) / jnp.sqrt(s + eps)

    def _to_tokens(v):
        B_, H_, W_, C_ = v.shape
        return v.reshape(B_, H_ * W_, C_)

    def _from_tokens(t, like):
        return t.reshape(like.shape)
    x = x + _L0_conv_ref(_ln_c(x), L0_conv_wq, L0_conv_bq, L0_conv_wk, L0_conv_bk, L0_conv_wv, L0_conv_bv, L0_conv_rel_pos_h, L0_conv_rel_pos_w, L0_conv_proj_w, L0_conv_proj_b)
    t = _to_tokens(x)
    t = t + _L0_ffn_ref(_ln_t(t), L0_ffn_Wg, L0_ffn_W1, L0_ffn_b1, L0_ffn_W2, L0_ffn_b2)
    x = _from_tokens(t, x)
    x = x + _L1_conv_ref(_ln_c(x), L1_conv_qkv_w, L1_conv_qkv_b, L1_conv_proj_w, L1_conv_proj_b, L1_conv_rel_pos_h, L1_conv_rel_pos_w)
    t = _to_tokens(x)
    t = t + _L1_ffn_ref(_ln_t(t), L1_ffn_Wr, L1_ffn_br, L1_ffn_Wfc, L1_ffn_bfc, L1_ffn_Wproj, L1_ffn_bproj)
    x = _from_tokens(t, x)
    x = x + _L2_conv_ref(_ln_c(x), L2_conv_qkv_w, L2_conv_qkv_b, L2_conv_proj_w, L2_conv_proj_b, L2_conv_rel_pos_h, L2_conv_rel_pos_w)
    t = _to_tokens(x)
    t = t + _L2_ffn_ref(_ln_t(t), L2_ffn_ln1_w, L2_ffn_ln2_w, L2_ffn_c_attn_w, L2_ffn_c_proj_w, L2_ffn_w_g, L2_ffn_c_fc, L2_ffn_c_proj_e)
    x = _from_tokens(t, x)
    x = x + _L3_conv_ref(_ln_c(x), L3_conv_gate_w, L3_conv_w1, L3_conv_b1, L3_conv_w2, L3_conv_b2, L3_conv_ws1, L3_conv_bs1, L3_conv_ws2, L3_conv_bs2)
    t = _to_tokens(x)
    t = t + _L3_ffn_ref(_ln_t(t), L3_ffn_Wg_s, L3_ffn_Wu_s, L3_ffn_Wd_s, L3_ffn_Wg_r, L3_ffn_Wu_r, L3_ffn_Wd_r, L3_ffn_W_router, L3_ffn_expert_bias)
    x = _from_tokens(t, x)
    return x

_drawn_inputs = setup_inputs


def setup_inputs(seed=0):
    import zlib

    import numpy as np

    out = dict(_drawn_inputs(seed))
    spreads = {'L0_ffn_b1': (0.0, 0.1),
     'L0_ffn_b2': (0.0, 0.1),
     'L1_conv_qkv_b': (0.0, 0.1),
     'L1_conv_proj_b': (0.0, 0.1),
     'L1_ffn_br': (0.0, 0.1),
     'L1_ffn_bfc': (0.0, 0.295),
     'L1_ffn_bproj': (0.0, 0.1),
     'L2_conv_qkv_b': (0.0, 0.1),
     'L2_conv_proj_b': (0.0, 0.1),
     'L2_ffn_ln1_w': (1.0, 0.6),
     'L2_ffn_ln2_w': (1.0, 0.6),
     'L3_ffn_expert_bias': (0.0, 0.1)}
    factors = {'L0_conv_wq': 8.0,
     'L0_conv_bq': 8.0,
     'L0_conv_wk': 6.593,
     'L0_conv_bk': 200.0,
     'L0_conv_rel_pos_h': 8.0,
     'L0_conv_rel_pos_w': 8.0,
     'L1_conv_qkv_w': 4.191,
     'L1_conv_rel_pos_h': 8.0,
     'L1_conv_rel_pos_w': 8.0,
     'L2_conv_rel_pos_h': 64.0,
     'L2_conv_rel_pos_w': 182.539,
     'L2_ffn_c_attn_w': 2.898,
     'L2_ffn_c_proj_w': 3.312,
     'L3_conv_b1': 6.213,
     'L3_conv_b2': 3.904,
     'L3_conv_bs1': 7.849,
     'L3_conv_bs2': 3.315}
    for name, (base, spread) in spreads.items():
        noise = np.random.default_rng([zlib.crc32(name.encode()), seed]).standard_normal(out[name].shape)
        drawn = base * np.exp(spread * noise) if base else spread * noise
        out[name] = jnp.asarray(drawn.astype(out[name].dtype))
    for name, factor in factors.items():
        out[name] = (out[name] * factor).astype(out[name].dtype)
    return out
```

```python
from contextlib import ExitStack

import concourse.bass as bass
from concourse import mybir

F32 = mybir.dt.float32
U32 = mybir.dt.uint32
ALU = mybir.AluOpType
ACT = mybir.ActivationFunctionType
AX = mybir.AxisListType

P = 128
SIDE = 16
T = SIDE * SIDE
TT = T // P
C = 192
KC = 2
CH = C // KC
NH = 12
HD = C // NH
SLOT = 64
PAIRS = NH // 2
GROUPS = NH // 4
REL = 2 * SIDE - 1
RELS = 2 * REL
RELW = RELS * NH
RELH = RELW // KC
E = 8
HB = 3
CAP = 64
NEG = -3.0e38

CONST = {}
_at = 0
for _name, _n in (("ident", P), ("earlier", P), ("ones", P), ("iota", E), ("onehot", TT * 2 * SIDE), ("rowhot", TT * SIDE),
                  ("causal", TT * T)):
    CONST[_name] = slice(_at, _at + _n)
    _at += _n
CONST_W = _at

ATTN = (dict(rel=True, eps=1e-6), dict(rel=True, eps=1e-6), dict(rel=True, eps=1e-6), dict(rel=False, eps=1e-5))
MOE = (
    dict(n=8, act="relu", b=True, rbias=False, over_all=True, cap=False, eps=1e-5),
    dict(n=8, act="gelu_tanh", b=True, rbias=True, over_all=False, cap=False, eps=1e-5),
    dict(n=8, act="gelu", b=False, rbias=False, over_all=False, cap=True, eps=1e-5),
    dict(n=9, act="gelu", b=True, rbias=False, over_all=False, cap=False, eps=1e-6),
    dict(n=9, act="glu", b=False, rbias=True, over_all=False, cap=False, eps=1e-5),
)
BASE = [sum(m["n"] for m in MOE[:i]) for i in range(len(MOE) + 1)]
FUNC = {"relu": ACT.Relu, "gelu_tanh": ACT.Gelu_apprx_tanh, "gelu": ACT.Gelu, "glu": ACT.Silu}
BLOCKS = (("attn", 0), ("moe", 0), ("attn", 1), ("moe", 1), ("attn", 2), ("attn", 3), ("moe", 2), ("moe", 3), ("moe", 4))


def metaformer_kernel(nc, a, out):
    ctx = ExitStack()
    with ctx:
        def sb(name, shape, dt=F32):
            return ctx.enter_context(nc.sbuf_tensor(name, shape, dt))

        def sem(name):
            return ctx.enter_context(nc.semaphore(name))

        x = sb("x", [P, TT, C])
        tln = sb("tln", [P, TT, C])
        xb = sb("xb", [P, TT, C])
        stats = sb("stats", [P, TT, 6])
        moments = sb("moments", [P, TT, 2])
        var_eps = sb("var_eps", [P, TT])
        minus_half = sb("minus_half", [P, TT])
        rstd = sb("rstd", [P, TT])
        xn = sb("xn", [P, TT, C])
        xT = sb("xT", [CH, KC, T])
        consts = sb("consts", [P, CONST_W])
        ident = consts[:, CONST["ident"]]
        wqkv = sb("wqkv", [CH, 4, KC, 3 * C])
        wproj = sb("wproj", [P, 4, GROUPS, C])
        bqkv = sb("bqkv", [P, 3, 3 * C])
        bproj = sb("bproj", [P, 3, C])
        bq4 = sb("bq4", [P, 3, C])
        bq_col = sb("bq_col", [CH, 3, KC])
        reltab = sb("reltab", [CH, 3, RELH])
        qTs = sb("qTs", [CH, KC, T])
        relall = sb("relall", [P, TT, RELS, NH])
        rel = sb("rel", [P, TT, 2, SIDE, NH])
        q_st = sb("q_st", [P, TT, NH, SLOT])
        k_st = sb("k_st", [P, TT, NH, SLOT])
        v_st = sb("v_st", [P, TT, NH, 32])
        qT = sb("qT", [P, PAIRS, T])
        kT = sb("kT", [P, PAIRS, 2, T])
        smask = sb("smask", [P, 2, TT, 2, T])
        nmax = sb("nmax", [P, 2, TT, 2])
        rsum = sb("rsum", [P, 2, TT, 2])
        rinv = sb("rinv", [P, 2, TT, 2])
        probs = sb("probs", [P, 2, TT, 2, T])
        pT = sb("pT", [P, 2, TT, 2, T])
        oT = sb("oT", [P, GROUPS, T])
        w1 = [sb(f"w1_{s}", [CH, KC * 768]) for s in range(2)]
        w2 = [sb(f"w2_{s}", [P, 2 * HB * C]) for s in range(2)]
        wr = sb("wr", [CH, 5, KC, E])
        rbias = sb("rbias", [P, 2, TT, E])
        b1 = sb("b1", [P, 3, 9 * 2 * HB])
        b2 = sb("b2", [9, 3, C])
        lnw = sb("lnw", [CH, 2, KC])
        hid = sb("hid", [P, 2 * HB, T])
        silu_g = sb("silu_g", [P, HB, T])
        logits = sb("logits", [P, TT, E])
        top8 = sb("top8", [P, TT, 8])
        top_i = sb("top_i", [P, TT, 8], U32)
        top_f = sb("top_f", [P, TT, 2])
        nmax_l = sb("nmax_l", [P, TT])
        expl = sb("expl", [P, TT, E])
        first = sb("first", [P, TT, E])
        sel = sb("sel", [P, TT, E])
        chosen = sb("chosen", [P, TT, E])
        den = sb("den", [P, TT])
        rden = sb("rden", [P, TT])
        valid = sb("valid", [P, TT, E])
        gates = sb("gates", [P, TT, E + 1])
        gT = sb("gT", [E + 1, T])
        scratch = nc.dram_tensor("rel_scratch", [3, T, RELW], F32, kind="Internal").ap()

        bank = [ctx.enter_context(nc.psum_tensor(f"bank{i}", [P, 512], F32)) for i in range(8)]
        B_QT0, B_QK, B_REL, B_V = 0, (1, 2), (3, 4, 5, 6), 7
        B_KT, B_QT = (0, 1, 2), (3, 4, 5)
        B_S, B_PT, B_O, B_PROJ = ((6, 7), (0, 1)), (2, 3), (4, 5, 4), 2
        B_H, B_Y, B_R, B_B2, B_LN = (0, 1, 2), (3, 4), 5, 6, 7

        x_in, c_in = sem("x_in"), sem("consts_in")
        aw_in = [sem(f"attn_weights_in{i}") for i in range(4)]
        mw_in = [sem(f"moe_small_in{i}") for i in range(5)]
        slot_in = [sem(f"expert_weights_in{s}") for s in range(2)]
        rel_out = [sem(f"rel_to_dram{t}") for t in range(TT)]
        rel_in = [sem(f"rel_from_dram{t}") for t in range(TT)]
        y_out = sem("result_out")
        dve_own, pool_own = sem("dve_own"), sem("pool_own")
        pool_ready = sem("pool_constants_ready")
        kst_ready = sem("k_onehots_ready")
        var_ready, rstd_ready, xn_ready = sem("var_ready"), sem("rstd_ready"), sem("xn_ready")
        xT_psum, xT_ready = sem("xT_psum"), sem("xT_ready")
        qTs_psum, qTs_ready = sem("qTs_psum"), sem("qTs_ready")
        qk_psum, qk_ready = sem("qk_psum"), sem("qk_ready")
        rel_psum, rel_dve, rel_act = sem("rel_psum"), sem("rel_copied_dve"), sem("rel_copied_act")
        q_rel_ready = sem("q_rel_ready")
        v_psum, v_ready = sem("v_psum"), sem("v_ready")
        kT_psum, kT_dve, kT_act = sem("kT_psum"), sem("kT_dve"), sem("kT_act")
        qT_psum, qT_dve, qT_act = sem("qT_psum"), sem("qT_dve"), sem("qT_act")
        s_psum, nmax_ready, exp_ready = sem("scores_psum"), sem("nmax_ready"), sem("exp_ready")
        rinv_ready, p_ready = sem("rinv_ready"), sem("probs_ready")
        pT_psum, pT_dve, pT_act = sem("pT_psum"), sem("pT_dve"), sem("pT_act")
        o_psum, o_ready = sem("o_psum"), sem("o_ready")
        proj_psum = sem("proj_psum")
        r_psum, negm_ready, expl_ready = sem("router_psum"), sem("neg_logit_max_ready"), sem("exp_logits_ready")
        sel_ready, pos_psum, gates_ready = sem("selection_ready"), sem("positions_psum"), sem("gates_ready")
        gT_psum, gT_ready, b2_psum = sem("gatesT_psum"), sem("gatesT_ready"), sem("b2_psum")
        h_psum, h_ready = sem("hidden_psum"), sem("hidden_ready")
        silu_ready, glu_ready = sem("silu_ready"), sem("glu_ready")
        y_psum, acc_done = sem("expert_out_psum"), sem("expert_out_added")

        def rel_ap(i, t, along):
            step_h, step_w = SIDE * RELW, RELW
            if along == 0:
                first_at, step_h = t * (SIDE // TT) * NH, step_h + NH
            else:
                first_at, step_w = REL * NH, step_w + NH
            return bass.AP(scratch.tensor, i * T * RELW + t * P * RELW + first_at,
                           [[step_h, SIDE // TT], [step_w, SIDE], [1, SIDE * NH]])

        def rel_keys_ap(kh):
            return bass.AP(scratch.tensor, kh * (RELW - NH) + (REL + SIDE - 1) * NH,
                           [[NH, SIDE], [SIDE * RELW, SIDE], [1, NH]])

        def rel_loads(n):
            return 16 * (1 + SIDE // TT) + 32 * n

        block = ctx.enter_context(nc.Block())

        @block.sync
        def _(sp):
            def load_expert(m, j, i):
                g = BASE[m] + i
                s = g % 2
                e = 2 * j + i
                if m or not isinstance(j, int) or j:
                    sp.wait_ge(y_psum, 2 * (2 * j + g - 1))
                n2 = a[f"M{m}_w2"].shape[2]
                sp.dma_start(w1[s][:, :], a[f"M{m}_w1"][bass.ds(e, 1)].rearrange("a p n -> (a p) n"))\
                    .then_inc(slot_in[s], 16)
                sp.dma_start(w2[s][:, 0:n2], a[f"M{m}_w2"][bass.ds(e, 1)].rearrange("a p n -> (a p) n"))\
                    .then_inc(slot_in[s], 16)

            def load_attn(i):
                sp.dma_start(wqkv[:, i], a[f"A{i}_wqkv"]).then_inc(aw_in[i], 16)
                sp.dma_start(wproj[:, i], a[f"A{i}_wproj"]).then_inc(aw_in[i], 16)
                if ATTN[i]["rel"]:
                    sp.dma_start(bq_col[:, i], a[f"A{i}_bq"]).then_inc(aw_in[i], 16)
                    sp.dma_start(reltab[:, i], a[f"A{i}_reltab"]).then_inc(aw_in[i], 16)
                    sp.dma_start(bqkv[:, i], a[f"A{i}_bqkv"].partition_broadcast(P)).then_inc(aw_in[i], 16)
                    sp.dma_start(bproj[:, i], a[f"A{i}_bproj"].partition_broadcast(P)).then_inc(aw_in[i], 16)

            def load_small(m):
                sp.dma_start(wr[:, m], a[f"M{m}_wr"]).then_inc(mw_in[m], 16)
                if MOE[m]["rbias"]:
                    for t in range(TT):
                        sp.dma_start(rbias[:, m // 4, t], a[f"M{m}_rbias"].partition_broadcast(P)).then_inc(mw_in[m], 16)
                if MOE[m]["b"]:
                    n = MOE[m]["n"]
                    k = (0, 1, None, 2)[m]
                    sp.dma_start(b1[:, k, 0:n * 2 * HB], a[f"M{m}_b1"]).then_inc(mw_in[m], 16)
                    sp.dma_start(b2[0:n, k], a[f"M{m}_b2"]).then_inc(mw_in[m], 16)

            sp.dma_start(x[:, :, :], a["x"].rearrange("(t p) c -> p t c", p=P)).then_inc(x_in, 16)
            sp.dma_start(consts[:, :], a["consts"]).then_inc(c_in, 16)
            load_attn(0)
            load_small(0)
            nrel = 0
            for kind, n in BLOCKS:
                if kind == "attn":
                    if n < 3:
                        for i in range(2):
                            load_expert(n, 0, i)
                        if n < 2:
                            load_attn(n + 1)
                            load_small(n + 1)
                        else:
                            load_attn(3)
                            for m in (2, 3, 4):
                                load_small(m)
                            sp.dma_start(lnw[:, :, :], a["lnw"]).then_inc(mw_in[2], 16)
                    if ATTN[n]["rel"]:
                        for t in range(TT):
                            sp.wait_ge(rel_dve, TT * n + t + 1)
                            sp.wait_ge(rel_act, TT * n + t + 1)
                            sp.dma_start(scratch[n, t * P:(t + 1) * P, :], relall[:, t].rearrange("p r n -> p (r n)"))\
                                .then_inc(rel_out[t], 16)
                        for t in range(TT):
                            sp.wait_ge(rel_out[t], 16 * (n + 1))
                            if n == 0 and t == 0:
                                sp.wait_ge(rel_out[1], 16)
                            for along in range(1 if n == 0 else 2):
                                sp.dma_start(rel[:, t, along].rearrange("p r n -> p (r n)"), rel_ap(n, t, along))\
                                    .then_inc(rel_in[t], 16)
                            for k in range(SIDE // TT if n == 0 else 0):
                                sp.dma_start(rel[k * SIDE:(k + 1) * SIDE, t, 1], rel_keys_ap(t * (SIDE // TT) + k))\
                                    .then_inc(rel_in[t], 16)
                else:
                    if n > 2:
                        for i in range(2):
                            load_expert(n, 0, i)
                    with sp.Fori(1, E // 2) as j:
                        for i in range(2):
                            load_expert(n, j, i)
                    if MOE[n]["n"] > E:
                        load_expert(n, E // 2, 0)
            sp.wait_ge(acc_done, 2 * BASE[-1])
            sp.dma_start(out.rearrange("(t p) c -> p t c", p=P), x[:, :, :]).then_inc(y_out, 16)
            sp.wait_ge(y_out, 16)

        @block.gpsimd
        def _(pool):
            own = [0]

            def then(ins):
                own[0] += 1
                ins.then_inc(pool_own, 1)

            def ln(n):
                pool.wait_ge(var_ready, n + 1)
                pool.tensor_tensor(rstd[:, :], var_eps[:, :], minus_half[:, :], ALU.pow).then_inc(rstd_ready, 1)

            pool.memset(minus_half[:, :], -0.5).then_inc(pool_own, 1)
            pool.wait_ge(pool_own, 1)
            ln(0)
            pool.memset(q_st[:, :, :, :], 0.0).then_inc(pool_ready, 1)
            pool.memset(k_st[:, :, :, :], 0.0).then_inc(pool_ready, 1)
            pool.memset(v_st[:, :, :, :], 0.0).then_inc(pool_ready, 1)
            pool.memset(kT[:, :, :, :], 0.0).then_inc(pool_ready, 1)
            pool.memset(gates[:, :, E:E + 1], 1.0).then_inc(pool_ready, 1)
            pool.wait_ge(c_in, 16)
            pool.wait_ge(pool_ready, 2)
            for t in range(TT):
                at = CONST["onehot"].start + t * 2 * SIDE
                oh = consts[:, at:at + SIDE].unsqueeze(1).broadcast_to([P, NH, SIDE])
                pool.tensor_copy(k_st[:, t, :, HD:HD + SIDE], oh).then_inc(kst_ready, 1)
                at = CONST["rowhot"].start + t * SIDE
                oh = consts[:, at:at + SIDE].unsqueeze(1).broadcast_to([P, NH, SIDE])
                pool.tensor_copy(q_st[:, t, :, HD + SIDE:HD + 2 * SIDE], oh).then_inc(kst_ready, 1)

            def attn(n):
                if n == 1:
                    pool.wait_ge(kT_psum, 3)
                    for t in range(TT):
                        at = CONST["onehot"].start + t * 2 * SIDE + SIDE
                        oh = consts[:, at:at + SIDE].unsqueeze(1).broadcast_to([P, NH, SIDE])
                        pool.tensor_copy(k_st[:, t, :, HD + SIDE:HD + 2 * SIDE], oh).then_inc(kst_ready, 1)
                if ATTN[n]["rel"]:
                    for t in range(TT):
                        pool.wait_ge(rel_in[t], rel_loads(n))
                        for along in range(2):
                            side = k_st if n == 0 and along else q_st
                            pool.tensor_copy(side[:, t, :, HD + along * SIDE:HD + (along + 1) * SIDE],
                                             rel[:, t, along].rearrange("p r n -> p n r"))\
                                .then_inc(q_rel_ready, 1)
                else:
                    pool.wait_ge(qT_psum, 3 * n)
                    pool.memset(q_st[:, :, :, HD:HD + 2 * SIDE], 0.0).then_inc(q_rel_ready, 1)
                for p in range(PAIRS):
                    g = n * PAIRS + p
                    pool.wait_ge(rinv_ready, g + 1)
                    for t in range(TT):
                        pr = probs[:, p % 2, t]
                        pool.tensor_tensor(pr, pr, rinv[:, p % 2, t].unsqueeze(2).broadcast_to([P, 2, T]), ALU.mult)\
                            .then_inc(p_ready, 1)

            nln = 1
            for kind, n in BLOCKS:
                if kind == "attn":
                    if n == 3:
                        ln(nln)
                        nln += 1
                    if n > 0:
                        ln(nln)
                        nln += 1
                    attn(n)
                else:
                    ln(nln)
                    nln += 1

        @block.scalar
        def _(act):
            def x_transposed(k, weight):
                act.wait_ge(xT_psum, k + 1)
                if weight is None:
                    act.activation(xT[:, :, :].rearrange("p k t -> p (k t)"), bank[B_LN][0:CH, :], ACT.Copy).then_inc(xT_ready, 1)
                else:
                    act.wait_ge(mw_in[2], 32)
                    act.activation(xT[:, 0], bank[B_LN][0:CH, 0:T], ACT.Copy, scale=lnw[:, weight, 0:1])
                    act.activation(xT[:, 1], bank[B_LN][0:CH, T:2 * T], ACT.Copy, scale=lnw[:, weight, 1:2]).then_inc(xT_ready, 1)

            def attn(n):
                if ATTN[n]["rel"]:
                    for t in range(TT):
                        act.wait_ge(rel_psum, 4 * n + 2 * t + 2)
                        act.activation(relall[:, t, :, NH // 2:NH],
                                       bank[B_REL[2 * t + 1]][:, 0:RELH].rearrange("p (r n) -> p r n", n=NH // 2),
                                       ACT.Copy).then_inc(rel_act, 1)
                if n == 0:
                    act.wait_ge(pool_ready, 4)
                for b in range(3):
                    act.wait_ge(kT_psum, 3 * n + b + 1)
                    act.activation(kT[0:SLOT, 2 * b:2 * b + 2, 0, :],
                                   bank[B_KT[b]][0:SLOT, :].rearrange("p (a t) -> p a t", a=2), ACT.Copy).then_inc(kT_act, 1)
                for b in (0, 2):
                    act.wait_ge(qT_psum, 3 * n + b + 1)
                    act.activation(qT[:, 2 * b:2 * b + 2, :].rearrange("p a t -> p (a t)"), bank[B_QT[b]][:, :], ACT.Copy).then_inc(qT_act, 1)

                def exps(p):
                    for t in range(TT):
                        act.wait_ge(nmax_ready, 2 * (n * PAIRS + p) + t + 1)
                        for h in range(2):
                            src = smask[:, p % 2, t, h] if n == 3 else bank[B_S[p % 2][t]][:, h * T:(h + 1) * T]
                            act.activation(probs[:, p % 2, t, h], src, ACT.Exp, bias=nmax[:, p % 2, t, h:h + 1],
                                           accum_out=rsum[:, p % 2, t, h:h + 1]).then_inc(exp_ready, 1)

                exps(0)
                exps(1)
                for p in range(PAIRS):
                    act.wait_ge(pT_psum, n * PAIRS + p + 1)
                    act.activation(pT[:, p % 2, 0].rearrange("p h t -> p (h t)"), bank[B_PT[0]][:, :], ACT.Copy).then_inc(pT_act, 1)
                    if p + 2 < PAIRS:
                        exps(p + 2)
                    if p % 2:
                        g = p // 2
                        act.wait_ge(o_psum, n * PAIRS + p + 1)
                        act.activation(oT[:, g, :], bank[B_O[g]][:, 0:T], ACT.Copy).then_inc(o_ready, 1)

            def moe(m):
                cfg = MOE[m]
                act.wait_ge(negm_ready, m + 1)
                for t in range(TT):
                    act.activation(expl[:, t, :], logits[:, t, :], ACT.Exp, bias=nmax_l[:, t:t + 1]).then_inc(expl_ready, 1)
                if cfg["b"]:
                    act.wait_ge(mw_in[m], {0: 48, 1: 80, 3: 48}[m])

                def expert(j, i):
                    g = BASE[m] + i
                    for b in range(HB):
                        act.wait_ge(h_psum, 3 * (2 * j + g) + b + 1)
                        if cfg["act"] == "glu":
                            act.activation(silu_g[:, b, :], bank[B_H[b]][:, 0:T], ACT.Silu).then_inc(silu_ready, 1)
                        elif not cfg["b"]:
                            act.activation(hid[:, 2 * b:2 * b + 2, :].rearrange("p c t -> p (c t)"), bank[B_H[b]][:, :],
                                           FUNC[cfg["act"]]).then_inc(h_ready, 1)
                        else:
                            k = (0, 1, None, 2)[m]
                            for c in range(2):
                                at = (2 * j + i) * 2 * HB + 2 * b + c
                                ins = act.activation(hid[:, 2 * b + c, :], bank[B_H[b]][:, c * T:(c + 1) * T],
                                                     FUNC[cfg["act"]], bias=b1[:, k, bass.ds(at, 1)])
                            ins.then_inc(h_ready, 1)

                for i in range(2):
                    expert(0, i)
                    if cfg["b"] and i == 0:
                        k = (0, 1, None, 2)[m]
                        act.wait_ge(gT_psum, (k + 1))
                        act.activation(gT[0:cfg["n"], :], bank[B_R][0:cfg["n"], T:2 * T], ACT.Copy).then_inc(gT_ready, 1)
                with act.Fori(1, E // 2) as j:
                    for i in range(2):
                        expert(j, i)
                if cfg["n"] > E:
                    expert(E // 2, 0)

            k = 0
            for kind, n in BLOCKS:
                x_transposed(k, {("attn", 3): 0, ("moe", 2): 1}.get((kind, n)))
                k += 1
                (attn if kind == "attn" else moe)(n)

        @block.tensor
        def _(pe):
            def x_transposed(k, n):
                if k == 0:
                    pe.wait_ge(c_in, 16)
                for t in range(TT):
                    pe.wait_ge(xn_ready, 2 * n + t + 1)
                    for c in range(KC):
                        ins = pe.transpose(bank[B_LN][0:CH, c * T + t * P:c * T + (t + 1) * P],
                                           xn[:, t, c * CH:(c + 1) * CH], ident)
                ins.then_inc(xT_psum, 1)

            def attn(n, k):
                pe.wait_ge(aw_in[n], 96 if ATTN[n]["rel"] else 32)
                pe.wait_ge(xT_ready, k + 1)
                if ATTN[n]["rel"]:
                    for h in range(KC):
                        for c in range(KC):
                            ins = pe.matmul(bank[B_QT0][0:CH, h * T:(h + 1) * T], wqkv[:, n, c, h * CH:(h + 1) * CH],
                                            xT[:, c, :], start=(c == 0), stop=(c == KC - 1))
                    ins.then_inc(qTs_psum, 1)
                for t in range(TT):
                    for c in range(KC):
                        ins = pe.matmul(bank[B_QK[t]][:, 0:2 * C], xT[:, c, t * P:(t + 1) * P], wqkv[:, n, c, 0:2 * C],
                                        start=(c == 0), stop=(c == KC - 1))
                    ins.then_inc(qk_psum, 1)
                if ATTN[n]["rel"]:
                    pe.wait_ge(qTs_ready, 2 * (n + 1))
                    for t in range(TT):
                        for h in range(KC):
                            pe.matmul(bank[B_REL[2 * t + h]][:, 0:RELH], qTs[:, h, t * P:(t + 1) * P], reltab[:, n],
                                      start=True, stop=True).then_inc(rel_psum, 1)
                for t in range(TT):
                    for c in range(KC):
                        ins = pe.matmul(bank[B_V][:, t * C:(t + 1) * C], xT[:, c, t * P:(t + 1) * P],
                                        wqkv[:, n, c, 2 * C:3 * C], start=(c == 0), stop=(c == KC - 1))
                ins.then_inc(v_psum, 1)
                if n == 0:
                    pe.wait_ge(kst_ready, 2 * TT)
                    pe.wait_ge(q_rel_ready, 4)
                elif n == 1:
                    pe.wait_ge(kst_ready, 3 * TT)
                pe.wait_ge(qk_ready, TT * (n + 1))
                for b in range(3):
                    for p in range(2):
                        for t in range(TT):
                            h = 2 * (2 * b + p)
                            ins = pe.transpose(bank[B_KT[b]][:, p * T + t * P:p * T + (t + 1) * P],
                                               k_st[:, t, h:h + 2, :].rearrange("p h s -> p (h s)"), ident)
                    ins.then_inc(kT_psum, 1)
                pe.wait_ge(q_rel_ready, 4 * (n + 1) if n < 3 else 13)
                for b in range(3):
                    for p in range(2):
                        for t in range(TT):
                            h = 2 * (2 * b + p)
                            ins = pe.transpose(bank[B_QT[b]][:, p * T + t * P:p * T + (t + 1) * P],
                                               q_st[:, t, h:h + 2, :].rearrange("p h s -> p (h s)"), ident)
                    ins.then_inc(qT_psum, 1)

                def scores(p):
                    b = p // 2
                    if p == 0:
                        pe.wait_ge(v_ready, n + 1)
                        pe.wait_ge(kT_act, 3 * (n + 1))
                        pe.wait_ge(kT_dve, 3 * (n + 1))
                        pe.wait_ge(qT_act, 2 * n + 1)
                    if p == 2:
                        pe.wait_ge(qT_dve, n + 1)
                    if p == 4:
                        pe.wait_ge(qT_act, 2 * n + 2)
                    for t in range(TT):
                        pe.matmul(bank[B_S[p % 2][t]][:, :], qT[:, p, t * P:(t + 1) * P],
                                  kT[:, p].rearrange("p h t -> p (h t)"), start=True, stop=True).then_inc(s_psum, 1)

                scores(0)
                scores(1)
                for p in range(PAIRS):
                    g = n * PAIRS + p
                    if p == 0:
                        pe.wait_ge(qT_dve, n + 1)
                    for t in range(TT):
                        pe.wait_ge(p_ready, 2 * g + t + 1)
                        for h in range(2):
                            for kt in range(TT):
                                ins = pe.transpose(bank[B_PT[kt]][:, h * T + t * P:h * T + (t + 1) * P],
                                                   probs[:, p % 2, t, h, kt * P:(kt + 1) * P], ident)
                    ins.then_inc(pT_psum, 1)
                    if p + 2 < PAIRS:
                        scores(p + 2)
                    pe.wait_ge(pT_act, g + 1)
                    pe.wait_ge(pT_dve, g + 1)
                    if p == 0:
                        pe.wait_ge(qT_act, 2 * n + 2)
                    if p == 4:
                        pe.wait_ge(o_ready, GROUPS * n + 1)
                    for kt in range(TT):
                        for h in range(2):
                            row = 32 * ((2 * p + h) % 4)
                            ins = pe.matmul(bank[B_O[p // 2]][row:row + 32, 0:T], v_st[:, kt, 2 * p + h, :],
                                            pT[:, p % 2, kt, h, :], start=(kt == 0), stop=(kt == TT - 1))
                    ins.then_inc(o_psum, 1)
                for g in range(GROUPS):
                    pe.wait_ge(o_ready, GROUPS * n + g + 1)
                for t in range(TT):
                    for g in range(GROUPS):
                        ins = pe.matmul(bank[B_PROJ][:, t * C:(t + 1) * C], oT[:, g, t * P:(t + 1) * P], wproj[:, n, g, :],
                                        start=(g == 0), stop=(g == GROUPS - 1))
                ins.then_inc(proj_psum, 1)

            def moe(m, k):
                cfg = MOE[m]
                pe.wait_ge(mw_in[m], {0: 48, 1: 80, 2: 32, 3: 48, 4: 48}[m])
                pe.wait_ge(xT_ready, k + 1)
                for t in range(TT):
                    for c in range(KC):
                        ins = pe.matmul(bank[B_R][:, t * E:(t + 1) * E], xT[:, c, t * P:(t + 1) * P], wr[:, m, c, :],
                                        start=(c == 0), stop=(c == KC - 1))
                ins.then_inc(r_psum, 1)

                def expert(j, i):
                    g = BASE[m] + i
                    s = g % 2
                    glu = cfg["act"] == "glu"
                    pe.wait_ge(slot_in[s], 32 * (j + g // 2 + 1))
                    for b in range(HB):
                        for c2 in range(2):
                            at = (2 * b + c2) * P
                            for c in range(KC):
                                ins = pe.matmul(bank[B_H[b]][:, c2 * T:(c2 + 1) * T], w1[s][:, c * 768 + at:c * 768 + at + P],
                                                xT[:, c, :], start=(c == 0), stop=(c == KC - 1))
                        ins.then_inc(h_psum, 1)
                    pe.wait_ge(acc_done, 2 * (2 * j + g))
                    nc2 = HB if glu else 2 * HB
                    for t in range(TT):
                        for c in range(nc2):
                            if t == 0 and glu:
                                pe.wait_ge(glu_ready, 3 * (2 * j + g - BASE[4]) + c + 1)
                            if t == 0 and not glu and c % 2 == 0:
                                pe.wait_ge(h_ready, 3 * (2 * j + g) + c // 2 + 1)
                            ins = pe.matmul(bank[B_Y[t]][:, 0:C], hid[:, c, t * P:(t + 1) * P], w2[s][:, c * C:(c + 1) * C],
                                            start=(c == 0), stop=(c == nc2 - 1))
                        ins.then_inc(y_psum, 1)

                for i in range(2):
                    expert(0, i)
                    if i == 0 and cfg["cap"]:
                        pe.wait_ge(sel_ready, 1)
                        earlier, ones = consts[:, CONST["earlier"]], consts[:, CONST["ones"]]
                        pe.matmul(bank[B_R][:, 64:64 + E], earlier, sel[:, 0, :], start=True, stop=True)
                        pe.matmul(bank[B_R][:, 64 + E:64 + 2 * E], ones, sel[:, 0, :], start=True, stop=False)
                        pe.matmul(bank[B_R][:, 64 + E:64 + 2 * E], earlier, sel[:, 1, :], start=False, stop=True)\
                            .then_inc(pos_psum, 1)
                    if cfg["b"]:
                        kb = (0, 1, None, 2)[m]
                        n = cfg["n"]
                        if i == 0:
                            pe.wait_ge(gates_ready, m + 1)
                            for t in range(TT):
                                ins = pe.transpose(bank[B_R][0:n, T + t * P:T + (t + 1) * P], gates[:, t, 0:n], ident)
                            ins.then_inc(gT_psum, 1)
                        else:
                            pe.wait_ge(gT_ready, kb + 1)
                            for t in range(TT):
                                ins = pe.matmul(bank[B_B2][:, t * C:(t + 1) * C], gT[0:n, t * P:(t + 1) * P], b2[0:n, kb, :],
                                                start=True, stop=True)
                            ins.then_inc(b2_psum, 1)
                with pe.Fori(1, E // 2) as j:
                    for i in range(2):
                        expert(j, i)
                if cfg["n"] > E:
                    expert(E // 2, 0)

            nln = 0
            for k, (kind, n) in enumerate(BLOCKS):
                if (kind, n) == ("attn", 3):
                    nln += 1
                x_transposed(k, nln)
                nln += 1
                (attn if kind == "attn" else moe)(n, k)

        @block.vector
        def _(dve):
            own = [0]

            def then(ins):
                own[0] += 1
                ins.then_inc(dve_own, 1)

            def settle():
                dve.wait_ge(dve_own, own[0])

            def ln(n, src, eps, dst=xn):
                for t in range(TT):
                    then(dve.bn_stats(stats[:, t, :], src[:, t, :]))
                settle()
                for t in range(TT):
                    then(dve.bn_aggr(moments[:, t, :], stats[:, t, :]))
                settle()
                dve.tensor_scalar(var_eps[:, :], moments[:, :, 1], eps, None, ALU.add).then_inc(var_ready, 1)
                dve.wait_ge(rstd_ready, n + 1)
                for t in range(TT):
                    dve.tensor_scalar(dst[:, t, :], src[:, t, :], moments[:, t, 0:1], rstd[:, t:t + 1],
                                      ALU.subtract, ALU.mult).then_inc(xn_ready, 1)

            def attn(n):
                src = tln if n == 3 else x
                scale = float(HD) ** -0.5
                heads = "p (h d) -> p h d"
                if ATTN[n]["rel"]:
                    dve.wait_ge(aw_in[n], 96)
                    then(dve.tensor_scalar(bq4[:, n, :], bqkv[:, n, 0:C], scale, None, ALU.mult))
                    dve.wait_ge(qTs_psum, n + 1)
                    for h in range(KC):
                        dve.tensor_scalar(qTs[:, h, :], bank[B_QT0][0:CH, h * T:(h + 1) * T], bq_col[:, n, h:h + 1], None, ALU.add)\
                            .then_inc(qTs_ready, 1)
                    settle()
                if n == 0:
                    dve.wait_ge(pool_ready, 5)
                for t in range(TT):
                    dve.wait_ge(qk_psum, TT * n + t + 1)
                    qp = bank[B_QK[t]][:, 0:C].rearrange(heads, h=NH)
                    kp = bank[B_QK[t]][:, C:2 * C].rearrange(heads, h=NH)
                    if ATTN[n]["rel"]:
                        dve.scalar_tensor_tensor(q_st[:, t, :, 0:HD], qp, scale, bq4[:, n, :].rearrange(heads, h=NH),
                                                 ALU.mult, ALU.add)
                        dve.tensor_tensor(k_st[:, t, :, 0:HD], kp, bqkv[:, n, C:2 * C].rearrange(heads, h=NH), ALU.add)\
                            .then_inc(qk_ready, 1)
                    else:
                        dve.tensor_scalar(q_st[:, t, :, 0:HD], qp, scale, None, ALU.mult)
                        dve.tensor_copy(k_st[:, t, :, 0:HD], kp).then_inc(qk_ready, 1)
                if ATTN[n]["rel"]:
                    for t in range(TT):
                        dve.wait_ge(rel_psum, 4 * n + 2 * t + 1)
                        dve.tensor_copy(relall[:, t, :, 0:NH // 2],
                                        bank[B_REL[2 * t]][:, 0:RELH].rearrange("p (r n) -> p r n", n=NH // 2))\
                            .then_inc(rel_dve, 1)
                dve.wait_ge(v_psum, n + 1)
                for t in range(TT):
                    vp = bank[B_V][:, t * C:(t + 1) * C].rearrange(heads, h=NH)
                    if ATTN[n]["rel"]:
                        ins = dve.tensor_tensor(v_st[:, t, :, 0:HD], vp, bqkv[:, n, 2 * C:3 * C].rearrange(heads, h=NH), ALU.add)
                    else:
                        ins = dve.tensor_copy(v_st[:, t, :, 0:HD], vp)
                ins.then_inc(v_ready, 1)
                for b in range(3):
                    dve.wait_ge(kT_psum, 3 * n + b + 1)
                    dve.tensor_copy(kT[SLOT:P, 2 * b:2 * b + 2, 1, :],
                                    bank[B_KT[b]][SLOT:P, :].rearrange("p (a t) -> p a t", a=2)).then_inc(kT_dve, 1)
                if ATTN[n]["rel"]:
                    for t in range(TT):
                        then(dve.tensor_tensor(xb[:, t, :], src[:, t, :], bproj[:, n, :], ALU.add))
                dve.wait_ge(qT_psum, 3 * n + 2)
                dve.tensor_copy(qT[:, 2:4, :].rearrange("p a t -> p (a t)"), bank[B_QT[1]][:, :]).then_inc(qT_dve, 1)

                def row_max(p):
                    for t in range(TT):
                        dve.wait_ge(s_psum, 2 * (n * PAIRS + p) + t + 1)
                        s = bank[B_S[p % 2][t]][:, :].rearrange("p (h k) -> p h k", h=2)
                        if n == 3:
                            at = CONST["causal"].start + t * T
                            mask = consts[:, at:at + T].unsqueeze(1).broadcast_to([P, 2, T])
                            then(dve.tensor_tensor(smask[:, p % 2, t], s, mask, ALU.add))
                            settle()
                            s = smask[:, p % 2, t]
                        dve.tensor_reduce(nmax[:, p % 2, t, :], s, AX.X, ALU.max, negate=True).then_inc(nmax_ready, 1)

                def recip(p):
                    dve.wait_ge(exp_ready, 4 * (n * PAIRS + p + 1))
                    dve.reciprocal(rinv[:, p % 2].rearrange("p t h -> p (t h)"), rsum[:, p % 2].rearrange("p t h -> p (t h)"))\
                        .then_inc(rinv_ready, 1)

                row_max(0)
                row_max(1)
                recip(0)
                for p in range(PAIRS):
                    if p + 1 < PAIRS:
                        recip(p + 1)
                    dve.wait_ge(pT_psum, n * PAIRS + p + 1)
                    dve.tensor_copy(pT[:, p % 2, 1].rearrange("p h t -> p (h t)"), bank[B_PT[1]][:, :]).then_inc(pT_dve, 1)
                    if p + 2 < PAIRS:
                        row_max(p + 2)
                dve.wait_ge(proj_psum, n + 1)
                settle()
                res = (tln if n == 3 else xb)[:, :, :].rearrange("p t c -> p (t c)")
                dst = (tln if n == 3 else x)[:, :, :].rearrange("p t c -> p (t c)")
                then(dve.tensor_tensor(dst, bank[B_PROJ][:, 0:TT * C], res, ALU.add))
                settle()

            def moe(m):
                cfg = MOE[m]
                iota = consts[:, CONST["iota"]]
                dve.wait_ge(r_psum, m + 1)
                lp = bank[B_R][:, 0:TT * E].rearrange("p (t e) -> p t e", t=TT)
                if cfg["rbias"]:
                    dve.wait_ge(mw_in[m], {1: 80, 4: 48}[m])
                    then(dve.tensor_tensor(logits[:, :, :], lp, rbias[:, m // 4], ALU.add))
                else:
                    then(dve.tensor_copy(logits[:, :, :], lp))
                settle()
                for t in range(TT):
                    then(dve.max(top8[:, t, :], logits[:, t, :]))
                settle()
                dve.tensor_scalar(nmax_l[:, :], top8[:, :, 0], -1.0, None, ALU.mult).then_inc(negm_ready, 1)
                for t in range(TT):
                    then(dve.max_index(top_i[:, t, :], top8[:, t, :], logits[:, t, :]))
                settle()
                then(dve.tensor_copy(top_f[:, :, :], top_i[:, :, 0:2]))
                settle()
                for t in range(TT):
                    then(dve.tensor_scalar(first[:, t, :], iota, top_f[:, t, 0:1], None, ALU.is_equal))
                settle()
                for t in range(TT):
                    ins = dve.scalar_tensor_tensor(sel[:, t, :], iota, top_f[:, t, 1:2], first[:, t, :], ALU.is_equal, ALU.add)
                    if cfg["cap"] and t:
                        ins.then_inc(sel_ready, 1)
                    else:
                        then(ins)
                settle()
                if cfg["cap"]:
                    dve.wait_ge(sel_ready, 1)
                dve.wait_ge(expl_ready, 2 * (m + 1))
                then(dve.tensor_tensor(chosen[:, :, :], expl[:, :, :], sel[:, :, :], ALU.mult))
                settle()
                then(dve.tensor_reduce(den[:, :], (expl if cfg["over_all"] else chosen)[:, :, :], AX.X, ALU.add))
                settle()
                then(dve.reciprocal(rden[:, :], den[:, :]))
                settle()
                if cfg["cap"]:
                    dve.wait_ge(pos_psum, 1)
                    then(dve.tensor_scalar(valid[:, :, :], bank[B_R][:, 64:64 + TT * E].rearrange("p (t e) -> p t e", t=TT),
                                           float(CAP), None, ALU.is_lt))
                    settle()
                    then(dve.tensor_tensor(chosen[:, :, :], chosen[:, :, :], valid[:, :, :], ALU.mult))
                    settle()
                for t in range(TT):
                    ins = dve.tensor_scalar(gates[:, t, 0:E], chosen[:, t, :], rden[:, t:t + 1], None, ALU.mult)
                    if t == 0:
                        then(ins)
                ins.then_inc(gates_ready, 1)
                settle()
                dve.wait_ge(gates_ready, m + 1)

                def expert(j, i):
                    g = BASE[m] + i
                    if cfg["act"] == "glu":
                        for b in range(HB):
                            dve.wait_ge(silu_ready, 3 * (2 * j + i) + b + 1)
                            dve.tensor_tensor(hid[:, b, :], silu_g[:, b, :], bank[B_H[b]][:, T:2 * T], ALU.mult)\
                                .then_inc(glu_ready, 1)
                    for t in range(TT):
                        dve.wait_ge(y_psum, 2 * (2 * j + g) + t + 1)
                        dve.scalar_tensor_tensor(x[:, t, :], bank[B_Y[t]][:, 0:C], gates[:, t, bass.ds(2 * j + i, 1)],
                                                 x[:, t, :], ALU.mult, ALU.add).then_inc(acc_done, 1)

                if m == 2:
                    then(dve.tensor_tensor(x[:, :, :], x[:, :, :], tln[:, :, :], ALU.add))
                    settle()
                for i in range(2):
                    expert(0, i)
                if cfg["b"]:
                    k = (0, 1, None, 2)[m]
                    dve.wait_ge(b2_psum, k + 1)
                    dve.wait_ge(acc_done, 2 * (BASE[m] + 2))
                    then(dve.tensor_tensor(x[:, :, :], bank[B_B2][:, 0:TT * C].rearrange("p (t c) -> p t c", t=TT), x[:, :, :], ALU.add))
                    settle()
                with dve.Fori(1, E // 2) as j:
                    for i in range(2):
                        expert(j, i)
                if cfg["n"] > E:
                    expert(E // 2, 0)
                dve.wait_ge(acc_done, 2 * BASE[m + 1])

            dve.wait_ge(x_in, 16)
            nln = 0
            for kind, n in BLOCKS:
                if (kind, n) == ("attn", 3):
                    ln(nln, x, 1e-5, tln)
                    nln += 1
                    dve.wait_ge(xn_ready, 2 * nln)
                    ln(nln, tln, 1e-5)
                elif (kind, n) == ("moe", 2):
                    ln(nln, tln, 1e-5)
                else:
                    ln(nln, x, (ATTN if kind == "attn" else MOE)[n]["eps"])
                nln += 1
                (attn if kind == "attn" else moe)(n)


def _layout(i):
    import numpy as np

    def rows(w):
        return np.ascontiguousarray(w.reshape(KC, CH, -1).transpose(1, 0, 2))

    def heads_padded(w):
        p = np.zeros((GROUPS, 4, 32, w.shape[1]), w.dtype)
        p[:, :, :HD] = w.reshape(GROUPS, 4, HD, -1)
        return np.ascontiguousarray(p.reshape(GROUPS, P, -1).transpose(1, 0, 2))

    def rel_table(th, tw, n):
        t = np.zeros((NH // KC, HD, RELS, NH // KC), th.dtype)
        tw = tw[:REL]
        both = np.concatenate([th[:REL], tw if n else tw[::-1]], 0).T
        for h in range(NH // KC):
            t[h, :, :, h] = both
        return np.ascontiguousarray(t.reshape(CH, RELH))

    def up(w):
        return np.ascontiguousarray(w.reshape(w.shape[0], KC, CH, -1).transpose(0, 2, 1, 3).reshape(w.shape[0], CH, -1))

    def down(w):
        n = w.shape[0]
        return np.ascontiguousarray(w.reshape(n, -1, P, C).transpose(0, 2, 1, 3).reshape(n, P, -1))

    def cols(b):
        return np.ascontiguousarray(b.reshape(b.shape[0], -1, P).transpose(2, 0, 1).reshape(P, -1))

    a = {"x": i["x"].reshape(T, C)}
    qkv = [np.concatenate([i[f"L0_conv_w{n}"].reshape(C, C).T for n in "qkv"], 1), i["L1_conv_qkv_w"],
           i["L2_conv_qkv_w"], i["L2_ffn_c_attn_w"].T]
    bias = [np.concatenate([i[f"L0_conv_b{n}"].reshape(C) for n in "qkv"]), i["L1_conv_qkv_b"], i["L2_conv_qkv_b"]]
    proj = [i["L0_conv_proj_w"].T, i["L1_conv_proj_w"], i["L2_conv_proj_w"], i["L2_ffn_c_proj_w"].T]
    for n in range(4):
        a[f"A{n}_wqkv"] = rows(qkv[n])
        a[f"A{n}_wproj"] = heads_padded(proj[n])
        if n < 3:
            a[f"A{n}_bqkv"] = bias[n]
            a[f"A{n}_bproj"] = i[f"L{n}_conv_proj_b"]
            a[f"A{n}_bq"] = np.ascontiguousarray(bias[n][:C].reshape(KC, CH).T)
            a[f"A{n}_reltab"] = rel_table(i[f"L{n}_conv_rel_pos_h"], i[f"L{n}_conv_rel_pos_w"], n)
    w1 = [i["L0_ffn_W1"], i["L1_ffn_Wfc"], i["L2_ffn_c_fc"],
          np.concatenate([i["L3_conv_w1"], i["L3_conv_ws1"][None]], 0).transpose(0, 2, 1)]
    w2 = [i["L0_ffn_W2"], i["L1_ffn_Wproj"], i["L2_ffn_c_proj_e"],
          np.concatenate([i["L3_conv_w2"], i["L3_conv_ws2"][None]], 0).transpose(0, 2, 1)]
    gu = [np.concatenate([i[f"L3_ffn_{n}_r"], i[f"L3_ffn_{n}_s"]], 0).reshape(E + 1, C, HB, 1, P) for n in ("Wg", "Wu")]
    w1.append(np.concatenate(gu, 3).reshape(E + 1, C, 2 * HB * P))
    w2.append(np.concatenate([i["L3_ffn_Wd_r"], i["L3_ffn_Wd_s"]], 0))
    wr = [i["L0_ffn_Wg"], i["L1_ffn_Wr"], i["L2_ffn_w_g"].T, i["L3_conv_gate_w"].T, i["L3_ffn_W_router"]]
    for m in range(5):
        a[f"M{m}_w1"], a[f"M{m}_w2"], a[f"M{m}_wr"] = up(w1[m]), down(w2[m]), rows(wr[m])
    a["M1_rbias"], a["M4_rbias"] = i["L1_ffn_br"], i["L3_ffn_expert_bias"]
    a["M0_b1"], a["M0_b2"] = cols(i["L0_ffn_b1"]), i["L0_ffn_b2"]
    a["M1_b1"], a["M1_b2"] = cols(i["L1_ffn_bfc"]), i["L1_ffn_bproj"]
    a["M3_b1"] = cols(np.concatenate([i["L3_conv_b1"], i["L3_conv_bs1"][None]], 0))
    a["M3_b2"] = np.concatenate([i["L3_conv_b2"], i["L3_conv_bs2"][None]], 0)
    a["lnw"] = np.ascontiguousarray(np.stack([i["L2_ffn_ln1_w"], i["L2_ffn_ln2_w"]], 0).reshape(2, KC, CH).transpose(2, 0, 1))
    c = np.zeros((P, CONST_W), np.float32)
    c[:, CONST["ident"]] = np.eye(P)
    c[:, CONST["earlier"]] = np.triu(np.ones((P, P)), 1)
    c[:, CONST["ones"]] = 1.0
    c[:, CONST["iota"]] = np.arange(E)
    tok = np.arange(T)
    hot = np.zeros((T, 2, SIDE), np.float32)
    hot[tok, 0, SIDE - 1 - tok // SIDE] = 1.0
    hot[tok, 1, SIDE - 1 - tok % SIDE] = 1.0
    c[:, CONST["onehot"]] = hot.reshape(TT, P, 2 * SIDE).transpose(1, 0, 2).reshape(P, -1)
    row = (tok[:, None] // SIDE == np.arange(SIDE)).astype(np.float32)
    c[:, CONST["rowhot"]] = row.reshape(TT, P, SIDE).transpose(1, 0, 2).reshape(P, -1)
    mask = np.where(tok[None, :] > tok[:, None], np.float32(NEG), np.float32(0.0))
    c[:, CONST["causal"]] = mask.reshape(TT, P, T).transpose(1, 0, 2).reshape(P, -1)
    a["consts"] = c
    return a


def kernel(**inputs):
    import numpy as _np
    import concourse.bacc as _bacc
    from concourse import mybir as _mybir
    from concourse.bass_utils import run_bass_kernel_spmd as _run

    nc = _bacc.Bacc("TRN2", target_bir_lowering=False, num_devices=1)
    arrays, args = {}, {}
    for name, v in _layout({k: _np.asarray(v) for k, v in inputs.items()}).items():
        v = _np.ascontiguousarray(v)
        arrays[f"in_{name}_dram"] = v
        args[name] = nc.dram_tensor(f"in_{name}_dram", v.shape, _mybir.dt.from_np(v.dtype), kind="ExternalInput").ap()
    out = nc.dram_tensor("out_dram", (T, C), F32, kind="ExternalOutput").ap()
    metaformer_kernel(nc, args, out)
    r = _run(nc, [arrays], core_ids=[0])
    return r.results[0]["out_dram"].reshape(1, SIDE, SIDE, C)
```

```python
from contextlib import ExitStack

import concourse.bass as bass
from concourse import mybir

F32 = mybir.dt.float32
F32R = mybir.dt.float32r
U32 = mybir.dt.uint32
ALU = mybir.AluOpType
ACT = mybir.ActivationFunctionType
AX = mybir.AxisListType

P = 128
SIDE = 16
T = SIDE * SIDE
TT = T // P
C = 192
KC = 2
CH = C // KC
NH = 12
HD = C // NH
SLOT = 64
PAIRS = NH // 2
GROUPS = NH // 4
REL = 2 * SIDE - 1
RELS = 2 * REL
RELW = RELS * NH
RELH = RELW // KC
E = 8
HB = 3
CAP = 64
NEG = -3.0e38

CONST = {}
_at = 0
for _name, _n in (("ident", P), ("earlier", P), ("ones", P), ("iota", E), ("onehot", TT * 2 * SIDE), ("rowhot", TT * SIDE), ("places", 64),
                  ("causal", TT * T)):
    CONST[_name] = slice(_at, _at + _n)
    _at += _n
CONST_W = _at

ATTN = (dict(rel=True, eps=1e-6), dict(rel=True, eps=1e-6), dict(rel=True, eps=1e-6), dict(rel=False, eps=1e-5))
MOE = (
    dict(n=8, act="relu", b=True, rbias=False, over_all=True, cap=False, eps=1e-5),
    dict(n=8, act="gelu_tanh", b=True, rbias=True, over_all=False, cap=False, eps=1e-5),
    dict(n=8, act="gelu", b=False, rbias=False, over_all=False, cap=True, eps=1e-5),
    dict(n=9, act="gelu", b=True, rbias=False, over_all=False, cap=False, eps=1e-6),
    dict(n=9, act="glu", b=False, rbias=True, over_all=False, cap=False, eps=1e-5),
)
BASE = [sum(m["n"] for m in MOE[:i] if not m["cap"]) for i in range(len(MOE) + 1)]
EP = E // 2
SHIFT = (0, 0, 0, 0, 1)
CAP_SLOT = (0, 1, 2, 3, 4, 5, 0, 1)
USED = ((0, 0), (4, 4), (8, 8), (10, 10), (15, 14))
FUNC = {"relu": ACT.Relu, "gelu_tanh": ACT.Gelu_apprx_tanh, "gelu": ACT.Gelu, "glu": ACT.Silu}
BLOCKS = (("attn", 0), ("moe", 0), ("attn", 1), ("moe", 1), ("attn", 2), ("attn", 3), ("moe", 2), ("moe", 3), ("moe", 4))


def metaformer_kernel(nc, a, out):
    ctx = ExitStack()
    with ctx:
        def sb(name, shape, dt=F32):
            return ctx.enter_context(nc.sbuf_tensor(name, shape, dt))

        def sem(name):
            return ctx.enter_context(nc.semaphore(name))

        x = sb("x", [P, TT, C])
        tln = sb("tln", [P, TT, C])
        xb = sb("xb", [P, TT, C])
        stats = sb("stats", [P, TT, 6])
        moments = sb("moments", [P, TT, 2])
        var_eps = sb("var_eps", [P, TT])
        minus_half = sb("minus_half", [P, TT])
        rstd = sb("rstd", [P, TT])
        xn = sb("xn", [P, TT, C])
        xT = sb("xT", [CH, KC, T])
        consts = sb("consts", [P, CONST_W])
        ident = consts[:, CONST["ident"]]
        wqkv = sb("wqkv", [CH, 4, KC, 3 * C])
        wproj = sb("wproj", [P, 4, GROUPS, C])
        bqkv = sb("bqkv", [P, 3, 3 * C])
        bproj = sb("bproj", [P, 3, C])
        bq4 = sb("bq4", [P, 3, C])
        bq_col = sb("bq_col", [CH, 3, KC])
        reltab = sb("reltab", [CH, 3, RELH])
        qTs = sb("qTs", [CH, KC, T])
        relall = sb("relall", [P, TT, RELS, NH])
        rel = sb("rel", [P, TT, 2, SIDE, NH])
        q_st = sb("q_st", [P, TT, NH, SLOT])
        k_st = sb("k_st", [P, TT, NH, SLOT])
        v_st = sb("v_st", [P, TT, NH, 32])
        qT = sb("qT", [P, PAIRS, T])
        kT = sb("kT", [P, PAIRS, 2, T])
        smask = sb("smask", [P, 2, TT, 2, T])
        nmax = sb("nmax", [P, 2, TT, 2])
        rsum = sb("rsum", [P, 2, TT, 2])
        rinv = sb("rinv", [P, 2, TT, 2])
        probs = sb("probs", [P, 2, TT, 2, T])
        pT = sb("pT", [P, 2, TT, 2, T])
        oT = sb("oT", [P, GROUPS, T])
        w1 = [sb(f"w1_{s}", [CH, KC * 768]) for s in range(4)]
        w2 = [sb(f"w2_{s}", [P, 2 * HB * C]) for s in range(4)]
        w1 += [wqkv[:, :, :, :].rearrange("p i c n -> p (i c n)")[:, k * KC * 768:(k + 1) * KC * 768] for k in range(2)]
        w2 += [wproj[:, :, :, :].rearrange("p i g n -> p (i g n)")[:, 0:2 * HB * C],
               bqkv[:, :, :].rearrange("p i n -> p (i n)")[:, 0:2 * HB * C]]
        wr = sb("wr", [CH, 5, KC, E])
        rbias = sb("rbias", [P, 2, TT, E])
        b1 = sb("b1", [P, 3, 9 * 2 * HB])
        b2 = sb("b2", [9, 3, C])
        lnw = sb("lnw", [CH, 2, KC])
        w1_hi, w1_lo = sb("w1_hi", [CH, KC, 768], F32R), sb("w1_lo", [CH, KC, 768], F32R)
        xT_hi, xT_lo = sb("xT_hi", [CH, KC, T], F32R), sb("xT_lo", [CH, KC, T], F32R)
        hid = sb("hid", [P, 2 * HB, T])
        silu_g = sb("silu_g", [P, HB, T])
        logits = sb("logits", [P, TT, E])
        top8 = sb("top8", [P, TT, 8])
        top_i = sb("top_i", [P, TT, 8], U32)
        top_f = sb("top_f", [P, TT, 2])
        nmax_l = sb("nmax_l", [P, TT])
        expl = sb("expl", [P, TT, E])
        first = sb("first", [P, TT, E])
        sel = sb("sel", [P, TT, E])
        chosen = sb("chosen", [P, TT, E])
        den = sb("den", [P, TT])
        rden = sb("rden", [P, TT])
        place = sb("place", [P, TT, E])
        gates = sb("gates", [P, TT, E + 1])
        gT = sb("gT", [E + 1, T])
        disp = probs[:, 0].rearrange("p t h k -> p t (h k)")
        comb = probs[:, 1].rearrange("p t h k -> p t (h k)")
        combT = pT[:, 0].rearrange("p t h k -> p (t h) k")
        xdT = pT[0:CH, 1].rearrange("p t h k -> p t (h k)")
        hplace = smask[:, 0].rearrange("p t h k -> p (t h k)")[:, 0:768]
        hplaceT = hid[:, 0:HB, :].rearrange("p c t -> p (c t)")
        yplace = smask[:, 1].rearrange("p t h k -> p (t h k)")[:, 0:C]
        scratch = nc.dram_tensor("rel_scratch", [3, T, RELW], F32, kind="Internal").ap()

        bank = [ctx.enter_context(nc.psum_tensor(f"bank{i}", [P, 512], F32)) for i in range(8)]
        B_QT0, B_QK, B_REL, B_V = 0, (1, 2), (3, 4, 5, 6), 7
        B_KT, B_QT = (0, 1, 2), (3, 4, 5)
        B_S, B_PT, B_O, B_PROJ = ((6, 7), (0, 1)), (2, 3), (4, 5, 4), 2
        B_H, B_Y, B_R, B_B2, B_LN = (0, 1, 2), (3, 4), 5, 6, 7
        B_XD, B_HP, B_HT, B_YP, B_SUM = (0, 1), ((0, 1), (2, 3)), (5, 6), 7, 4

        x_in, c_in = sem("x_in"), sem("consts_in")
        aw_in = [sem(f"attn_weights_in{i}") for i in range(4)]
        mw_in = [sem(f"moe_small_in{i}") for i in range(5)]
        slot_in = [sem(f"expert_weights_in{s}") for s in range(6)]
        rel_out = [sem(f"rel_to_dram{t}") for t in range(TT)]
        rel_in = [sem(f"rel_from_dram{t}") for t in range(TT)]
        y_out = sem("result_out")
        dve_own, pool_own = sem("dve_own"), sem("pool_own")
        pool_ready = sem("pool_constants_ready")
        kst_ready = sem("k_onehots_ready")
        var_ready, rstd_ready, xn_ready = sem("var_ready"), sem("rstd_ready"), sem("xn_ready")
        xT_psum, xT_ready = sem("xT_psum"), sem("xT_ready")
        qTs_psum, qTs_ready = sem("qTs_psum"), sem("qTs_ready")
        qk_psum, qk_ready = sem("qk_psum"), sem("qk_ready")
        rel_psum, rel_dve, rel_act = sem("rel_psum"), sem("rel_copied_dve"), sem("rel_copied_act")
        q_rel_ready = sem("q_rel_ready")
        v_psum, v_ready = sem("v_psum"), sem("v_ready")
        kT_psum, kT_dve, kT_act = sem("kT_psum"), sem("kT_dve"), sem("kT_act")
        qT_psum, qT_dve, qT_act = sem("qT_psum"), sem("qT_dve"), sem("qT_act")
        s_psum, nmax_ready, exp_ready = sem("scores_psum"), sem("nmax_ready"), sem("exp_ready")
        rinv_ready, p_ready = sem("rinv_ready"), sem("probs_ready")
        pT_psum, pT_dve, pT_act = sem("pT_psum"), sem("pT_dve"), sem("pT_act")
        o_psum, o_ready = sem("o_psum"), sem("o_ready")
        proj_psum = sem("proj_psum")
        r_psum, negm_ready, expl_ready = sem("router_psum"), sem("neg_logit_max_ready"), sem("exp_logits_ready")
        sel_ready, pos_psum, gates_ready = sem("selection_ready"), sem("positions_psum"), sem("gates_ready")
        gT_psum, gT_ready, b2_psum = sem("gatesT_psum"), sem("gatesT_ready"), sem("b2_psum")
        h_psum, h_ready = sem("hidden_psum"), sem("hidden_ready")
        silu_ready, glu_ready = sem("silu_ready"), sem("glu_ready")
        xT_hi_ready, xT_lo_ready = sem("xT_high_ready"), sem("xT_low_ready")
        w1_hi_ready, w1_lo_ready = sem("w1_high_ready"), sem("w1_low_ready")
        disp_ready, comb_ready = sem("dispatch_ready"), sem("combine_ready")
        xd_psum, xd_act, xd_dve = sem("dispatched_psum"), sem("dispatched_act"), sem("dispatched_dve")
        combT_psum, combT_act, combT_dve = sem("combT_psum"), sem("combT_act"), sem("combT_dve")
        hp_psum, hp_ready = sem("pair_hidden_psum"), sem("pair_hidden_ready")
        hpT_psum, hpT_act, hpT_dve = sem("pair_hiddenT_psum"), sem("pair_hiddenT_act"), sem("pair_hiddenT_dve")
        yp_psum, yp_ready, sum_psum = sem("pair_out_psum"), sem("pair_out_ready"), sem("sum_psum")
        y_psum, acc_done = sem("expert_out_psum"), sem("expert_out_added")

        def w1_cols(w, b):
            w = w[:, :] if len(w.shape) == 2 else w[:, :, :].rearrange("p k n -> p (k n)")
            return w.rearrange("p (k n) -> p k n", k=KC)[:, :, b * 2 * P:(b + 1) * 2 * P]

        def split_count(m):
            return m + 1 if m < 2 else m

        def rel_ap(i, t, along):
            step_h, step_w = SIDE * RELW, RELW
            if along == 0:
                first_at, step_h = t * (SIDE // TT) * NH, step_h + NH
            else:
                first_at, step_w = REL * NH, step_w + NH
            return bass.AP(scratch.tensor, i * T * RELW + t * P * RELW + first_at,
                           [[step_h, SIDE // TT], [step_w, SIDE], [1, SIDE * NH]])

        def rel_keys_ap(kh):
            return bass.AP(scratch.tensor, kh * (RELW - NH) + (REL + SIDE - 1) * NH,
                           [[NH, SIDE], [SIDE * RELW, SIDE], [1, NH]])

        def rel_loads(n):
            return 16 * (1 + SIDE // TT) + 32 * n

        block = ctx.enter_context(nc.Block())

        @block.sync
        def _(sp):
            def load_expert(m, j, i):
                e = 2 * j + i
                s = (i + SHIFT[m]) % 2
                first = isinstance(j, int) and j == 0
                if m == 2:
                    s = CAP_SLOT[e]
                    if e < 2:
                        sp.wait_ge(y_psum, 2 * (BASE[m] + i - 1))
                    elif e in (4, 5):
                        sp.wait_ge(v_psum, 3)
                    elif e >= 6:
                        sp.wait_ge(yp_psum, 1)
                elif m == 3 and first:
                    sp.wait_ge(yp_psum, EP)
                elif m or not first:
                    sp.wait_ge(y_psum, 2 * (2 * j + BASE[m] + i - 1))
                n2 = a[f"M{m}_w2"].shape[2]
                sp.dma_start(w1[s][:, :], a[f"M{m}_w1"][bass.ds(e, 1)].rearrange("a p n -> (a p) n"))\
                    .then_inc(slot_in[s], 16)
                sp.dma_start(w2[s][:, 0:n2], a[f"M{m}_w2"][bass.ds(e, 1)].rearrange("a p n -> (a p) n"))\
                    .then_inc(slot_in[s], 16)

            def load_attn(i):
                sp.dma_start(wqkv[:, i], a[f"A{i}_wqkv"]).then_inc(aw_in[i], 16)
                sp.dma_start(wproj[:, i], a[f"A{i}_wproj"]).then_inc(aw_in[i], 16)
                if ATTN[i]["rel"]:
                    sp.dma_start(bq_col[:, i], a[f"A{i}_bq"]).then_inc(aw_in[i], 16)
                    sp.dma_start(reltab[:, i], a[f"A{i}_reltab"]).then_inc(aw_in[i], 16)
                    sp.dma_start(bqkv[:, i], a[f"A{i}_bqkv"].partition_broadcast(P)).then_inc(aw_in[i], 16)
                    sp.dma_start(bproj[:, i], a[f"A{i}_bproj"].partition_broadcast(P)).then_inc(aw_in[i], 16)

            def load_small(m):
                sp.dma_start(wr[:, m], a[f"M{m}_wr"]).then_inc(mw_in[m], 16)
                if MOE[m]["rbias"]:
                    for t in range(TT):
                        sp.dma_start(rbias[:, m // 4, t], a[f"M{m}_rbias"].partition_broadcast(P)).then_inc(mw_in[m], 16)
                if MOE[m]["b"]:
                    n = MOE[m]["n"]
                    k = (0, 1, None, 2)[m]
                    sp.dma_start(b1[:, k, 0:n * 2 * HB], a[f"M{m}_b1"]).then_inc(mw_in[m], 16)
                    sp.dma_start(b2[0:n, k], a[f"M{m}_b2"]).then_inc(mw_in[m], 16)

            sp.dma_start(x[:, :, :], a["x"].rearrange("(t p) c -> p t c", p=P)).then_inc(x_in, 16)
            sp.dma_start(consts[:, :], a["consts"]).then_inc(c_in, 16)
            load_attn(0)
            load_small(0)
            nrel = 0
            for kind, n in BLOCKS:
                if kind == "attn":
                    if n < 3:
                        if n == 2:
                            load_expert(2, 1, 0)
                            load_expert(2, 1, 1)
                        for i in range(2):
                            load_expert(n, 0, i)
                        if n < 2:
                            load_attn(n + 1)
                            load_small(n + 1)
                        else:
                            load_attn(3)
                            for m in (2, 3, 4):
                                load_small(m)
                            sp.dma_start(lnw[:, :, :], a["lnw"]).then_inc(mw_in[2], 16)
                    if ATTN[n]["rel"]:
                        for t in range(TT):
                            sp.wait_ge(rel_dve, TT * n + t + 1)
                            sp.wait_ge(rel_act, TT * n + t + 1)
                            sp.dma_start(scratch[n, t * P:(t + 1) * P, :], relall[:, t].rearrange("p r n -> p (r n)"))\
                                .then_inc(rel_out[t], 16)
                        for t in range(TT):
                            sp.wait_ge(rel_out[t], 16 * (n + 1))
                            if n == 0 and t == 0:
                                sp.wait_ge(rel_out[1], 16)
                            for along in range(1 if n == 0 else 2):
                                sp.dma_start(rel[:, t, along].rearrange("p r n -> p (r n)"), rel_ap(n, t, along))\
                                    .then_inc(rel_in[t], 16)
                            for k in range(SIDE // TT if n == 0 else 0):
                                sp.dma_start(rel[k * SIDE:(k + 1) * SIDE, t, 1], rel_keys_ap(t * (SIDE // TT) + k))\
                                    .then_inc(rel_in[t], 16)
                    if n == 2:
                        for e in (4, 5):
                            load_expert(2, e // 2, e % 2)
                else:
                    if n > 2:
                        for i in range(2):
                            load_expert(n, 0, i)
                    if n == 2:
                        for e in (6, 7):
                            load_expert(n, e // 2, e % 2)
                        continue
                    with sp.Fori(1, E // 2) as j:
                        for i in range(2):
                            load_expert(n, j, i)
                    if MOE[n]["n"] > E:
                        load_expert(n, E // 2, 0)
            sp.wait_ge(acc_done, 2 * BASE[-1])
            sp.dma_start(out.rearrange("(t p) c -> p t c", p=P), x[:, :, :]).then_inc(y_out, 16)
            sp.wait_ge(y_out, 16)

        @block.gpsimd
        def _(pool):
            own = [0]

            def then(ins):
                own[0] += 1
                ins.then_inc(pool_own, 1)

            def ln(n):
                pool.wait_ge(var_ready, n + 1)
                pool.tensor_tensor(rstd[:, :], var_eps[:, :], minus_half[:, :], ALU.pow).then_inc(rstd_ready, 1)

            pool.memset(minus_half[:, :], -0.5).then_inc(pool_own, 1)
            pool.wait_ge(pool_own, 1)
            ln(0)
            pool.memset(q_st[:, :, :, :], 0.0).then_inc(pool_ready, 1)
            pool.memset(k_st[:, :, :, :], 0.0).then_inc(pool_ready, 1)
            pool.memset(v_st[:, :, :, :], 0.0).then_inc(pool_ready, 1)
            pool.memset(kT[:, :, :, :], 0.0).then_inc(pool_ready, 1)
            pool.memset(gates[:, :, E:E + 1], 1.0).then_inc(pool_ready, 1)
            pool.wait_ge(c_in, 16)
            pool.wait_ge(pool_ready, 2)
            for t in range(TT):
                at = CONST["onehot"].start + t * 2 * SIDE
                oh = consts[:, at:at + SIDE].unsqueeze(1).broadcast_to([P, NH, SIDE])
                pool.tensor_copy(k_st[:, t, :, HD:HD + SIDE], oh).then_inc(kst_ready, 1)
                at = CONST["rowhot"].start + t * SIDE
                oh = consts[:, at:at + SIDE].unsqueeze(1).broadcast_to([P, NH, SIDE])
                pool.tensor_copy(q_st[:, t, :, HD + SIDE:HD + 2 * SIDE], oh).then_inc(kst_ready, 1)

            def attn(n):
                if n == 1:
                    pool.wait_ge(kT_psum, 3)
                    for t in range(TT):
                        at = CONST["onehot"].start + t * 2 * SIDE + SIDE
                        oh = consts[:, at:at + SIDE].unsqueeze(1).broadcast_to([P, NH, SIDE])
                        pool.tensor_copy(k_st[:, t, :, HD + SIDE:HD + 2 * SIDE], oh).then_inc(kst_ready, 1)
                if ATTN[n]["rel"]:
                    for t in range(TT):
                        pool.wait_ge(rel_in[t], rel_loads(n))
                        for along in range(2):
                            side = k_st if n == 0 and along else q_st
                            pool.tensor_copy(side[:, t, :, HD + along * SIDE:HD + (along + 1) * SIDE],
                                             rel[:, t, along].rearrange("p r n -> p n r"))\
                                .then_inc(q_rel_ready, 1)
                else:
                    pool.wait_ge(qT_psum, 3 * n)
                    pool.memset(q_st[:, :, :, HD:HD + 2 * SIDE], 0.0).then_inc(q_rel_ready, 1)
                for p in range(PAIRS):
                    g = n * PAIRS + p
                    pool.wait_ge(rinv_ready, g + 1)
                    for t in range(TT):
                        pr = probs[:, p % 2, t]
                        pool.tensor_tensor(pr, pr, rinv[:, p % 2, t].unsqueeze(2).broadcast_to([P, 2, T]), ALU.mult)\
                            .then_inc(p_ready, 1)

            nln = 1
            for kind, n in BLOCKS:
                if kind == "attn":
                    if n == 3:
                        ln(nln)
                        nln += 1
                    if n > 0:
                        ln(nln)
                        nln += 1
                    attn(n)
                else:
                    ln(nln)
                    nln += 1
                    if n == 2:
                        pool.wait_ge(gates_ready, n + 1)
                        for t in range(TT):
                            pool.wait_ge(disp_ready, t + 1)
                            pool.tensor_tensor(comb[:, t].rearrange("p (e c) -> p e c", e=E),
                                               disp[:, t].rearrange("p (e c) -> p e c", e=E),
                                               gates[:, t, 0:E].unsqueeze(2).broadcast_to([P, E, CAP]), ALU.mult)\
                                .then_inc(comb_ready, 1)

        @block.scalar
        def _(act):
            def x_transposed(k, weight):
                act.wait_ge(xT_psum, k + 1)
                if weight is None:
                    act.activation(xT[:, :, :].rearrange("p k t -> p (k t)"), bank[B_LN][0:CH, :], ACT.Copy).then_inc(xT_ready, 1)
                else:
                    act.wait_ge(mw_in[2], 32)
                    act.activation(xT[:, 0], bank[B_LN][0:CH, 0:T], ACT.Copy, scale=lnw[:, weight, 0:1])
                    act.activation(xT[:, 1], bank[B_LN][0:CH, T:2 * T], ACT.Copy, scale=lnw[:, weight, 1:2]).then_inc(xT_ready, 1)

            def attn(n):
                if ATTN[n]["rel"]:
                    for t in range(TT):
                        act.wait_ge(rel_psum, 4 * n + 2 * t + 2)
                        act.activation(relall[:, t, :, NH // 2:NH],
                                       bank[B_REL[2 * t + 1]][:, 0:RELH].rearrange("p (r n) -> p r n", n=NH // 2),
                                       ACT.Copy).then_inc(rel_act, 1)
                if n == 0:
                    act.wait_ge(pool_ready, 4)
                for b in range(3):
                    act.wait_ge(kT_psum, 3 * n + b + 1)
                    act.activation(kT[0:SLOT, 2 * b:2 * b + 2, 0, :],
                                   bank[B_KT[b]][0:SLOT, :].rearrange("p (a t) -> p a t", a=2), ACT.Copy).then_inc(kT_act, 1)
                for b in (0, 2):
                    act.wait_ge(qT_psum, 3 * n + b + 1)
                    act.activation(qT[:, 2 * b:2 * b + 2, :].rearrange("p a t -> p (a t)"), bank[B_QT[b]][:, :], ACT.Copy).then_inc(qT_act, 1)

                def exps(p):
                    for t in range(TT):
                        act.wait_ge(nmax_ready, 2 * (n * PAIRS + p) + t + 1)
                        for h in range(2):
                            src = smask[:, p % 2, t, h] if n == 3 else bank[B_S[p % 2][t]][:, h * T:(h + 1) * T]
                            act.activation(probs[:, p % 2, t, h], src, ACT.Exp, bias=nmax[:, p % 2, t, h:h + 1],
                                           accum_out=rsum[:, p % 2, t, h:h + 1]).then_inc(exp_ready, 1)

                exps(0)
                exps(1)
                for p in range(PAIRS):
                    act.wait_ge(pT_psum, n * PAIRS + p + 1)
                    act.activation(pT[:, p % 2, 0].rearrange("p h t -> p (h t)"), bank[B_PT[0]][:, :], ACT.Copy).then_inc(pT_act, 1)
                    if p + 2 < PAIRS:
                        exps(p + 2)
                    if p % 2:
                        g = p // 2
                        act.wait_ge(o_psum, n * PAIRS + p + 1)
                        act.activation(oT[:, g, :], bank[B_O[g]][:, 0:T], ACT.Copy).then_inc(o_ready, 1)

            def split(m, j, i):
                s = (i + SHIFT[m]) % 2
                act.wait_ge(slot_in[s], 32 * (j + USED[m][s] + 1))
                for b in range(HB):
                    act.activation(w1_cols(w1_hi, b), w1_cols(w1[s], b), ACT.Copy).then_inc(w1_hi_ready, 1)

            def places():
                act.wait_ge(xd_psum, 1)
                act.activation(xdT[:, 0], bank[B_XD[0]][0:CH, :], ACT.Copy, scale=lnw[:, 1, 0:1]).then_inc(xd_act, 1)

                def gelu(ep):
                    for b in range(2):
                        act.wait_ge(hp_psum, 2 * ep + b + 1)
                        if ep and b:
                            act.wait_ge(hpT_psum, 2 * ep)
                        act.activation(hplace[:, b * 384:(b + 1) * 384], bank[B_HP[ep % 2][b]][:, 0:384], ACT.Gelu)\
                            .then_inc(hp_ready, 1)

                gelu(0)
                act.wait_ge(combT_psum, 2)
                act.activation(combT[:, 2:4, :].rearrange("p a t -> p (a t)"), bank[B_HT[1]][:, :], ACT.Copy).then_inc(combT_act, 1)
                for ep in range(EP):
                    act.wait_ge(hpT_psum, 2 * ep + 1)
                    act.activation(hplaceT[:, 0:384], bank[B_HT[0]][:, 0:384], ACT.Copy).then_inc(hpT_act, 1)
                    if ep + 1 < EP:
                        gelu(ep + 1)

            def moe(m, k):
                cfg = MOE[m]
                if not cfg["cap"]:
                    act.wait_ge(xT_ready, k + 1)
                    act.activation(xT_hi[:, :, :], xT[:, :, :], ACT.Copy).then_inc(xT_hi_ready, 1)
                act.wait_ge(negm_ready, m + 1)
                for t in range(TT):
                    act.activation(expl[:, t, :], logits[:, t, :], ACT.Exp, bias=nmax_l[:, t:t + 1]).then_inc(expl_ready, 1)
                if cfg["b"]:
                    act.wait_ge(mw_in[m], {0: 48, 1: 80, 3: 48}[m])

                def expert(j, i):
                    g = BASE[m] + i
                    if not (isinstance(j, int) and j + i == 0):
                        split(m, j, i)
                    for b in range(HB):
                        act.wait_ge(h_psum, 3 * (2 * j + g) + b + 1)
                        if cfg["act"] == "glu":
                            act.activation(silu_g[:, b, :], bank[B_H[b]][:, 0:T], ACT.Silu).then_inc(silu_ready, 1)
                        elif not cfg["b"]:
                            act.activation(hid[:, 2 * b:2 * b + 2, :].rearrange("p c t -> p (c t)"), bank[B_H[b]][:, :],
                                           FUNC[cfg["act"]]).then_inc(h_ready, 1)
                        else:
                            kb = (0, 1, None, 2)[m]
                            for c in range(2):
                                at = (2 * j + i) * 2 * HB + 2 * b + c
                                ins = act.activation(hid[:, 2 * b + c, :], bank[B_H[b]][:, c * T:(c + 1) * T],
                                                     FUNC[cfg["act"]], bias=b1[:, kb, bass.ds(at, 1)])
                            ins.then_inc(h_ready, 1)

                if cfg["cap"]:
                    return places()
                for i in range(2):
                    expert(0, i)
                    if cfg["b"] and i == 0:
                        kb = (0, 1, None, 2)[m]
                        act.wait_ge(gT_psum, kb + 1)
                        act.activation(gT[0:cfg["n"], :], bank[B_R][0:cfg["n"], T:2 * T], ACT.Copy).then_inc(gT_ready, 1)
                with act.Fori(1, E // 2) as j:
                    for i in range(2):
                        expert(j, i)
                if cfg["n"] > E:
                    expert(E // 2, 0)

            k = 0
            for kind, n in BLOCKS:
                if kind == "moe" and n != 2:
                    split(n, 0, 0)
                x_transposed(k, {("attn", 3): 0, ("moe", 2): 1}.get((kind, n)))
                if kind == "attn":
                    attn(n)
                else:
                    moe(n, k)
                k += 1

        @block.tensor
        def _(pe):
            def x_transposed(k, n):
                if k == 0:
                    pe.wait_ge(c_in, 16)
                for t in range(TT):
                    pe.wait_ge(xn_ready, 2 * n + t + 1)
                    for c in range(KC):
                        ins = pe.transpose(bank[B_LN][0:CH, c * T + t * P:c * T + (t + 1) * P],
                                           xn[:, t, c * CH:(c + 1) * CH], ident)
                ins.then_inc(xT_psum, 1)

            def attn(n, k):
                pe.wait_ge(aw_in[n], 96 if ATTN[n]["rel"] else 32)
                pe.wait_ge(xT_ready, k + 1)
                if ATTN[n]["rel"]:
                    for h in range(KC):
                        for c in range(KC):
                            ins = pe.matmul(bank[B_QT0][0:CH, h * T:(h + 1) * T], wqkv[:, n, c, h * CH:(h + 1) * CH],
                                            xT[:, c, :], start=(c == 0), stop=(c == KC - 1))
                    ins.then_inc(qTs_psum, 1)
                for t in range(TT):
                    for c in range(KC):
                        ins = pe.matmul(bank[B_QK[t]][:, 0:2 * C], xT[:, c, t * P:(t + 1) * P], wqkv[:, n, c, 0:2 * C],
                                        start=(c == 0), stop=(c == KC - 1))
                    ins.then_inc(qk_psum, 1)
                if ATTN[n]["rel"]:
                    pe.wait_ge(qTs_ready, 2 * (n + 1))
                    for t in range(TT):
                        for h in range(KC):
                            pe.matmul(bank[B_REL[2 * t + h]][:, 0:RELH], qTs[:, h, t * P:(t + 1) * P], reltab[:, n],
                                      start=True, stop=True).then_inc(rel_psum, 1)
                for t in range(TT):
                    for c in range(KC):
                        ins = pe.matmul(bank[B_V][:, t * C:(t + 1) * C], xT[:, c, t * P:(t + 1) * P],
                                        wqkv[:, n, c, 2 * C:3 * C], start=(c == 0), stop=(c == KC - 1))
                ins.then_inc(v_psum, 1)
                if n == 0:
                    pe.wait_ge(kst_ready, 2 * TT)
                    pe.wait_ge(q_rel_ready, 4)
                elif n == 1:
                    pe.wait_ge(kst_ready, 3 * TT)
                pe.wait_ge(qk_ready, TT * (n + 1))
                for b in range(3):
                    for p in range(2):
                        for t in range(TT):
                            h = 2 * (2 * b + p)
                            ins = pe.transpose(bank[B_KT[b]][:, p * T + t * P:p * T + (t + 1) * P],
                                               k_st[:, t, h:h + 2, :].rearrange("p h s -> p (h s)"), ident)
                    ins.then_inc(kT_psum, 1)
                pe.wait_ge(q_rel_ready, 4 * (n + 1) if n < 3 else 13)
                for b in range(3):
                    for p in range(2):
                        for t in range(TT):
                            h = 2 * (2 * b + p)
                            ins = pe.transpose(bank[B_QT[b]][:, p * T + t * P:p * T + (t + 1) * P],
                                               q_st[:, t, h:h + 2, :].rearrange("p h s -> p (h s)"), ident)
                    ins.then_inc(qT_psum, 1)

                def scores(p):
                    b = p // 2
                    if p == 0:
                        pe.wait_ge(v_ready, n + 1)
                        pe.wait_ge(kT_act, 3 * (n + 1))
                        pe.wait_ge(kT_dve, 3 * (n + 1))
                        pe.wait_ge(qT_act, 2 * n + 1)
                    if p == 2:
                        pe.wait_ge(qT_dve, n + 1)
                    if p == 4:
                        pe.wait_ge(qT_act, 2 * n + 2)
                    for t in range(TT):
                        pe.matmul(bank[B_S[p % 2][t]][:, :], qT[:, p, t * P:(t + 1) * P],
                                  kT[:, p].rearrange("p h t -> p (h t)"), start=True, stop=True).then_inc(s_psum, 1)

                scores(0)
                scores(1)
                for p in range(PAIRS):
                    g = n * PAIRS + p
                    if p == 0:
                        pe.wait_ge(qT_dve, n + 1)
                    for t in range(TT):
                        pe.wait_ge(p_ready, 2 * g + t + 1)
                        for h in range(2):
                            for kt in range(TT):
                                ins = pe.transpose(bank[B_PT[kt]][:, h * T + t * P:h * T + (t + 1) * P],
                                                   probs[:, p % 2, t, h, kt * P:(kt + 1) * P], ident)
                    ins.then_inc(pT_psum, 1)
                    if p + 2 < PAIRS:
                        scores(p + 2)
                    pe.wait_ge(pT_act, g + 1)
                    pe.wait_ge(pT_dve, g + 1)
                    if p == 0:
                        pe.wait_ge(qT_act, 2 * n + 2)
                    if p == 4:
                        pe.wait_ge(o_ready, GROUPS * n + 1)
                    for kt in range(TT):
                        for h in range(2):
                            row = 32 * ((2 * p + h) % 4)
                            ins = pe.matmul(bank[B_O[p // 2]][row:row + 32, 0:T], v_st[:, kt, 2 * p + h, :],
                                            pT[:, p % 2, kt, h, :], start=(kt == 0), stop=(kt == TT - 1))
                    ins.then_inc(o_psum, 1)
                for g in range(GROUPS):
                    pe.wait_ge(o_ready, GROUPS * n + g + 1)
                for t in range(TT):
                    for g in range(GROUPS):
                        ins = pe.matmul(bank[B_PROJ][:, t * C:(t + 1) * C], oT[:, g, t * P:(t + 1) * P], wproj[:, n, g, :],
                                        start=(g == 0), stop=(g == GROUPS - 1))
                ins.then_inc(proj_psum, 1)

            def places():
                pe.wait_ge(sel_ready, 1)
                earlier, ones = consts[:, CONST["earlier"]], consts[:, CONST["ones"]]
                pe.matmul(bank[B_R][:, 64:64 + E], earlier, sel[:, 0, :], start=True, stop=True)
                pe.matmul(bank[B_R][:, 64 + E:64 + 2 * E], ones, sel[:, 0, :], start=True, stop=False)
                pe.matmul(bank[B_R][:, 64 + E:64 + 2 * E], earlier, sel[:, 1, :], start=False, stop=True)\
                    .then_inc(pos_psum, 1)
                for t in range(TT):
                    pe.wait_ge(disp_ready, t + 1)
                    for c in range(KC):
                        ins = pe.matmul(bank[B_XD[c]][0:CH, :], xn[:, t, c * CH:(c + 1) * CH], disp[:, t],
                                        start=(t == 0), stop=(t == TT - 1))
                ins.then_inc(xd_psum, 1)

                def up(ep):
                    for ab in range(2):
                        s = CAP_SLOT[2 * ep + ab]
                        pe.wait_ge(slot_in[s], 32 * ((USED[2][s] if s < 2 else 0) + (ep == 3) + 1))
                    for b in range(2):
                        for c in range(KC):
                            for ab in range(2):
                                e = 2 * ep + ab
                                ins = pe.matmul(bank[B_HP[ep % 2][b]][ab * CAP:(ab + 1) * CAP, 0:384],
                                                xdT[:, c, e * CAP:(e + 1) * CAP],
                                                w1[CAP_SLOT[e]][:, c * 768 + b * 384:c * 768 + (b + 1) * 384],
                                                start=(c == 0), stop=(c == KC - 1))
                        ins.then_inc(hp_psum, 1)

                def add(ep):
                    pe.wait_ge(yp_ready, ep + 1)
                    if ep == 0:
                        pe.wait_ge(combT_act, 1)
                        pe.wait_ge(combT_dve, 1)
                    for t in range(TT):
                        ins = pe.matmul(bank[B_SUM][:, t * C:(t + 1) * C], combT[:, ep, t * P:(t + 1) * P], yplace,
                                        start=(ep == 0 and t == 0), stop=(ep == EP - 1), skip_group_check=True)
                    if ep == EP - 1:
                        ins.then_inc(sum_psum, 1)

                pe.wait_ge(xd_act, 1)
                pe.wait_ge(xd_dve, 1)
                up(0)
                for t in range(TT):
                    pe.wait_ge(comb_ready, t + 1)
                for b in range(2):
                    for p in range(2):
                        for t in range(TT):
                            ep = 2 * b + p
                            ins = pe.transpose(bank[B_HT[b]][:, p * T + t * P:p * T + (t + 1) * P],
                                               comb[:, t, ep * P:(ep + 1) * P], ident)
                    ins.then_inc(combT_psum, 1)
                for ep in range(EP):
                    if ep + 1 < EP:
                        up(ep + 1)
                    for b in range(2):
                        pe.wait_ge(hp_ready, 2 * ep + b + 1)
                        if ep == 0 and b == 0:
                            pe.wait_ge(combT_dve, 1)
                        if ep == 0 and b == 1:
                            pe.wait_ge(combT_act, 1)
                        for c in range(HB):
                            ins = pe.transpose(bank[B_HT[b]][:, c * P:(c + 1) * P],
                                               hplace[:, (b * HB + c) * P:(b * HB + c + 1) * P], ident)
                        ins.then_inc(hpT_psum, 1)
                    if ep:
                        add(ep - 1)
                    for c in range(2 * HB):
                        if c == 0:
                            pe.wait_ge(hpT_act, ep + 1)
                        if c == HB:
                            pe.wait_ge(hpT_dve, ep + 1)
                        for ab in range(2):
                            ins = pe.matmul(bank[B_YP][ab * CAP:(ab + 1) * CAP, 0:C],
                                            hplaceT[:, c * P + ab * CAP:c * P + (ab + 1) * CAP],
                                            w2[CAP_SLOT[2 * ep + ab]][:, c * C:(c + 1) * C],
                                            start=(c == 0), stop=(c == 2 * HB - 1))
                    ins.then_inc(yp_psum, 1)
                add(EP - 1)

            def moe(m, k):
                cfg = MOE[m]
                pe.wait_ge(mw_in[m], {0: 48, 1: 80, 2: 32, 3: 48, 4: 48}[m])
                pe.wait_ge(xT_ready, k + 1)
                for t in range(TT):
                    for c in range(KC):
                        ins = pe.matmul(bank[B_R][:, t * E:(t + 1) * E], xT[:, c, t * P:(t + 1) * P], wr[:, m, c, :],
                                        start=(c == 0), stop=(c == KC - 1))
                ins.then_inc(r_psum, 1)

                def expert(j, i):
                    g = BASE[m] + i
                    s = (i + SHIFT[m]) % 2
                    glu = cfg["act"] == "glu"
                    pe.wait_ge(slot_in[s], 32 * (j + USED[m][s] + 1))
                    if isinstance(j, int) and j == 0 and i == 0:
                        pe.wait_ge(xT_lo_ready, split_count(m))
                    for b in range(HB):
                        pe.wait_ge(w1_lo_ready, 3 * (2 * j + g) + b + 1)
                        for c2 in range(2):
                            at = (2 * b + c2) * P
                            for c in range(KC):
                                for k, (w, xs) in enumerate(((w1_hi, xT_hi), (w1_hi, xT_lo), (w1_lo, xT_hi))):
                                    ins = pe.matmul(bank[B_H[b]][:, c2 * T:(c2 + 1) * T], w[:, c, at:at + P], xs[:, c, :],
                                                    start=(c == 0 and k == 0), stop=(c == KC - 1 and k == 2))
                        ins.then_inc(h_psum, 1)
                    pe.wait_ge(acc_done, 2 * (2 * j + g))
                    nc2 = HB if glu else 2 * HB
                    for c in range(nc2):
                        if glu:
                            pe.wait_ge(glu_ready, 3 * (2 * j + g - BASE[4]) + c + 1)
                        elif c % 2 == 0:
                            pe.wait_ge(h_ready, 3 * (2 * j + g) + c // 2 + 1)
                        for t in range(TT):
                            ins = pe.matmul(bank[B_Y[t]][:, 0:C], hid[:, c, t * P:(t + 1) * P], w2[s][:, c * C:(c + 1) * C],
                                            start=(c == 0), stop=(c == nc2 - 1))
                            if c == nc2 - 1:
                                ins.then_inc(y_psum, 1)

                if cfg["cap"]:
                    return places()
                for i in range(2):
                    expert(0, i)
                    if cfg["b"]:
                        kb = (0, 1, None, 2)[m]
                        n = cfg["n"]
                        if i == 0:
                            pe.wait_ge(gates_ready, m + 1)
                            for t in range(TT):
                                ins = pe.transpose(bank[B_R][0:n, T + t * P:T + (t + 1) * P], gates[:, t, 0:n], ident)
                            ins.then_inc(gT_psum, 1)
                        else:
                            pe.wait_ge(gT_ready, kb + 1)
                            for t in range(TT):
                                ins = pe.matmul(bank[B_B2][:, t * C:(t + 1) * C], gT[0:n, t * P:(t + 1) * P], b2[0:n, kb, :],
                                                start=True, stop=True)
                            ins.then_inc(b2_psum, 1)
                with pe.Fori(1, E // 2) as j:
                    for i in range(2):
                        expert(j, i)
                if cfg["n"] > E:
                    expert(E // 2, 0)

            nln = 0
            for k, (kind, n) in enumerate(BLOCKS):
                if (kind, n) == ("attn", 3):
                    nln += 1
                x_transposed(k, nln)
                nln += 1
                (attn if kind == "attn" else moe)(n, k)

        @block.vector
        def _(dve):
            own = [0]

            def then(ins):
                own[0] += 1
                ins.then_inc(dve_own, 1)

            def settle():
                dve.wait_ge(dve_own, own[0])

            def ln(n, src, eps, dst=xn):
                for t in range(TT):
                    then(dve.bn_stats(stats[:, t, :], src[:, t, :]))
                settle()
                for t in range(TT):
                    then(dve.bn_aggr(moments[:, t, :], stats[:, t, :]))
                settle()
                dve.tensor_scalar(var_eps[:, :], moments[:, :, 1], eps, None, ALU.add).then_inc(var_ready, 1)
                dve.wait_ge(rstd_ready, n + 1)
                for t in range(TT):
                    dve.tensor_scalar(dst[:, t, :], src[:, t, :], moments[:, t, 0:1], rstd[:, t:t + 1],
                                      ALU.subtract, ALU.mult).then_inc(xn_ready, 1)

            def attn(n):
                src = tln if n == 3 else x
                scale = float(HD) ** -0.5
                heads = "p (h d) -> p h d"
                if ATTN[n]["rel"]:
                    dve.wait_ge(aw_in[n], 96)
                    then(dve.tensor_scalar(bq4[:, n, :], bqkv[:, n, 0:C], scale, None, ALU.mult))
                    dve.wait_ge(qTs_psum, n + 1)
                    for h in range(KC):
                        dve.tensor_scalar(qTs[:, h, :], bank[B_QT0][0:CH, h * T:(h + 1) * T], bq_col[:, n, h:h + 1], None, ALU.add)\
                            .then_inc(qTs_ready, 1)
                    settle()
                if n == 0:
                    dve.wait_ge(pool_ready, 5)
                for t in range(TT):
                    dve.wait_ge(qk_psum, TT * n + t + 1)
                    qp = bank[B_QK[t]][:, 0:C].rearrange(heads, h=NH)
                    kp = bank[B_QK[t]][:, C:2 * C].rearrange(heads, h=NH)
                    if ATTN[n]["rel"]:
                        dve.scalar_tensor_tensor(q_st[:, t, :, 0:HD], qp, scale, bq4[:, n, :].rearrange(heads, h=NH),
                                                 ALU.mult, ALU.add)
                        dve.tensor_tensor(k_st[:, t, :, 0:HD], kp, bqkv[:, n, C:2 * C].rearrange(heads, h=NH), ALU.add)\
                            .then_inc(qk_ready, 1)
                    else:
                        dve.tensor_scalar(q_st[:, t, :, 0:HD], qp, scale, None, ALU.mult)
                        dve.tensor_copy(k_st[:, t, :, 0:HD], kp).then_inc(qk_ready, 1)
                if ATTN[n]["rel"]:
                    for t in range(TT):
                        dve.wait_ge(rel_psum, 4 * n + 2 * t + 1)
                        dve.tensor_copy(relall[:, t, :, 0:NH // 2],
                                        bank[B_REL[2 * t]][:, 0:RELH].rearrange("p (r n) -> p r n", n=NH // 2))\
                            .then_inc(rel_dve, 1)
                dve.wait_ge(v_psum, n + 1)
                for t in range(TT):
                    vp = bank[B_V][:, t * C:(t + 1) * C].rearrange(heads, h=NH)
                    if ATTN[n]["rel"]:
                        ins = dve.tensor_tensor(v_st[:, t, :, 0:HD], vp, bqkv[:, n, 2 * C:3 * C].rearrange(heads, h=NH), ALU.add)
                    else:
                        ins = dve.tensor_copy(v_st[:, t, :, 0:HD], vp)
                ins.then_inc(v_ready, 1)
                for b in range(3):
                    dve.wait_ge(kT_psum, 3 * n + b + 1)
                    dve.tensor_copy(kT[SLOT:P, 2 * b:2 * b + 2, 1, :],
                                    bank[B_KT[b]][SLOT:P, :].rearrange("p (a t) -> p a t", a=2)).then_inc(kT_dve, 1)
                if ATTN[n]["rel"]:
                    for t in range(TT):
                        then(dve.tensor_tensor(xb[:, t, :], src[:, t, :], bproj[:, n, :], ALU.add))
                dve.wait_ge(qT_psum, 3 * n + 2)
                dve.tensor_copy(qT[:, 2:4, :].rearrange("p a t -> p (a t)"), bank[B_QT[1]][:, :]).then_inc(qT_dve, 1)

                def row_max(p):
                    for t in range(TT):
                        dve.wait_ge(s_psum, 2 * (n * PAIRS + p) + t + 1)
                        s = bank[B_S[p % 2][t]][:, :].rearrange("p (h k) -> p h k", h=2)
                        if n == 3:
                            at = CONST["causal"].start + t * T
                            mask = consts[:, at:at + T].unsqueeze(1).broadcast_to([P, 2, T])
                            then(dve.tensor_tensor(smask[:, p % 2, t], s, mask, ALU.add))
                            settle()
                            s = smask[:, p % 2, t]
                        dve.tensor_reduce(nmax[:, p % 2, t, :], s, AX.X, ALU.max, negate=True).then_inc(nmax_ready, 1)

                def recip(p):
                    dve.wait_ge(exp_ready, 4 * (n * PAIRS + p + 1))
                    dve.reciprocal(rinv[:, p % 2].rearrange("p t h -> p (t h)"), rsum[:, p % 2].rearrange("p t h -> p (t h)"))\
                        .then_inc(rinv_ready, 1)

                row_max(0)
                row_max(1)
                recip(0)
                for p in range(PAIRS):
                    if p + 1 < PAIRS:
                        recip(p + 1)
                    dve.wait_ge(pT_psum, n * PAIRS + p + 1)
                    dve.tensor_copy(pT[:, p % 2, 1].rearrange("p h t -> p (h t)"), bank[B_PT[1]][:, :]).then_inc(pT_dve, 1)
                    if p + 2 < PAIRS:
                        row_max(p + 2)
                dve.wait_ge(proj_psum, n + 1)
                settle()
                res = (tln if n == 3 else xb)[:, :, :].rearrange("p t c -> p (t c)")
                dst = (tln if n == 3 else x)[:, :, :].rearrange("p t c -> p (t c)")
                then(dve.tensor_tensor(dst, bank[B_PROJ][:, 0:TT * C], res, ALU.add))
                settle()

            def split(m, j, i):
                s = (i + SHIFT[m]) % 2
                for b in range(HB):
                    dve.wait_ge(w1_hi_ready, 3 * (2 * j + BASE[m] + i) + b + 1)
                    dve.tensor_tensor(w1_cols(w1_lo, b), w1_cols(w1[s], b), w1_cols(w1_hi, b).bitcast(F32), ALU.subtract)\
                        .then_inc(w1_lo_ready, 1)

            def moe(m):
                cfg = MOE[m]
                iota = consts[:, CONST["iota"]]

                if not cfg["cap"]:
                    dve.wait_ge(xT_hi_ready, split_count(m))
                    dve.tensor_tensor(xT_lo[:, :, :], xT[:, :, :], xT_hi[:, :, :].bitcast(F32), ALU.subtract).then_inc(xT_lo_ready, 1)
                dve.wait_ge(r_psum, m + 1)
                lp = bank[B_R][:, 0:TT * E].rearrange("p (t e) -> p t e", t=TT)
                if cfg["rbias"]:
                    dve.wait_ge(mw_in[m], {1: 80, 4: 48}[m])
                    then(dve.tensor_tensor(logits[:, :, :], lp, rbias[:, m // 4], ALU.add))
                else:
                    then(dve.tensor_copy(logits[:, :, :], lp))
                settle()
                for t in range(TT):
                    then(dve.max(top8[:, t, :], logits[:, t, :]))
                settle()
                dve.tensor_scalar(nmax_l[:, :], top8[:, :, 0], -1.0, None, ALU.mult).then_inc(negm_ready, 1)
                for t in range(TT):
                    then(dve.max_index(top_i[:, t, :], top8[:, t, :], logits[:, t, :]))
                settle()
                then(dve.tensor_copy(top_f[:, :, :], top_i[:, :, 0:2]))
                settle()
                for t in range(TT):
                    then(dve.tensor_scalar(first[:, t, :], iota, top_f[:, t, 0:1], None, ALU.is_equal))
                settle()
                for t in range(TT):
                    ins = dve.scalar_tensor_tensor(sel[:, t, :], iota, top_f[:, t, 1:2], first[:, t, :], ALU.is_equal, ALU.add)
                    if cfg["cap"] and t:
                        ins.then_inc(sel_ready, 1)
                    else:
                        then(ins)
                settle()
                if cfg["cap"]:
                    dve.wait_ge(sel_ready, 1)
                if cfg["cap"]:
                    dve.wait_ge(pos_psum, 1)
                    then(dve.scalar_tensor_tensor(place[:, :, :], bank[B_R][:, 64:64 + TT * E].rearrange("p (t e) -> p t e", t=TT),
                                                  1.0, sel[:, :, :], ALU.add, ALU.mult))
                    settle()
                    for t in range(TT):
                        dve.tensor_tensor(disp[:, t].rearrange("p (e c) -> p e c", e=E),
                                          consts[:, CONST["places"]].unsqueeze(1).broadcast_to([P, E, CAP]),
                                          place[:, t, :].unsqueeze(2).broadcast_to([P, E, CAP]), ALU.is_equal)\
                            .then_inc(disp_ready, 1)
                dve.wait_ge(expl_ready, 2 * (m + 1))
                then(dve.tensor_tensor(chosen[:, :, :], expl[:, :, :], sel[:, :, :], ALU.mult))
                settle()
                then(dve.tensor_reduce(den[:, :], (expl if cfg["over_all"] else chosen)[:, :, :], AX.X, ALU.add))
                settle()
                then(dve.reciprocal(rden[:, :], den[:, :]))
                settle()
                for t in range(TT):
                    ins = dve.tensor_scalar(gates[:, t, 0:E], chosen[:, t, :], rden[:, t:t + 1], None, ALU.mult)
                    if t == 0:
                        then(ins)
                ins.then_inc(gates_ready, 1)
                settle()
                dve.wait_ge(gates_ready, m + 1)

                def glu(j, i):
                    for b in range(HB if cfg["act"] == "glu" else 0):
                        dve.wait_ge(silu_ready, 3 * (2 * j + i) + b + 1)
                        dve.tensor_tensor(hid[:, b, :], silu_g[:, b, :], bank[B_H[b]][:, T:2 * T], ALU.mult)\
                            .then_inc(glu_ready, 1)

                def add(j, i):
                    g = BASE[m] + i
                    for t in range(TT):
                        dve.wait_ge(y_psum, 2 * (2 * j + g) + t + 1)
                        dve.scalar_tensor_tensor(x[:, t, :], bank[B_Y[t]][:, 0:C], gates[:, t, bass.ds(2 * j + i, 1)],
                                                 x[:, t, :], ALU.mult, ALU.add).then_inc(acc_done, 1)

                if cfg["cap"]:
                    then(dve.tensor_tensor(x[:, :, :], x[:, :, :], tln[:, :, :], ALU.add))
                    dve.wait_ge(xd_psum, 1)
                    dve.tensor_scalar(xdT[:, 1], bank[B_XD[1]][0:CH, :], lnw[:, 1, 1:2], None, ALU.mult).then_inc(xd_dve, 1)
                    dve.wait_ge(combT_psum, 1)
                    dve.tensor_copy(combT[:, 0:2, :].rearrange("p a t -> p (a t)"), bank[B_HT[0]][:, :]).then_inc(combT_dve, 1)
                    for ep in range(EP):
                        dve.wait_ge(hpT_psum, 2 * ep + 2)
                        dve.tensor_copy(hplaceT[:, 384:768], bank[B_HT[1]][:, 0:384]).then_inc(hpT_dve, 1)
                        dve.wait_ge(yp_psum, ep + 1)
                        dve.tensor_copy(yplace, bank[B_YP][:, 0:C]).then_inc(yp_ready, 1)
                    dve.wait_ge(sum_psum, 1)
                    settle()
                    then(dve.tensor_tensor(x[:, :, :], bank[B_SUM][:, 0:TT * C].rearrange("p (t c) -> p t c", t=TT), x[:, :, :], ALU.add))
                    settle()
                    return
                glu(0, 0)
                split(m, 0, 1)
                add(0, 0)
                glu(0, 1)
                if cfg["b"]:
                    k = (0, 1, None, 2)[m]
                    dve.wait_ge(b2_psum, k + 1)
                    dve.wait_ge(acc_done, 2 * (BASE[m] + 1))
                    then(dve.tensor_tensor(x[:, :, :], bank[B_B2][:, 0:TT * C].rearrange("p (t c) -> p t c", t=TT), x[:, :, :], ALU.add))
                    settle()
                with dve.Fori(1, E // 2) as j:
                    for i in range(2):
                        split(m, j, i)
                        add(j - 1 + i, 1 - i)
                        glu(j, i)
                if cfg["n"] > E:
                    split(m, E // 2, 0)
                    add(E // 2 - 1, 1)
                    glu(E // 2, 0)
                    add(E // 2, 0)
                else:
                    add(E // 2 - 1, 1)
                dve.wait_ge(acc_done, 2 * BASE[m + 1])

            dve.wait_ge(x_in, 16)
            nln = 0
            for kind, n in BLOCKS:
                if (kind, n) == ("attn", 3):
                    ln(nln, x, 1e-5, tln)
                    nln += 1
                    dve.wait_ge(xn_ready, 2 * nln)
                    ln(nln, tln, 1e-5)
                elif (kind, n) == ("moe", 2):
                    ln(nln, tln, 1e-5)
                else:
                    ln(nln, x, (ATTN if kind == "attn" else MOE)[n]["eps"])
                nln += 1
                if kind == "moe" and n != 2:
                    split(n, 0, 0)
                (attn if kind == "attn" else moe)(n)


def _layout(i):
    import numpy as np

    def rows(w):
        return np.ascontiguousarray(w.reshape(KC, CH, -1).transpose(1, 0, 2))

    def heads_padded(w):
        p = np.zeros((GROUPS, 4, 32, w.shape[1]), w.dtype)
        p[:, :, :HD] = w.reshape(GROUPS, 4, HD, -1)
        return np.ascontiguousarray(p.reshape(GROUPS, P, -1).transpose(1, 0, 2))

    def rel_table(th, tw, n):
        t = np.zeros((NH // KC, HD, RELS, NH // KC), th.dtype)
        tw = tw[:REL]
        both = np.concatenate([th[:REL], tw if n else tw[::-1]], 0).T
        for h in range(NH // KC):
            t[h, :, :, h] = both
        return np.ascontiguousarray(t.reshape(CH, RELH))

    def up(w):
        return np.ascontiguousarray(w.reshape(w.shape[0], KC, CH, -1).transpose(0, 2, 1, 3).reshape(w.shape[0], CH, -1))

    def down(w):
        n = w.shape[0]
        return np.ascontiguousarray(w.reshape(n, -1, P, C).transpose(0, 2, 1, 3).reshape(n, P, -1))

    def cols(b):
        return np.ascontiguousarray(b.reshape(b.shape[0], -1, P).transpose(2, 0, 1).reshape(P, -1))

    a = {"x": i["x"].reshape(T, C)}
    qkv = [np.concatenate([i[f"L0_conv_w{n}"].reshape(C, C).T for n in "qkv"], 1), i["L1_conv_qkv_w"],
           i["L2_conv_qkv_w"], i["L2_ffn_c_attn_w"].T]
    bias = [np.concatenate([i[f"L0_conv_b{n}"].reshape(C) for n in "qkv"]), i["L1_conv_qkv_b"], i["L2_conv_qkv_b"]]
    proj = [i["L0_conv_proj_w"].T, i["L1_conv_proj_w"], i["L2_conv_proj_w"], i["L2_ffn_c_proj_w"].T]
    for n in range(4):
        a[f"A{n}_wqkv"] = rows(qkv[n])
        a[f"A{n}_wproj"] = heads_padded(proj[n])
        if n < 3:
            a[f"A{n}_bqkv"] = bias[n]
            a[f"A{n}_bproj"] = i[f"L{n}_conv_proj_b"]
            a[f"A{n}_bq"] = np.ascontiguousarray(bias[n][:C].reshape(KC, CH).T)
            a[f"A{n}_reltab"] = rel_table(i[f"L{n}_conv_rel_pos_h"], i[f"L{n}_conv_rel_pos_w"], n)
    w1 = [i["L0_ffn_W1"], i["L1_ffn_Wfc"], i["L2_ffn_c_fc"],
          np.concatenate([i["L3_conv_w1"], i["L3_conv_ws1"][None]], 0).transpose(0, 2, 1)]
    w2 = [i["L0_ffn_W2"], i["L1_ffn_Wproj"], i["L2_ffn_c_proj_e"],
          np.concatenate([i["L3_conv_w2"], i["L3_conv_ws2"][None]], 0).transpose(0, 2, 1)]
    gu = [np.concatenate([i[f"L3_ffn_{n}_r"], i[f"L3_ffn_{n}_s"]], 0).reshape(E + 1, C, HB, 1, P) for n in ("Wg", "Wu")]
    w1.append(np.concatenate(gu, 3).reshape(E + 1, C, 2 * HB * P))
    w2.append(np.concatenate([i["L3_ffn_Wd_r"], i["L3_ffn_Wd_s"]], 0))
    wr = [i["L0_ffn_Wg"], i["L1_ffn_Wr"], i["L2_ffn_w_g"].T, i["L3_conv_gate_w"].T, i["L3_ffn_W_router"]]
    for m in range(5):
        a[f"M{m}_w1"], a[f"M{m}_w2"], a[f"M{m}_wr"] = up(w1[m]), down(w2[m]), rows(wr[m])
    a["M1_rbias"], a["M4_rbias"] = i["L1_ffn_br"], i["L3_ffn_expert_bias"]
    a["M0_b1"], a["M0_b2"] = cols(i["L0_ffn_b1"]), i["L0_ffn_b2"]
    a["M1_b1"], a["M1_b2"] = cols(i["L1_ffn_bfc"]), i["L1_ffn_bproj"]
    a["M3_b1"] = cols(np.concatenate([i["L3_conv_b1"], i["L3_conv_bs1"][None]], 0))
    a["M3_b2"] = np.concatenate([i["L3_conv_b2"], i["L3_conv_bs2"][None]], 0)
    a["lnw"] = np.ascontiguousarray(np.stack([i["L2_ffn_ln1_w"], i["L2_ffn_ln2_w"]], 0).reshape(2, KC, CH).transpose(2, 0, 1))
    c = np.zeros((P, CONST_W), np.float32)
    c[:, CONST["ident"]] = np.eye(P)
    c[:, CONST["earlier"]] = np.triu(np.ones((P, P)), 1)
    c[:, CONST["ones"]] = 1.0
    c[:, CONST["iota"]] = np.arange(E)
    c[:, CONST["places"]] = np.arange(1, CAP + 1)
    tok = np.arange(T)
    hot = np.zeros((T, 2, SIDE), np.float32)
    hot[tok, 0, SIDE - 1 - tok // SIDE] = 1.0
    hot[tok, 1, SIDE - 1 - tok % SIDE] = 1.0
    c[:, CONST["onehot"]] = hot.reshape(TT, P, 2 * SIDE).transpose(1, 0, 2).reshape(P, -1)
    row = (tok[:, None] // SIDE == np.arange(SIDE)).astype(np.float32)
    c[:, CONST["rowhot"]] = row.reshape(TT, P, SIDE).transpose(1, 0, 2).reshape(P, -1)
    mask = np.where(tok[None, :] > tok[:, None], np.float32(NEG), np.float32(0.0))
    c[:, CONST["causal"]] = mask.reshape(TT, P, T).transpose(1, 0, 2).reshape(P, -1)
    a["consts"] = c
    return a


def kernel(**inputs):
    import numpy as _np
    import concourse.bacc as _bacc
    from concourse import mybir as _mybir
    from concourse.bass_utils import run_bass_kernel_spmd as _run

    nc = _bacc.Bacc("TRN2", target_bir_lowering=False, num_devices=1)
    arrays, args = {}, {}
    for name, v in _layout({k: _np.asarray(v) for k, v in inputs.items()}).items():
        v = _np.ascontiguousarray(v)
        arrays[f"in_{name}_dram"] = v
        args[name] = nc.dram_tensor(f"in_{name}_dram", v.shape, _mybir.dt.from_np(v.dtype), kind="ExternalInput").ap()
    out = nc.dram_tensor("out_dram", (T, C), F32, kind="ExternalOutput").ap()
    metaformer_kernel(nc, args, out)
    r = _run(nc, [arrays], core_ids=[0])
    return r.results[0]["out_dram"].reshape(1, SIDE, SIDE, C)
```

```python
from contextlib import ExitStack

import concourse.bass as bass
from concourse import mybir

F32 = mybir.dt.float32
F32R = mybir.dt.float32r
U32 = mybir.dt.uint32
ALU = mybir.AluOpType
ACT = mybir.ActivationFunctionType
AX = mybir.AxisListType

P = 128
SIDE = 16
T = SIDE * SIDE
TT = T // P
C = 192
KC = 2
CH = C // KC
CR = C - P
NH = 12
HD = C // NH
SLOT = 64
PAIRS = NH // 2
GROUPS = NH // 4
REL = 2 * SIDE - 1
RELS = 2 * REL
RELW = RELS * NH
RELH = RELW // KC
E = 8
HB = 3
SB = 2
SC = 2 * SB
CAP = 64
NEG = -3.0e38

CONST = {}
_at = 0
for _name, _n in (("ident", P), ("earlier", P), ("ones", P), ("iota", E), ("onehot", TT * 2 * SIDE), ("rowhot", TT * SIDE), ("places", 64),
                  ("causal", P)):
    CONST[_name] = slice(_at, _at + _n)
    _at += _n
CONST_W = _at

ATTN = (dict(rel=True, eps=1e-6), dict(rel=True, eps=1e-6), dict(rel=True, eps=1e-6), dict(rel=False, eps=1e-5))
MOE = (
    dict(n=8, act="relu", split2=True, b=True, rbias=False, over_all=True, cap=False, eps=1e-5),
    dict(n=8, act="gelu_tanh", split2=True, b=True, rbias=True, over_all=False, cap=False, eps=1e-5),
    dict(n=8, act="gelu", split2=False, b=False, rbias=False, over_all=False, cap=True, eps=1e-5),
    dict(n=9, act="gelu", split2=True, b=True, rbias=False, over_all=False, cap=False, eps=1e-6),
    dict(n=9, act="glu", split2=False, b=False, rbias=True, over_all=False, cap=False, eps=1e-5),
)
BASE = [sum(m["n"] for m in MOE[:i] if not m["cap"]) for i in range(len(MOE) + 1)]
EP = E // 2
SHIFT = (0, 0, 0, 0, 1)
USED = ((0, 0), (4, 4), (8, 8), (9, 9), (14, 13))
FUNC = {"relu": ACT.Relu, "gelu_tanh": ACT.Gelu_apprx_tanh, "gelu": ACT.Gelu, "glu": ACT.Silu}
BLOCKS = (("attn", 0), ("moe", 0), ("attn", 1), ("moe", 1), ("attn", 2), ("attn", 3), ("moe", 2), ("moe", 3), ("moe", 4))

LN_WEIGHT = {("attn", 3): 0, ("moe", 2): 1}


def metaformer_kernel(nc, a, out):
    ctx = ExitStack()
    with ctx:
        def sb(name, shape, dt=F32):
            return ctx.enter_context(nc.sbuf_tensor(name, shape, dt))

        def sem(name):
            return ctx.enter_context(nc.semaphore(name))

        x = sb("x", [P, TT, C])
        tln = sb("tln", [P, TT, C])
        xb = sb("xb", [P, TT, C])
        stats = sb("stats", [P, TT, 6])
        moments = sb("moments", [P, TT, 2])
        var_eps = sb("var_eps", [P, TT])
        minus_half = sb("minus_half", [P, TT])
        rstd = sb("rstd", [P, TT])
        xn = sb("xn", [P, TT, C + CR])
        xT = sb("xT", [P, KC, T])
        consts = sb("consts", [P, CONST_W])
        ident = consts[:, CONST["ident"]]
        wqkv = sb("wqkv", [CH, 4, KC, 3 * C])
        wproj = sb("wproj", [P, 4, GROUPS, C])
        bqkv = sb("bqkv", [P, 3, 3 * C])
        bproj = sb("bproj", [P, 3, C])
        bq4 = sb("bq4", [P, 3, C])
        bq_col = sb("bq_col", [CH, 3, KC])
        reltab = sb("reltab", [CH, 3, RELH])
        qTs = sb("qTs", [CH, KC, T])
        relall = sb("relall", [P, TT, RELS, NH])
        rel = sb("rel", [P, TT, 2, SIDE, NH])
        q_st = sb("q_st", [P, TT, NH, SLOT])
        k_st = sb("k_st", [P, TT, NH, SLOT])
        v_st = sb("v_st", [P, TT, NH, 32])
        qT = sb("qT", [P, PAIRS, T])
        kT = sb("kT", [P, PAIRS, 2, T])
        hplace = sb("hplace", [P, 768])
        yplace = sb("yplace", [P, C])
        nmax = sb("nmax", [P, 2, TT, 2])
        rsum = sb("rsum", [P, 2, TT, 2])
        rinv = sb("rinv", [P, 2, TT, 2])
        warm = sb("warm", [P, T])
        probs = sb("probs", [P, 2, TT, 2, T])
        pT = sb("pT", [P, 2, TT, 2, T])
        oT = sb("oT", [P, GROUPS, T])
        w1 = [sb(f"w1_{s}", [P, KC * 768]) for s in range(4)]
        w2 = [sb(f"w2_{s}", [P, 2 * HB * C]) for s in range(4)]
        w1 += [wqkv[:, :, :, :].rearrange("p i c n -> p (i c n)")[:, k * KC * 768:(k + 1) * KC * 768] for k in range(2)]
        w2 += [wproj[:, :, :, :].rearrange("p i g n -> p (i g n)")[:, 0:2 * HB * C],
               bqkv[:, :, :].rearrange("p i n -> p (i n)")[:, 0:2 * HB * C]]
        w1 += [kT[:, :, :, :].rearrange("p a h t -> p (a h t)")[:, k * KC * 768:(k + 1) * KC * 768] for k in range(2)]
        w2 += [qT[:, :, :].rearrange("p a t -> p (a t)")[:, 0:2 * HB * C],
               relall[:, :, :, :].rearrange("p t r n -> p (t r n)")[:, 0:2 * HB * C]]
        wr = sb("wr", [P, 5, KC, E])
        rbias = sb("rbias", [P, 2, TT, E])
        b1 = sb("b1", [P, 3, 9 * 2 * HB])
        b2 = sb("b2", [9, 3, C])
        lnw = sb("lnw", [CH, 2, KC])
        w1_hi, w1_lo = sb("w1_hi", [P, KC, 768], F32R), sb("w1_lo", [P, KC, 768], F32R)
        xT_hi, xT_lo = sb("xT_hi", [P, KC, T], F32R), sb("xT_lo", [P, T], F32R)
        hid = sb("hid", [P, 2 * HB, T])
        hid_hi, hid_lo = sb("hid_hi", [P, SC, T], F32R), sb("hid_lo", [P, SC, T], F32R)
        w2_hl = sb("w2_hl", [P, SC, 2, C], F32R)
        silu_g = sb("silu_g", [P, HB, T])
        logits = sb("logits", [P, TT, E])
        top8 = sb("top8", [P, TT, 8])
        top_i = sb("top_i", [P, TT, 8], U32)
        top_f = sb("top_f", [P, TT, 2])
        nmax_l = sb("nmax_l", [P, TT])
        expl = sb("expl", [P, TT, E])
        first = sb("first", [P, TT, E])
        sel = sb("sel", [P, TT, E])
        chosen = sb("chosen", [P, TT, E])
        den = sb("den", [P, TT])
        rden = sb("rden", [P, TT])
        place = sb("place", [P, TT, E])
        gates = sb("gates", [P, TT, E + 1])
        gT = sb("gT", [E + 1, T])
        disp = probs[:, 0].rearrange("p t h k -> p t (h k)")
        comb = probs[:, 1].rearrange("p t h k -> p t (h k)")
        combT = pT[:, 0].rearrange("p t h k -> p (t h) k")
        xdT = pT[0:CH, 1].rearrange("p t h k -> p t (h k)")
        hplaceT = hid[:, 0:HB, :].rearrange("p c t -> p (c t)")
        scratch = nc.dram_tensor("rel_scratch", [3, T, RELW], F32, kind="Internal").ap()

        bank = [ctx.enter_context(nc.psum_tensor(f"bank{i}", [P, 512], F32)) for i in range(8)]
        B_QT0, B_QK, B_REL, B_V = (0, 2), (1, 2), (3, 4, 5, 6), 7
        B_KT, B_QT = (0, 1, 2), (3, 4, 5)
        B_S, B_PT, B_O, B_PROJ = ((6, 7), (0, 1)), (2, 3), (4, 5, 4), (6, 7)
        B_H, B_Y, B_R, B_B2 = (0, 1, 2), (3, 4), 5, 6
        B_LN, B_WARM = (7, 6), 0
        B_XD, B_HP, B_HT, B_YP, B_SUM = (0, 1), ((0, 1), (2, 3)), (5, 6), 7, 4

        x_in, ident_in, c_in, wqkv0_in = sem("x_in"), sem("identity_in"), sem("consts_in"), sem("first_wqkv_in")
        aw_in = [sem(f"attn_weights_in{i}") for i in range(4)]
        mw_in = [sem(f"moe_small_in{i}") for i in range(5)]
        w1_in = [sem(f"expert_w1_in{s}") for s in range(8)]
        w2_in = [sem(f"expert_w2_in{s}") for s in range(8)]
        rel_out = [sem(f"rel_to_dram{t}") for t in range(TT)]
        rel_in = [sem(f"rel_from_dram{t}") for t in range(TT)]
        y_out = sem("result_out")
        dve_own, minus_half_ready = sem("dve_own"), sem("minus_half_ready")
        pool_ready, warm_ready = sem("pool_constants_ready"), sem("warm_up_operand_ready")
        kst_ready = sem("k_onehots_ready")
        var_ready, rstd_ready, xn_ready = sem("var_ready"), sem("rstd_ready"), sem("xn_ready")
        xT_psum, xT_act, xT_dve = sem("xT_psum"), sem("xT_act"), sem("xT_dve")
        qTs_psum, qTs_ready = sem("qTs_psum"), sem("qTs_ready")
        qk_psum, k_ready = sem("qk_psum"), sem("k_ready")
        rel_psum, rel_dve, rel_act = sem("rel_psum"), sem("rel_copied_dve"), sem("rel_copied_act")
        q_ready, q_rel_ready, q_clear = sem("q_ready"), sem("q_rel_ready"), sem("q_rel_cleared")
        kw_psum, kw_act, kw_dve = sem("keys_w_psum"), sem("keys_w_act"), sem("keys_w_dve")
        v_psum, v_ready = sem("v_psum"), sem("v_ready")
        kT_psum, kT_dve, kT_act = sem("kT_psum"), sem("kT_dve"), sem("kT_act")
        qT_psum, qT_dve, qT_act = sem("qT_psum"), sem("qT_dve"), sem("qT_act")
        s_psum, nmax_ready, exp_ready = sem("scores_psum"), sem("nmax_ready"), sem("exp_ready")
        rinv_ready, p_ready, p_ready_dve = sem("rinv_ready"), sem("probs_ready"), sem("probs_ready_dve")
        pT_psum, pT_dve, pT_act = sem("pT_psum"), sem("pT_dve"), sem("pT_act")
        o_psum, o_ready = sem("o_psum"), sem("o_ready")
        proj_psum = sem("proj_psum")
        r_psum, negm_ready, expl_ready = sem("router_psum"), sem("neg_logit_max_ready"), sem("exp_logits_ready")
        sel_ready, pos_psum, gates_ready = sem("selection_ready"), sem("positions_psum"), sem("gates_ready")
        gT_psum, gT_ready, b2_psum = sem("gatesT_psum"), sem("gatesT_ready"), sem("b2_psum")
        h_psum, h_ready = sem("hidden_psum"), sem("hidden_ready")
        silu_ready, glu_ready = sem("silu_ready"), sem("glu_ready")
        xT_hi_ready, xT_lo_ready = sem("xT_high_ready"), sem("xT_low_ready")
        w1_hi_ready, w1_lo_ready = sem("w1_high_ready"), sem("w1_low_ready")
        hid_hi_ready, hid_lo_ready = sem("hidden_high_ready"), sem("hidden_low_ready")
        w2_hi_ready, w2_lo_ready, w2_used = sem("w2_high_ready"), sem("w2_low_ready"), sem("w2_parts_used")
        acc_part = sem("expert_out_part_added")
        disp_ready, comb_ready = sem("dispatch_ready"), sem("combine_ready")
        xd_psum, xd_act, xd_dve = sem("dispatched_psum"), sem("dispatched_act"), sem("dispatched_dve")
        combT_psum, combT_act, combT_dve = sem("combT_psum"), sem("combT_act"), sem("combT_dve")
        hp_psum, hp_ready = sem("pair_hidden_psum"), sem("pair_hidden_ready")
        hpT_psum, hpT_act, hpT_dve = sem("pair_hiddenT_psum"), sem("pair_hiddenT_act"), sem("pair_hiddenT_dve")
        yp_psum, yp_ready, sum_psum = sem("pair_out_psum"), sem("pair_out_ready"), sem("sum_psum")
        y_psum, acc_done = sem("expert_out_psum"), sem("expert_out_added")

        def w1_cols(w, b):
            w = w[:, :] if len(w.shape) == 2 else w[:, :, :].rearrange("p k n -> p (k n)")
            return w.rearrange("p (k n) -> p k n", k=KC)[:, :, b * 2 * P:(b + 1) * 2 * P]

        def ln_bank(t, rows):
            return bank[B_LN[t]][0:rows, 0:KC * P].rearrange("p (k n) -> p k n", k=KC)

        def keys_of(n, t):
            return (t + 1) * P if n == 3 else T

        def scores_bank(n, p, t):
            return bank[B_S[p % 2][t]][:, :].rearrange("p (h k) -> p h k", h=2)[:, :, 0:keys_of(n, t)]

        def looped(m):
            return (MOE[m]["n"] - 1) // 2

        def split_count(m):
            return m + 1 if m < 2 else m

        def rel_ap(i, t, along):
            step_h, step_w = SIDE * RELW, RELW
            if along == 0:
                first_at, step_h = t * (SIDE // TT) * NH, step_h + NH
            else:
                first_at, step_w = REL * NH, step_w + NH
            return bass.AP(scratch.tensor, i * T * RELW + t * P * RELW + first_at,
                           [[step_h, SIDE // TT], [step_w, SIDE], [1, SIDE * NH]])

        def sides(n):
            return 1 if n == 0 else 2

        def rel_copies(n, t):
            return sum(TT * sides(i) for i in range(n)) + (t + 1) * sides(n)

        def kw_bank(i, row):
            return bank[B_REL[i]][row:row + SIDE, 0:3 * P].rearrange("p (a k) -> p a k", a=3)

        def kw_rows(i, head):
            row = head * SLOT + HD + SIDE
            return kT[row:row + SIDE, 3 * (i // 2):3 * (i // 2) + 3, head, (i % 2) * P:(i % 2 + 1) * P]

        block = ctx.enter_context(nc.Block())

        @block.sync
        def _(sp):
            def load_expert(m, j, i):
                e = 2 * j + i
                s = e if m == 2 else (i + SHIFT[m]) % 2
                first = isinstance(j, int) and j == 0
                last = 2 * j + BASE[m] + i - 1
                two_slots = s < 2 and not (first and m in (0, 3))
                if s in (4, 5):
                    sp.wait_ge(qk_psum, 3 * TT)
                elif s in (6, 7):
                    sp.wait_ge(s_psum, len(ATTN) * PAIRS * TT)
                elif m == 3 and first:
                    sp.wait_ge(yp_psum, 1)
                elif two_slots:
                    sp.wait_ge(w1_lo_ready, 3 * last)
                n2 = a[f"M{m}_w2"].shape[2]
                sp.dma_start(w1[s][0:a[f"M{m}_w1"].shape[1], :], a[f"M{m}_w1"][bass.ds(e, 1)].rearrange("a p n -> (a p) n"))\
                    .then_inc(w1_in[s], 16)
                if two_slots:
                    sp.wait_ge(y_psum, 2 * last)
                sp.dma_start(w2[s][:, 0:n2], a[f"M{m}_w2"][bass.ds(e, 1)].rearrange("a p n -> (a p) n"))\
                    .then_inc(w2_in[s], 16)

            def load_attn(i):
                if i:
                    sp.dma_start(wqkv[:, i], a[f"A{i}_wqkv"]).then_inc(aw_in[i], 16)
                if ATTN[i]["rel"]:
                    sp.dma_start(bq_col[:, i], a[f"A{i}_bq"]).then_inc(aw_in[i], 16)
                    sp.dma_start(reltab[:, i], a[f"A{i}_reltab"]).then_inc(aw_in[i], 16)
                    sp.dma_start(bqkv[:, i], a[f"A{i}_bqkv"].partition_broadcast(P)).then_inc(aw_in[i], 16)
                    sp.dma_start(bproj[:, i], a[f"A{i}_bproj"].partition_broadcast(P)).then_inc(aw_in[i], 16)
                sp.dma_start(wproj[:, i], a[f"A{i}_wproj"]).then_inc(aw_in[i], 16)

            def load_small(m):
                sp.dma_start(wr[0:a[f"M{m}_wr"].shape[0], m], a[f"M{m}_wr"]).then_inc(mw_in[m], 16)
                if MOE[m]["rbias"]:
                    for t in range(TT):
                        sp.dma_start(rbias[:, m // 4, t], a[f"M{m}_rbias"].partition_broadcast(P)).then_inc(mw_in[m], 16)
                if MOE[m]["b"]:
                    n = MOE[m]["n"]
                    k = (0, 1, None, 2)[m]
                    sp.dma_start(b1[:, k, 0:n * 2 * HB], a[f"M{m}_b1"]).then_inc(mw_in[m], 16)
                    sp.dma_start(b2[0:n, k], a[f"M{m}_b2"]).then_inc(mw_in[m], 16)

            sp.dma_start(x[:, :, :], a["x"].rearrange("(t p) c -> p t c", p=P)).then_inc(x_in, 16)
            sp.dma_start(ident, a["consts"][:, CONST["ident"]]).then_inc(ident_in, 16)
            sp.dma_start(wqkv[:, 0], a["A0_wqkv"]).then_inc(wqkv0_in, 16)
            load_attn(0)
            sp.dma_start(consts[:, P:], a["consts"][:, P:]).then_inc(c_in, 16)
            load_small(0)
            for kind, n in BLOCKS:
                if kind == "attn":
                    if ATTN[n]["rel"]:
                        for t in range(TT):
                            sp.wait_ge(rel_dve, TT * n + t + 1)
                            sp.wait_ge(rel_act, TT * n + t + 1)
                            offsets = sides(n) * REL
                            sp.dma_start(scratch[n, t * P:(t + 1) * P, 0:offsets * NH],
                                         relall[:, t, 0:offsets].rearrange("p r n -> p (r n)")).then_inc(rel_out[t], 16)
                        for t in range(TT):
                            sp.wait_ge(rel_out[t], 16 * (n + 1))
                            for along in range(sides(n)):
                                sp.dma_start(rel[:, t, along].rearrange("p r n -> p (r n)"), rel_ap(n, t, along))\
                                    .then_inc(rel_in[t], 16)
                    if n < 2:
                        for i in range(2):
                            load_expert(n, 0, i)
                        load_attn(n + 1)
                        load_small(n + 1)
                    elif n == 2:
                        load_attn(3)
                        for m in (3, 4):
                            load_small(m)
                        sp.dma_start(lnw[:, :, :], a["lnw"]).then_inc(mw_in[2], 16)
                        for e in range(6):
                            load_expert(2, e // 2, e % 2)
                else:
                    if n > 2:
                        for i in range(2):
                            load_expert(n, 0, i)
                    if n == 2:
                        for e in (6, 7):
                            load_expert(n, e // 2, e % 2)
                        continue
                    with sp.Fori(1, E // 2) as j:
                        for i in range(2):
                            load_expert(n, j, i)
                    if MOE[n]["n"] > E:
                        load_expert(n, E // 2, 0)
            sp.wait_ge(acc_done, 2 * BASE[-1])
            sp.dma_start(out.rearrange("(t p) c -> p t c", p=P), x[:, :, :]).then_inc(y_out, 16)
            sp.wait_ge(y_out, 16)

        @block.gpsimd
        def _(pool):
            def ln(n):
                pool.wait_ge(var_ready, n + 1)
                pool.tensor_tensor(rstd[:, :], var_eps[:, :], minus_half[:, :], ALU.pow).then_inc(rstd_ready, 1)

            pool.memset(minus_half[:, :], -0.5).then_inc(minus_half_ready, 1)
            pool.wait_ge(minus_half_ready, 1)
            ln(0)
            pool.memset(q_st[:, :, :, :], 0.0).then_inc(pool_ready, 1)
            pool.memset(k_st[:, :, :, :], 0.0).then_inc(pool_ready, 1)
            pool.memset(v_st[:, :, :, :], 0.0).then_inc(pool_ready, 1)
            pool.memset(kT[:, :, :, :], 0.0).then_inc(pool_ready, 1)
            pool.memset(gates[:, :, E:E + 1], 1.0).then_inc(pool_ready, 1)
            pool.wait_ge(c_in, 16)
            pool.wait_ge(pool_ready, 2)
            for t in range(TT):
                at = CONST["onehot"].start + t * 2 * SIDE
                oh = consts[:, at:at + 2 * SIDE].unsqueeze(1).broadcast_to([P, NH, 2 * SIDE])
                pool.tensor_copy(k_st[:, t, :, HD:HD + 2 * SIDE], oh).then_inc(kst_ready, 1)
                at = CONST["rowhot"].start + t * SIDE
                oh = consts[:, at:at + SIDE].unsqueeze(1).broadcast_to([P, NH, SIDE])
                pool.tensor_copy(q_st[:, t, :, HD + SIDE:HD + 2 * SIDE], oh).then_inc(kst_ready, 1)

            def attn(n):
                if not ATTN[n]["rel"]:
                    pool.wait_ge(qT_psum, 3 * n)
                    pool.memset(q_st[:, :, :, HD:HD + 2 * SIDE], 0.0).then_inc(q_clear, 1)
                for p in range(PAIRS):
                    g = n * PAIRS + p
                    for t in range(1 if p == 0 else 0, TT):
                        pool.wait_ge(rinv_ready, TT * g + t + 1)
                        keys = keys_of(n, t)
                        pr = probs[:, p % 2, t, :, 0:keys]
                        pool.tensor_tensor(pr, pr, rinv[:, p % 2, t].unsqueeze(2).broadcast_to([P, 2, keys]), ALU.mult)\
                            .then_inc(p_ready, 1)

            def split(m, j, i):
                s = (i + SHIFT[m]) % 2
                g = 2 * j + BASE[m] + i
                very_first = isinstance(g, int) and g == 0
                pool.wait_ge(w2_in[s], 16 * (j + USED[m][s] + 1))
                for b in range(SB):
                    if not very_first:
                        if b < SB - 1:
                            pool.wait_ge(w2_used, g)
                        else:
                            pool.wait_ge(y_psum, 2 * g)
                    at = 2 * (HB - SB + b) * C
                    w = w2[s][:, at:at + 2 * C].rearrange("p (c n) -> p c n", c=2)
                    parts = w2_hl[:, 2 * b:2 * (b + 1)]
                    one = consts[:, CONST["ones"]][:, 0:1].unsqueeze(1).broadcast_to([P, 2, C])
                    pool.tensor_tensor(parts[:, :, 0], w, one, ALU.mult).then_inc(w2_hi_ready, 1)
                    pool.wait_ge(w2_hi_ready, SB * g + b + 1)
                    pool.tensor_tensor(parts[:, :, 1], w, parts[:, :, 0].bitcast(F32), ALU.subtract).then_inc(w2_lo_ready, 1)

            nln = 1
            for kind, n in BLOCKS:
                if kind == "attn":
                    if n == 3:
                        ln(nln)
                        nln += 1
                    if n > 0:
                        ln(nln)
                        nln += 1
                    attn(n)
                else:
                    ln(nln)
                    nln += 1
                    if MOE[n]["split2"]:
                        for i in range(2):
                            split(n, 0, i)
                        with pool.Fori(1, E // 2) as j:
                            for i in range(2):
                                split(n, j, i)
                        if MOE[n]["n"] > E:
                            split(n, E // 2, 0)
                    if n == 2:
                        pool.wait_ge(gates_ready, n + 1)
                        for t in range(TT):
                            pool.wait_ge(disp_ready, t + 1)
                            pool.tensor_tensor(comb[:, t].rearrange("p (e c) -> p e c", e=E),
                                               disp[:, t].rearrange("p (e c) -> p e c", e=E),
                                               gates[:, t, 0:E].unsqueeze(2).broadcast_to([P, E, CAP]), ALU.mult)\
                                .then_inc(comb_ready, 1)

        @block.scalar
        def _(act):
            def x_transposed(k, weight):
                kind, n = BLOCKS[k]
                split_too = kind == "moe" and not MOE[n]["cap"]
                rows = P if split_too else CH
                for t in range(TT if split_too else 0):
                    act.wait_ge(xT_psum, TT * k + t + 1)
                    act.activation(xT_hi[:, :, t * P:(t + 1) * P], ln_bank(t, P), ACT.Copy).then_inc(xT_hi_ready, 1)
                act.wait_ge(xT_psum, TT * k + 1)
                if split_too:
                    act.wait_ge(xT_lo_ready, TT * (split_count(n) - 1) + 1)
                for c in range(KC if weight is not None else 0):
                    act.wait_ge(mw_in[2], 32)
                    ins = act.activation(xT[0:CH, c, 0:P], ln_bank(0, CH)[:, c], ACT.Copy, scale=lnw[:, weight, c:c + 1])
                if weight is None:
                    ins = act.activation(xT[0:rows, :, 0:P], ln_bank(0, rows), ACT.Copy)
                ins.then_inc(xT_act, 1)

            def attn(n):
                if ATTN[n]["rel"]:
                    for t in range(TT):
                        act.wait_ge(rel_psum, 4 * n + 2 * t + 2)
                        offsets = sides(n) * REL
                        act.activation(relall[:, t, 0:offsets, NH // 2:NH],
                                       bank[B_REL[2 * t + 1]][:, 0:offsets * NH // 2].rearrange("p (r n) -> p r n", n=NH // 2),
                                       ACT.Copy).then_inc(rel_act, 1)
                if n == 0:
                    act.wait_ge(pool_ready, 4)
                    for i in range(4):
                        act.wait_ge(kw_psum, i + 1)
                        act.activation(kw_rows(i, 0), kw_bank(i, HD + SIDE), ACT.Copy).then_inc(kw_act, 1)
                rows = HD + SIDE if n == 0 else SLOT
                for b in range(3):
                    act.wait_ge(kT_psum, 3 * n + b + 1)
                    act.activation(kT[0:rows, 2 * b:2 * b + 2, 0, :],
                                   bank[B_KT[b]][0:rows, :].rearrange("p (a t) -> p a t", a=2), ACT.Copy).then_inc(kT_act, 1)
                for b in (0, 2):
                    act.wait_ge(qT_psum, 3 * n + b + 1)
                    act.activation(qT[:, 2 * b:2 * b + 2, :].rearrange("p a t -> p (a t)"), bank[B_QT[b]][:, :], ACT.Copy).then_inc(qT_act, 1)

                def exps(p):
                    for t in range(TT):
                        act.wait_ge(nmax_ready, 2 * (n * PAIRS + p) + t + 1)
                        for h in range(2):
                            act.activation(probs[:, p % 2, t, h, 0:keys_of(n, t)], scores_bank(n, p, t)[:, h], ACT.Exp,
                                           bias=nmax[:, p % 2, t, h:h + 1],
                                           accum_out=rsum[:, p % 2, t, h:h + 1]).then_inc(exp_ready, 1)

                def outputs(g):
                    act.wait_ge(o_psum, n * PAIRS + 2 * (g + 1))
                    act.activation(oT[:, g, :], bank[B_O[g]][:, 0:T], ACT.Copy).then_inc(o_ready, 1)

                exps(0)
                exps(1)
                for p in range(PAIRS):
                    act.wait_ge(pT_psum, n * PAIRS + p + 1)
                    act.activation(pT[:, p % 2, 0].rearrange("p h t -> p (h t)"), bank[B_PT[0]][:, :], ACT.Copy).then_inc(pT_act, 1)
                    if p + 2 < PAIRS:
                        exps(p + 2)
                    if p and p % 2 == 0:
                        outputs(p // 2 - 1)
                outputs(GROUPS - 1)

            def split(m, j, i, b):
                s = (i + SHIFT[m]) % 2
                if b == 0:
                    act.wait_ge(w1_in[s], 16 * (j + USED[m][s] + 1))
                act.activation(w1_cols(w1_hi, b), w1_cols(w1[s], b), ACT.Copy).then_inc(w1_hi_ready, 1)

            def places():
                act.wait_ge(xd_psum, 1)
                act.activation(xdT[:, 0], bank[B_XD[0]][0:CH, :], ACT.Copy, scale=lnw[:, 1, 0:1]).then_inc(xd_act, 1)

                def gelu(ep):
                    for b in range(2):
                        act.wait_ge(hp_psum, 2 * ep + b + 1)
                        if ep and b:
                            act.wait_ge(hpT_psum, 2 * ep)
                        act.activation(hplace[:, b * 384:(b + 1) * 384], bank[B_HP[ep % 2][b]][:, 0:384], ACT.Gelu)\
                            .then_inc(hp_ready, 1)

                gelu(0)
                act.wait_ge(combT_psum, 2)
                act.activation(combT[:, 2:4, :].rearrange("p a t -> p (a t)"), bank[B_HT[1]][:, :], ACT.Copy).then_inc(combT_act, 1)
                for ep in range(EP):
                    act.wait_ge(hpT_psum, 2 * ep + 1)
                    act.activation(hplaceT[:, 0:384], bank[B_HT[0]][:, 0:384], ACT.Copy).then_inc(hpT_act, 1)
                    if ep + 1 < EP:
                        gelu(ep + 1)

            def moe(m, k):
                cfg = MOE[m]

                def logit_exps():
                    act.wait_ge(negm_ready, m + 1)
                    for t in range(TT):
                        act.activation(expl[:, t, :], logits[:, t, :], ACT.Exp, bias=nmax_l[:, t:t + 1]).then_inc(expl_ready, 1)

                if cfg["b"]:
                    act.wait_ge(mw_in[m], {0: 48, 1: 80, 3: 48}[m])

                def expert(j, i, last=False):
                    g = BASE[m] + i
                    for b in range(HB):
                        act.wait_ge(h_psum, 3 * (2 * j + g) + b + 1)
                        if cfg["act"] == "glu":
                            act.activation(silu_g[:, b, :], bank[B_H[b]][:, 0:T], ACT.Silu).then_inc(silu_ready, 1)
                        elif not cfg["b"]:
                            act.activation(hid[:, 2 * b:2 * b + 2, :].rearrange("p c t -> p (c t)"), bank[B_H[b]][:, :],
                                           FUNC[cfg["act"]]).then_inc(h_ready, 1)
                        else:
                            kb = (0, 1, None, 2)[m]
                            for c in range(2):
                                at = (2 * j + i) * 2 * HB + 2 * b + c
                                ins = act.activation(hid[:, 2 * b + c, :], bank[B_H[b]][:, c * T:(c + 1) * T],
                                                     FUNC[cfg["act"]], bias=b1[:, kb, bass.ds(at, 1)])
                            ins.then_inc(h_ready, 1)
                        if not cfg["split2"] and not last:
                            split(m, j + i, 1 - i, b)
                    for b in range(HB if cfg["split2"] and not last else 0):
                        split(m, j + i, 1 - i, b)

                if cfg["cap"]:
                    logit_exps()
                    return places()
                expert(0, 0)
                logit_exps()
                expert(0, 1)
                if cfg["b"]:
                    kb = (0, 1, None, 2)[m]
                    act.wait_ge(gT_psum, kb + 1)
                    act.activation(gT[0:cfg["n"], :], bank[B_R][0:cfg["n"], T:2 * T], ACT.Copy).then_inc(gT_ready, 1)
                with act.Fori(1, looped(m)) as j:
                    for i in range(2):
                        expert(j, i)
                if cfg["n"] > E:
                    expert(E // 2, 0, last=True)
                else:
                    expert(E // 2 - 1, 0)
                    expert(E // 2 - 1, 1, last=True)

            k = 0
            for kind, n in BLOCKS:
                if kind == "moe" and n != 2:
                    for b in range(HB):
                        split(n, 0, 0, b)
                x_transposed(k, LN_WEIGHT.get((kind, n)))
                if kind == "attn":
                    attn(n)
                else:
                    moe(n, k)
                k += 1

        @block.tensor
        def _(pe):
            def x_transposed(k, n):
                wide = P if BLOCKS[k][0] == "moe" and BLOCKS[k][1] != 2 else CH
                stay_warm(9 if BLOCKS[k] == ("attn", 3) else 5)
                if k == 0:
                    pe.wait_ge(ident_in, 16)
                for t in range(TT):
                    pe.wait_ge(xn_ready, 2 * n + t + 1)
                    for c in range(KC):
                        ins = pe.transpose(bank[B_LN[t]][0:wide, c * P:(c + 1) * P], xn[:, t, c * wide:(c + 1) * wide], ident)
                    ins.then_inc(xT_psum, 1)
                stay_warm(2 if BLOCKS[k][0] == "moe" else 1)

            def stay_warm(times, b=B_WARM):
                for _ in range(times):
                    pe.matmul(bank[b][:, 0:T], warm[:, 0:P], warm[:, :], start=True, stop=True)

            def attn(n, k):
                if n == 0:
                    pe.wait_ge(wqkv0_in, 16)
                else:
                    pe.wait_ge(aw_in[n], 96 if ATTN[n]["rel"] else 32)
                pe.wait_ge(xT_act, k + 1)
                pe.wait_ge(xT_dve, k + 1)
                if ATTN[n]["rel"]:
                    for h in range(KC):
                        for c in range(KC):
                            ins = pe.matmul(bank[B_QT0[h]][0:CH, 0:T], wqkv[:, n, c, h * CH:(h + 1) * CH],
                                            xT[0:CH, c, :], start=(c == 0), stop=(c == KC - 1))
                        ins.then_inc(qTs_psum, 1)

                def values(*tiles):
                    for t in tiles:
                        for c in range(KC):
                            ins = pe.matmul(bank[B_V][:, t * C:(t + 1) * C], xT[0:CH, c, t * P:(t + 1) * P],
                                            wqkv[:, n, c, 2 * C:3 * C], start=(c == 0), stop=(c == KC - 1))
                        ins.then_inc(v_psum, 1)

                if ATTN[n]["rel"]:
                    values(0)
                    if n == 0:
                        pe.wait_ge(aw_in[0], 80)
                    pe.wait_ge(qTs_ready, 2 * (n + 1))
                    for t in range(TT):
                        for h in range(KC):
                            cols = sides(n) * REL * NH // 2
                            pe.matmul(bank[B_REL[2 * t + h]][:, 0:cols], qTs[:, h, t * P:(t + 1) * P], reltab[:, n, 0:cols],
                                      start=True, stop=True).then_inc(rel_psum, 1)
                    values(1)
                for t in range(TT):
                    for c in range(KC):
                        ins = pe.matmul(bank[B_QK[t]][:, 0:2 * C], xT[0:CH, c, t * P:(t + 1) * P], wqkv[:, n, c, 0:2 * C],
                                        start=(c == 0), stop=(c == KC - 1))
                    ins.then_inc(qk_psum, 1)
                if not ATTN[n]["rel"]:
                    values(0, 1)
                if n == 0:
                    pe.wait_ge(rel_dve, TT)
                    pe.wait_ge(rel_act, TT)
                    for i in range(4):
                        half, key_rows = i // 2, range(i % 2 * (SIDE // 2), (i % 2 + 1) * (SIDE // 2))
                        for kh in key_rows:
                            tokens = qTs[:, half, :].rearrange("p (h w) -> p w h", w=SIDE)[:, kh, :]
                            offsets = reltab[:, 0, (REL + SIDE - 1 - kh) * NH // 2:(REL + 2 * SIDE - 1 - kh) * NH // 2]\
                                .rearrange("p (r a h) -> p h r a", r=SIDE, h=2)
                            for head in range(2):
                                row = head * SLOT + HD + SIDE
                                at = (kh - key_rows[0]) * SIDE
                                ins = pe.matmul(kw_bank(i, row)[:, :, at:at + SIDE].rearrange("p a k -> p k a"), tokens,
                                                offsets[:, head], start=True, stop=True)
                        ins.then_inc(kw_psum, 1)
                if n == 0:
                    pe.wait_ge(kst_ready, 2 * TT)
                pe.wait_ge(k_ready, TT * (n + 1))
                for b in range(3):
                    if b == 1:
                        pe.wait_ge(q_ready, TT * (n + 1))
                    for p in range(2):
                        for t in range(TT):
                            h = 2 * (2 * b + p)
                            ins = pe.transpose(bank[B_KT[b]][:, p * T + t * P:p * T + (t + 1) * P],
                                               k_st[:, t, h:h + 2, :].rearrange("p h s -> p (h s)"), ident)
                    ins.then_inc(kT_psum, 1)
                pe.wait_ge(v_ready, n + 1)
                stay_warm(3 if n < 3 else 0, B_V)
                if n == 0:
                    pe.wait_ge(kw_act, 4)
                    pe.wait_ge(kw_dve, 4)
                if ATTN[n]["rel"]:
                    pe.wait_ge(q_rel_ready, rel_copies(n, TT - 1))
                else:
                    pe.wait_ge(q_clear, 1)
                for b in range(3):
                    for p in range(2):
                        for t in range(TT):
                            h = 2 * (2 * b + p)
                            ins = pe.transpose(bank[B_QT[b]][:, p * T + t * P:p * T + (t + 1) * P],
                                               q_st[:, t, h:h + 2, :].rearrange("p h s -> p (h s)"), ident)
                    ins.then_inc(qT_psum, 1)

                def scores(p):
                    b = p // 2
                    if p == 0:
                        pe.wait_ge(kT_act, 3 * (n + 1))
                        pe.wait_ge(kT_dve, 3 * (n + 1))
                        pe.wait_ge(qT_act, 2 * n + 1)
                    if p == 2:
                        pe.wait_ge(qT_dve, n + 1)
                    if p == 4:
                        pe.wait_ge(qT_act, 2 * n + 2)
                    for t in range(TT):
                        pe.matmul(scores_bank(n, p, t), qT[:, p, t * P:(t + 1) * P], kT[:, p, :, 0:keys_of(n, t)],
                                  start=True, stop=True).then_inc(s_psum, 1)

                def project(g):
                    pe.wait_ge(o_ready, GROUPS * n + g + 1)
                    for t in range(TT):
                        ins = pe.matmul(bank[B_PROJ[t]][:, 0:C], oT[:, g, t * P:(t + 1) * P], wproj[:, n, g, :],
                                        start=(g == 0), stop=(g == GROUPS - 1))
                        if g == GROUPS - 1:
                            ins.then_inc(proj_psum, 1)

                scores(0)
                scores(1)
                def probs_transposed(p):
                    if p:
                        pe.wait_ge(pT_act, n * PAIRS + p)
                        pe.wait_ge(pT_dve, n * PAIRS + p)
                    for t in range(TT):
                        if p == 0 and t == 0:
                            pe.wait_ge(p_ready_dve, n + 1)
                        else:
                            pe.wait_ge(p_ready, (TT * PAIRS - 1) * n + TT * p + t)
                        for h in range(2):
                            for kt in range(keys_of(n, t) // P):
                                ins = pe.transpose(bank[B_PT[kt]][:, h * T + t * P:h * T + (t + 1) * P],
                                                   probs[:, p % 2, t, h, kt * P:(kt + 1) * P], ident)
                    ins.then_inc(pT_psum, 1)

                def values_summed(p):
                    pe.wait_ge(pT_act, n * PAIRS + p + 1)
                    pe.wait_ge(pT_dve, n * PAIRS + p + 1)
                    if p == 4:
                        pe.wait_ge(o_ready, GROUPS * n + 1)
                    for kt in range(TT):
                        for h in range(2):
                            row = 32 * ((2 * p + h) % 4)
                            first_q = kt * P if n == 3 else 0
                            ins = pe.matmul(bank[B_O[p // 2]][row:row + 32, first_q:T], v_st[:, kt, 2 * p + h, :],
                                            pT[:, p % 2, kt, h, first_q:T], start=(kt == 0), stop=(kt == TT - 1),
                                            skip_group_check=(n == 3))
                    ins.then_inc(o_psum, 1)

                pe.wait_ge(qT_dve, n + 1)
                stay_warm(2 if n == 3 else 1, B_PT[0])
                for p in range(PAIRS):
                    if p == 0:
                        probs_transposed(0)
                        scores(2)
                        pe.wait_ge(qT_act, 2 * n + 2)
                        continue
                    if p + 2 < PAIRS:
                        pe.wait_ge(p_ready, (TT * PAIRS - 1) * n + TT * p + 1)
                        scores(p + 2)
                    probs_transposed(p)
                    values_summed(p - 1)
                    if p + 2 >= PAIRS:
                        project(p + 2 - PAIRS)
                values_summed(PAIRS - 1)
                project(GROUPS - 1)

            def places():
                stay_warm(5)
                pe.wait_ge(sel_ready, 1)
                earlier, ones = consts[:, CONST["earlier"]], consts[:, CONST["ones"]]
                pe.matmul(bank[B_R][:, 64:64 + E], earlier, sel[:, 0, :], start=True, stop=True)
                pe.matmul(bank[B_R][:, 64 + E:64 + 2 * E], ones, sel[:, 0, :], start=True, stop=False)
                pe.matmul(bank[B_R][:, 64 + E:64 + 2 * E], earlier, sel[:, 1, :], start=False, stop=True)\
                    .then_inc(pos_psum, 1)
                stay_warm(2)
                for t in range(TT):
                    pe.wait_ge(disp_ready, t + 1)
                    for c in range(KC):
                        ins = pe.matmul(bank[B_XD[c]][0:CH, :], xn[:, t, c * CH:(c + 1) * CH], disp[:, t],
                                        start=(t == 0), stop=(t == TT - 1))
                ins.then_inc(xd_psum, 1)

                def up(ep):
                    for ab in range(2):
                        s = 2 * ep + ab
                        times = (USED[2][s] if s < 2 else 0) + 1
                        pe.wait_ge(w1_in[s], 16 * times)
                        pe.wait_ge(w2_in[s], 16 * times)
                    for b in range(2):
                        for c in range(KC):
                            for ab in range(2):
                                e = 2 * ep + ab
                                ins = pe.matmul(bank[B_HP[ep % 2][b]][ab * CAP:(ab + 1) * CAP, 0:384],
                                                xdT[:, c, e * CAP:(e + 1) * CAP],
                                                w1[e][0:CH, c * 768 + b * 384:c * 768 + (b + 1) * 384],
                                                start=(c == 0), stop=(c == KC - 1))
                        ins.then_inc(hp_psum, 1)

                def add(ep):
                    pe.wait_ge(yp_ready, ep + 1)
                    if ep == 0:
                        pe.wait_ge(combT_act, 1)
                        pe.wait_ge(combT_dve, 1)
                    for t in range(TT):
                        ins = pe.matmul(bank[B_SUM][:, t * C:(t + 1) * C], combT[:, ep, t * P:(t + 1) * P], yplace[:, :],
                                        start=(ep == 0 and t == 0), stop=(ep == EP - 1), skip_group_check=True)
                    if ep == EP - 1:
                        ins.then_inc(sum_psum, 1)

                pe.wait_ge(xd_act, 1)
                pe.wait_ge(xd_dve, 1)
                up(0)
                for t in range(TT):
                    pe.wait_ge(comb_ready, t + 1)
                for b in range(2):
                    for p in range(2):
                        for t in range(TT):
                            ep = 2 * b + p
                            ins = pe.transpose(bank[B_HT[b]][:, p * T + t * P:p * T + (t + 1) * P],
                                               comb[:, t, ep * P:(ep + 1) * P], ident)
                    ins.then_inc(combT_psum, 1)
                for ep in range(EP):
                    if ep + 1 < EP:
                        up(ep + 1)
                    for b in range(2):
                        pe.wait_ge(hp_ready, 2 * ep + b + 1)
                        if ep == 0 and b == 0:
                            pe.wait_ge(combT_dve, 1)
                        if ep == 0 and b == 1:
                            pe.wait_ge(combT_act, 1)
                        for c in range(HB):
                            ins = pe.transpose(bank[B_HT[b]][:, c * P:(c + 1) * P],
                                               hplace[:, (b * HB + c) * P:(b * HB + c + 1) * P], ident)
                        ins.then_inc(hpT_psum, 1)
                    if ep:
                        add(ep - 1)
                    for c in range(2 * HB):
                        if c == 0:
                            pe.wait_ge(hpT_act, ep + 1)
                        if c == HB:
                            pe.wait_ge(hpT_dve, ep + 1)
                        for ab in range(2):
                            ins = pe.matmul(bank[B_YP][ab * CAP:(ab + 1) * CAP, 0:C],
                                            hplaceT[:, c * P + ab * CAP:c * P + (ab + 1) * CAP],
                                            w2[2 * ep + ab][:, c * C:(c + 1) * C],
                                            start=(c == 0), stop=(c == 2 * HB - 1))
                    ins.then_inc(yp_psum, 1)
                add(EP - 1)

            def moe(m, k):
                cfg = MOE[m]
                pe.wait_ge(mw_in[m], {0: 48, 1: 80, 2: 32, 3: 48, 4: 48}[m])

                def router():
                    pe.wait_ge(xT_act, k + 1)
                    pe.wait_ge(xT_dve, k + 1)
                    for t in range(TT):
                        for c in range(KC):
                            rows = CH if cfg["cap"] else (P, CR)[c]
                            ins = pe.matmul(bank[B_R][:, t * E:(t + 1) * E], xT[0:rows, c, t * P:(t + 1) * P],
                                            wr[0:rows, m, c, :], start=(c == 0), stop=(c == KC - 1))
                    ins.then_inc(r_psum, 1)

                def expert(j, i):
                    g = BASE[m] + i
                    s = (i + SHIFT[m]) % 2
                    glu = cfg["act"] == "glu"
                    very_first = isinstance(j, int) and j == 0 and i == 0
                    if very_first:
                        pe.wait_ge(xT_lo_ready, TT * split_count(m))
                    for b in range(HB):
                        if very_first and b == 1:
                            router()
                        pe.wait_ge(w1_lo_ready, 3 * (2 * j + g) + b + 1)
                        for c2 in range(2):
                            at = (2 * b + c2) * P
                            for q, (w, xs) in enumerate(((w1_hi[:, 0, at:at + P], xT_hi[:, 0, :]),
                                                         (w1_hi[:, 0, at:at + P], xT_lo[:, :]),
                                                         (w1_hi[:, 1, at:at + P], xT_hi[:, 1, :]),
                                                         (w1_lo[:, 0, at:at + P], xT_hi[:, 0, :]),
                                                         (w1_lo[0:CR, 1, at:at + P], xT_hi[0:CR, 1, :]))):
                                ins = pe.matmul(bank[B_H[b]][:, c2 * T:(c2 + 1) * T], w, xs, start=(q == 0), stop=(q == 4))
                        ins.then_inc(h_psum, 1)
                    pe.wait_ge(w2_in[s], 16 * (j + USED[m][s] + 1))
                    pe.wait_ge(acc_done, 2 * (2 * j + g))
                    nc2 = HB if glu else 2 * HB
                    plain = nc2 - (SC if cfg["split2"] else 0)
                    for c in range(plain):
                        if glu:
                            pe.wait_ge(glu_ready, 3 * (2 * j + g - BASE[4]) + c + 1)
                        elif c % 2 == 0:
                            pe.wait_ge(h_ready, 3 * (2 * j + g) + c // 2 + 1)
                        for t in range(TT):
                            ins = pe.matmul(bank[B_Y[t]][:, 0:C], hid[:, c, t * P:(t + 1) * P], w2[s][:, c * C:(c + 1) * C],
                                            start=(c == 0), stop=(c == nc2 - 1), skip_group_check=cfg["split2"])
                            if c == nc2 - 1:
                                ins.then_inc(y_psum, 1)
                    for c in range(nc2 - plain):
                        if c % 2 == 0:
                            pe.wait_ge(hid_lo_ready, SB * (2 * j + g) + c // 2 + 1)
                            pe.wait_ge(w2_lo_ready, SB * (2 * j + g) + c // 2 + 1)
                        for t in range(TT):
                            tok = slice(t * P, (t + 1) * P)
                            out = bank[B_Y[t]]
                            pe.matmul(out[:, 0:2 * C], hid_hi[:, c, tok], w2_hl[:, c].rearrange("p a n -> p (a n)"),
                                      start=False, stop=(c == SC - 1), skip_group_check=True)
                            ins = pe.matmul(out[:, 0:C], hid_lo[:, c, tok], w2_hl[:, c, 0], start=False, stop=(c == SC - 1),
                                            skip_group_check=True)
                            if c == SC - 1:
                                ins.then_inc(y_psum, 1)
                        if c == 1:
                            ins.then_inc(w2_used, 1)

                if cfg["cap"]:
                    router()
                    return places()
                for i in range(2):
                    expert(0, i)
                n = cfg["n"]
                if cfg["b"]:
                    pe.wait_ge(gates_ready, m + 1)
                    for t in range(TT):
                        ins = pe.transpose(bank[B_R][0:n, T + t * P:T + (t + 1) * P], gates[:, t, 0:n], ident)
                    ins.then_inc(gT_psum, 1)
                with pe.Fori(1, looped(m)) as j:
                    for i in range(2):
                        expert(j, i)
                if cfg["b"]:
                    kb = (0, 1, None, 2)[m]
                    pe.wait_ge(gT_ready, kb + 1)
                    for t in range(TT):
                        ins = pe.matmul(bank[B_B2][:, t * C:(t + 1) * C], gT[0:n, t * P:(t + 1) * P], b2[0:n, kb, :],
                                        start=True, stop=True)
                    ins.then_inc(b2_psum, 1)
                for e in range(2 * looped(m), n):
                    expert(e // 2, e % 2)

            pe.wait_ge(warm_ready, 1)
            nln = 0
            for k, (kind, n) in enumerate(BLOCKS):
                if (kind, n) == ("attn", 3):
                    nln += 1
                x_transposed(k, nln)
                nln += 1
                (attn if kind == "attn" else moe)(n, k)

        @block.vector
        def _(dve):
            own = [0]

            def then(ins):
                own[0] += 1
                ins.then_inc(dve_own, 1)

            def settle():
                dve.wait_ge(dve_own, own[0])

            def ln(n, src, eps, dst=xn, twice=False, m=None, src_at=None):
                for t in range(TT):
                    if src_at is not None:
                        dve.wait_ge(dve_own, src_at[t])
                    then(dve.bn_stats(stats[:, t, :], src[:, t, :]))
                settle()
                for t in range(TT):
                    then(dve.bn_aggr(moments[:, t, :], stats[:, t, :]))
                settle()
                dve.tensor_scalar(var_eps[:, :], moments[:, :, 1], eps, None, ALU.add).then_inc(var_ready, 1)
                if m is not None:
                    split(m, 0, 0, 0)
                dve.wait_ge(rstd_ready, n + 1)
                for t in range(TT):
                    ins = dve.tensor_scalar(dst[:, t, 0:C], src[:, t, :], moments[:, t, 0:1], rstd[:, t:t + 1],
                                            ALU.subtract, ALU.mult)
                    if twice:
                        ins = dve.tensor_scalar(dst[:, t, C:], src[:, t, P:], moments[:, t, 0:1], rstd[:, t:t + 1],
                                                ALU.subtract, ALU.mult)
                    ins.then_inc(xn_ready, 1)

            def x_transposed(k, weight):
                kind, n = BLOCKS[k]
                split_too = kind == "moe" and not MOE[n]["cap"]
                rows = P if split_too else CH
                for t in range(TT if split_too else 0):
                    dve.wait_ge(xT_hi_ready, TT * (split_count(n) - 1) + t + 1)
                    tok = slice(t * P, (t + 1) * P)
                    dve.tensor_tensor(xT_lo[:, tok], ln_bank(t, P)[:, 0], xT_hi[:, 0, tok].bitcast(F32), ALU.subtract)
                    dve.tensor_tensor(xT_hi[CR:P, 1, tok], ln_bank(t, P)[CR:P, 1], xT_hi[CR:P, 1, tok].bitcast(F32), ALU.subtract)\
                        .then_inc(xT_lo_ready, 1)
                dve.wait_ge(xT_psum, TT * (k + 1))
                for c in range(KC if weight is not None else 0):
                    dve.wait_ge(mw_in[2], 32)
                    ins = dve.tensor_scalar(xT[0:CH, c, P:T], ln_bank(1, CH)[:, c], lnw[:, weight, c:c + 1], None, ALU.mult)
                if weight is None:
                    ins = dve.tensor_copy(xT[0:rows, :, P:T], ln_bank(1, rows))
                ins.then_inc(xT_dve, 1)

            def attn(n):
                src = tln if n == 3 else x
                scale = float(HD) ** -0.5
                heads = "p (h d) -> p h d"
                if ATTN[n]["rel"]:
                    dve.wait_ge(aw_in[n], 96 if n else 80)
                    then(dve.tensor_scalar(bq4[:, n, :], bqkv[:, n, 0:C], scale, None, ALU.mult))
                    for h in range(KC):
                        dve.wait_ge(qTs_psum, KC * n + h + 1)
                        dve.tensor_scalar(qTs[:, h, :], bank[B_QT0[h]][0:CH, 0:T], bq_col[:, n, h:h + 1], None, ALU.add)\
                            .then_inc(qTs_ready, 1)
                    settle()
                if n == 0:
                    dve.wait_ge(pool_ready, 5)
                def values():
                    dve.wait_ge(v_psum, TT * (n + 1))
                    for t in range(TT):
                        vp = bank[B_V][:, t * C:(t + 1) * C].rearrange(heads, h=NH)
                        if ATTN[n]["rel"]:
                            ins = dve.tensor_tensor(v_st[:, t, :, 0:HD], vp, bqkv[:, n, 2 * C:3 * C].rearrange(heads, h=NH), ALU.add)
                        else:
                            ins = dve.tensor_copy(v_st[:, t, :, 0:HD], vp)
                    ins.then_inc(v_ready, 1)

                if ATTN[n]["rel"]:
                    for t in range(TT):
                        dve.wait_ge(rel_psum, 4 * n + 2 * t + 1)
                        offsets = sides(n) * REL
                        dve.tensor_copy(relall[:, t, 0:offsets, 0:NH // 2],
                                        bank[B_REL[2 * t]][:, 0:offsets * NH // 2].rearrange("p (r n) -> p r n", n=NH // 2))\
                            .then_inc(rel_dve, 1)
                    values()
                for t in range(TT):
                    dve.wait_ge(qk_psum, TT * n + t + 1)
                    kp = bank[B_QK[t]][:, C:2 * C].rearrange(heads, h=NH)
                    if ATTN[n]["rel"]:
                        ins = dve.tensor_tensor(k_st[:, t, :, 0:HD], kp, bqkv[:, n, C:2 * C].rearrange(heads, h=NH), ALU.add)
                    else:
                        ins = dve.tensor_copy(k_st[:, t, :, 0:HD], kp)
                    ins.then_inc(k_ready, 1)
                for t in range(TT):
                    qp = bank[B_QK[t]][:, 0:C].rearrange(heads, h=NH)
                    if ATTN[n]["rel"]:
                        ins = dve.scalar_tensor_tensor(q_st[:, t, :, 0:HD], qp, scale, bq4[:, n, :].rearrange(heads, h=NH),
                                                       ALU.mult, ALU.add)
                    else:
                        ins = dve.tensor_scalar(q_st[:, t, :, 0:HD], qp, scale, None, ALU.mult)
                    ins.then_inc(q_ready, 1)
                if not ATTN[n]["rel"]:
                    values()
                for i in range(4 if n == 0 else 0):
                    dve.wait_ge(kw_psum, i + 1)
                    dve.tensor_copy(kw_rows(i, 1), kw_bank(i, SLOT + HD + SIDE)).then_inc(kw_dve, 1)
                rows = HD + SIDE if n == 0 else SLOT
                for b in range(3):
                    dve.wait_ge(kT_psum, 3 * n + b + 1)
                    dve.tensor_copy(kT[SLOT:SLOT + rows, 2 * b:2 * b + 2, 1, :],
                                    bank[B_KT[b]][SLOT:SLOT + rows, :].rearrange("p (a t) -> p a t", a=2)).then_inc(kT_dve, 1)
                for t in range(TT if ATTN[n]["rel"] else 0):
                    dve.wait_ge(rel_in[t], 16 * sum(sides(i) for i in range(n + 1)))
                    for along in range(sides(n)):
                        dve.tensor_copy(q_st[:, t, :, HD + along * SIDE:HD + (along + 1) * SIDE],
                                        rel[:, t, along].rearrange("p r n -> p n r")).then_inc(q_rel_ready, 1)
                if ATTN[n]["rel"]:
                    for t in range(TT):
                        then(dve.tensor_tensor(xb[:, t, :], src[:, t, :], bproj[:, n, :], ALU.add))
                dve.wait_ge(qT_psum, 3 * n + 2)
                dve.tensor_copy(qT[:, 2:4, :].rearrange("p a t -> p (a t)"), bank[B_QT[1]][:, :]).then_inc(qT_dve, 1)

                def row_max(p, *tiles):
                    for t in tiles or range(TT):
                        dve.wait_ge(s_psum, 2 * (n * PAIRS + p) + t + 1)
                        s = scores_bank(n, p, t)
                        if n == 3:
                            mask = consts[:, CONST["causal"]].unsqueeze(1).broadcast_to([P, 2, P])
                            own_keys = s[:, :, t * P:(t + 1) * P]
                            then(dve.tensor_tensor(own_keys, own_keys, mask, ALU.add))
                            settle()
                        dve.tensor_reduce(nmax[:, p % 2, t, :], s, AX.X, ALU.max, negate=True).then_inc(nmax_ready, 1)

                def recip(p, t):
                    dve.wait_ge(exp_ready, 4 * (n * PAIRS + p) + 2 * (t + 1))
                    dve.reciprocal(rinv[:, p % 2, t], rsum[:, p % 2, t]).then_inc(rinv_ready, 1)

                row_max(0)
                row_max(1, 0)
                recip(0, 0)
                dve.wait_ge(rinv_ready, TT * n * PAIRS + 1)
                keys = keys_of(n, 0)
                pr = probs[:, 0, 0, :, 0:keys]
                dve.tensor_tensor(pr, pr, rinv[:, 0, 0].unsqueeze(2).broadcast_to([P, 2, keys]), ALU.mult)\
                    .then_inc(p_ready_dve, 1)
                recip(0, 1)
                row_max(1, 1)
                for p in range(PAIRS):
                    if p + 1 < PAIRS:
                        for t in range(TT):
                            recip(p + 1, t)
                    if p and p + 2 < PAIRS:
                        row_max(p + 2)
                    dve.wait_ge(pT_psum, n * PAIRS + p + 1)
                    first_q = P if n == 3 else 0
                    dve.tensor_copy(pT[:, p % 2, 1, :, first_q:T],
                                    bank[B_PT[1]][:, :].rearrange("p (h t) -> p h t", h=2)[:, :, first_q:T]).then_inc(pT_dve, 1)
                    if p == 0:
                        row_max(2)
                settle()
                at = []
                for t in range(TT):
                    dve.wait_ge(proj_psum, TT * n + t + 1)
                    then(dve.tensor_tensor((tln if n == 3 else x)[:, t], bank[B_PROJ[t]][:, 0:C], (tln if n == 3 else xb)[:, t], ALU.add))
                    at.append(own[0])
                return at

            def split(m, j, i, b):
                s = (i + SHIFT[m]) % 2
                dve.wait_ge(w1_hi_ready, 3 * (2 * j + BASE[m] + i) + b + 1)
                dve.tensor_tensor(w1_cols(w1_lo, b), w1_cols(w1[s], b), w1_cols(w1_hi, b).bitcast(F32), ALU.subtract)\
                    .then_inc(w1_lo_ready, 1)

            def moe(m):
                cfg = MOE[m]
                iota = consts[:, CONST["iota"]]

                dve.wait_ge(r_psum, m + 1)
                lp = bank[B_R][:, 0:TT * E].rearrange("p (t e) -> p t e", t=TT)
                if cfg["rbias"]:
                    dve.wait_ge(mw_in[m], {1: 80, 4: 48}[m])
                    then(dve.tensor_tensor(logits[:, :, :], lp, rbias[:, m // 4], ALU.add))
                else:
                    then(dve.tensor_copy(logits[:, :, :], lp))
                settle()
                for t in range(TT):
                    then(dve.max(top8[:, t, :], logits[:, t, :]))
                settle()
                dve.tensor_scalar(nmax_l[:, :], top8[:, :, 0], -1.0, None, ALU.mult).then_inc(negm_ready, 1)
                for t in range(TT):
                    then(dve.max_index(top_i[:, t, :], top8[:, t, :], logits[:, t, :]))
                settle()
                then(dve.tensor_copy(top_f[:, :, :], top_i[:, :, 0:2]))
                settle()
                for t in range(TT):
                    then(dve.tensor_scalar(first[:, t, :], iota, top_f[:, t, 0:1], None, ALU.is_equal))
                settle()
                for t in range(TT):
                    ins = dve.scalar_tensor_tensor(sel[:, t, :], iota, top_f[:, t, 1:2], first[:, t, :], ALU.is_equal, ALU.add)
                    if cfg["cap"] and t:
                        ins.then_inc(sel_ready, 1)
                    else:
                        then(ins)
                settle()
                if cfg["cap"]:
                    dve.wait_ge(sel_ready, 1)
                if cfg["cap"]:
                    dve.wait_ge(pos_psum, 1)
                    then(dve.scalar_tensor_tensor(place[:, :, :], bank[B_R][:, 64:64 + TT * E].rearrange("p (t e) -> p t e", t=TT),
                                                  1.0, sel[:, :, :], ALU.add, ALU.mult))
                    settle()
                    for t in range(TT):
                        dve.tensor_tensor(disp[:, t].rearrange("p (e c) -> p e c", e=E),
                                          consts[:, CONST["places"]].unsqueeze(1).broadcast_to([P, E, CAP]),
                                          place[:, t, :].unsqueeze(2).broadcast_to([P, E, CAP]), ALU.is_equal)\
                            .then_inc(disp_ready, 1)
                def gate():
                    dve.wait_ge(expl_ready, 2 * (m + 1))
                    then(dve.tensor_tensor(chosen[:, :, :], expl[:, :, :], sel[:, :, :], ALU.mult))
                    settle()
                    then(dve.tensor_reduce(den[:, :], (expl if cfg["over_all"] else chosen)[:, :, :], AX.X, ALU.add))
                    settle()
                    then(dve.reciprocal(rden[:, :], den[:, :]))
                    settle()
                    for t in range(TT):
                        ins = dve.tensor_scalar(gates[:, t, 0:E], chosen[:, t, :], rden[:, t:t + 1], None, ALU.mult)
                        if t == 0:
                            then(ins)
                    ins.then_inc(gates_ready, 1)
                    settle()
                    dve.wait_ge(gates_ready, m + 1)

                def hidden(j, i, last=False):
                    for b in range(HB):
                        if cfg["act"] == "glu":
                            dve.wait_ge(silu_ready, 3 * (2 * j + i) + b + 1)
                            dve.tensor_tensor(hid[:, b, :], silu_g[:, b, :], bank[B_H[b]][:, T:2 * T], ALU.mult)\
                                .then_inc(glu_ready, 1)
                        if cfg["split2"] and b >= HB - SB:
                            part = b - (HB - SB)
                            sb2 = 2 * part
                            dve.wait_ge(h_ready, 3 * (2 * j + BASE[m] + i) + b + 1)
                            dve.tensor_copy(hid_hi[:, sb2:sb2 + 2, :], hid[:, 2 * b:2 * b + 2, :]).then_inc(hid_hi_ready, 1)
                            dve.wait_ge(hid_hi_ready, SB * (2 * j + BASE[m] + i) + part + 1)
                            dve.tensor_tensor(hid_lo[:, sb2:sb2 + 2, :], hid[:, 2 * b:2 * b + 2, :],
                                              hid_hi[:, sb2:sb2 + 2, :].bitcast(F32), ALU.subtract).then_inc(hid_lo_ready, 1)
                        if not cfg["split2"] and not last:
                            split(m, j + i, 1 - i, b)
                    for b in range(HB if cfg["split2"] and not last else 0):
                        split(m, j + i, 1 - i, b)

                def add(j, i):
                    g = BASE[m] + i
                    for t in range(TT if cfg["split2"] else 0):
                        dve.wait_ge(y_psum, 2 * (2 * j + g) + t + 1)
                        dve.scalar_tensor_tensor(x[:, t, :], bank[B_Y[t]][:, C:2 * C], gates[:, t, bass.ds(2 * j + i, 1)],
                                                 x[:, t, :], ALU.mult, ALU.add).then_inc(acc_part, 1)
                    for t in range(TT):
                        dve.wait_ge(y_psum, 2 * (2 * j + g) + t + 1)
                        if cfg["split2"]:
                            dve.wait_ge(acc_part, 2 * (2 * j + g) + t + 1)
                        dve.scalar_tensor_tensor(x[:, t, :], bank[B_Y[t]][:, 0:C], gates[:, t, bass.ds(2 * j + i, 1)],
                                                 x[:, t, :], ALU.mult, ALU.add).then_inc(acc_done, 1)

                if cfg["cap"]:
                    gate()
                    then(dve.tensor_tensor(x[:, :, :], x[:, :, :], tln[:, :, :], ALU.add))
                    dve.wait_ge(xd_psum, 1)
                    dve.tensor_scalar(xdT[:, 1], bank[B_XD[1]][0:CH, :], lnw[:, 1, 1:2], None, ALU.mult).then_inc(xd_dve, 1)
                    dve.wait_ge(combT_psum, 1)
                    dve.tensor_copy(combT[:, 0:2, :].rearrange("p a t -> p (a t)"), bank[B_HT[0]][:, :]).then_inc(combT_dve, 1)
                    for ep in range(EP):
                        dve.wait_ge(hpT_psum, 2 * ep + 2)
                        dve.tensor_copy(hplaceT[:, 384:768], bank[B_HT[1]][:, 0:384]).then_inc(hpT_dve, 1)
                        dve.wait_ge(yp_psum, ep + 1)
                        dve.tensor_copy(yplace[:, :], bank[B_YP][:, 0:C]).then_inc(yp_ready, 1)
                    dve.wait_ge(sum_psum, 1)
                    settle()
                    then(dve.tensor_tensor(x[:, :, :], bank[B_SUM][:, 0:TT * C].rearrange("p (t c) -> p t c", t=TT), x[:, :, :], ALU.add))
                    settle()
                    return
                for i in range(2):
                    hidden(0, i)
                    if i == 0:
                        gate()
                    add(0, i)
                with dve.Fori(1, looped(m)) as j:
                    for i in range(2):
                        hidden(j, i)
                        add(j, i)
                if cfg["b"]:
                    k = (0, 1, None, 2)[m]
                    dve.wait_ge(b2_psum, k + 1)
                    dve.wait_ge(acc_done, 2 * (BASE[m] + 2 * looped(m)))
                    then(dve.tensor_tensor(x[:, :, :], bank[B_B2][:, 0:TT * C].rearrange("p (t c) -> p t c", t=TT), x[:, :, :], ALU.add))
                    settle()
                for e in range(2 * looped(m), cfg["n"]):
                    hidden(e // 2, e % 2, last=e == cfg["n"] - 1)
                    add(e // 2, e % 2)
                dve.wait_ge(acc_done, 2 * BASE[m + 1])

            dve.memset(warm[:, :], 1.0).then_inc(warm_ready, 1)
            dve.wait_ge(x_in, 16)
            nln, at = 0, None
            for k, (kind, n) in enumerate(BLOCKS):
                if (kind, n) == ("attn", 3):
                    ln(nln, x, 1e-5, tln, src_at=at)
                    nln += 1
                    dve.wait_ge(xn_ready, 2 * nln)
                    ln(nln, tln, 1e-5)
                elif (kind, n) == ("moe", 2):
                    ln(nln, tln, 1e-5, src_at=at)
                else:
                    ln(nln, x, (ATTN if kind == "attn" else MOE)[n]["eps"], twice=kind == "moe", m=n if kind == "moe" else None,
                       src_at=at)
                nln += 1
                x_transposed(k, LN_WEIGHT.get((kind, n)))
                for b in range(1, HB if kind == "moe" and n != 2 else 1):
                    split(n, 0, 0, b)
                at = (attn if kind == "attn" else moe)(n)


def _layout(i):
    import numpy as np

    def rows(w):
        return np.ascontiguousarray(w.reshape(KC, CH, -1).transpose(1, 0, 2))

    def heads_padded(w):
        p = np.zeros((GROUPS, 4, 32, w.shape[1]), w.dtype)
        p[:, :, :HD] = w.reshape(GROUPS, 4, HD, -1)
        return np.ascontiguousarray(p.reshape(GROUPS, P, -1).transpose(1, 0, 2))

    def rel_table(th, tw, n):
        t = np.zeros((NH // KC, HD, RELS, NH // KC), th.dtype)
        tw = tw[:REL]
        both = np.concatenate([th[:REL], tw if n else tw[::-1]], 0).T
        for h in range(NH // KC):
            t[h, :, :, h] = both
        return np.ascontiguousarray(t.reshape(CH, RELH))

    def rows_twice(w):
        return np.ascontiguousarray(np.stack([w[:P], np.concatenate([w[P:], w[P:]], 0)], 1))

    def up_twice(w):
        return np.stack([rows_twice(v).reshape(P, -1) for v in w], 0)

    def up(w):
        return np.ascontiguousarray(w.reshape(w.shape[0], KC, CH, -1).transpose(0, 2, 1, 3).reshape(w.shape[0], CH, -1))

    def down(w):
        n = w.shape[0]
        return np.ascontiguousarray(w.reshape(n, -1, P, C).transpose(0, 2, 1, 3).reshape(n, P, -1))

    def cols(b):
        return np.ascontiguousarray(b.reshape(b.shape[0], -1, P).transpose(2, 0, 1).reshape(P, -1))

    a = {"x": i["x"].reshape(T, C)}
    qkv = [np.concatenate([i[f"L0_conv_w{n}"].reshape(C, C).T for n in "qkv"], 1), i["L1_conv_qkv_w"],
           i["L2_conv_qkv_w"], i["L2_ffn_c_attn_w"].T]
    bias = [np.concatenate([i[f"L0_conv_b{n}"].reshape(C) for n in "qkv"]), i["L1_conv_qkv_b"], i["L2_conv_qkv_b"]]
    proj = [i["L0_conv_proj_w"].T, i["L1_conv_proj_w"], i["L2_conv_proj_w"], i["L2_ffn_c_proj_w"].T]
    for n in range(4):
        a[f"A{n}_wqkv"] = rows(qkv[n])
        a[f"A{n}_wproj"] = heads_padded(proj[n])
        if n < 3:
            a[f"A{n}_bqkv"] = bias[n]
            a[f"A{n}_bproj"] = i[f"L{n}_conv_proj_b"]
            a[f"A{n}_bq"] = np.ascontiguousarray(bias[n][:C].reshape(KC, CH).T)
            a[f"A{n}_reltab"] = rel_table(i[f"L{n}_conv_rel_pos_h"], i[f"L{n}_conv_rel_pos_w"], n)
    w1 = [i["L0_ffn_W1"], i["L1_ffn_Wfc"], i["L2_ffn_c_fc"],
          np.concatenate([i["L3_conv_w1"], i["L3_conv_ws1"][None]], 0).transpose(0, 2, 1)]
    w2 = [i["L0_ffn_W2"], i["L1_ffn_Wproj"], i["L2_ffn_c_proj_e"],
          np.concatenate([i["L3_conv_w2"], i["L3_conv_ws2"][None]], 0).transpose(0, 2, 1)]
    gu = [np.concatenate([i[f"L3_ffn_{n}_r"], i[f"L3_ffn_{n}_s"]], 0).reshape(E + 1, C, HB, 1, P) for n in ("Wg", "Wu")]
    w1.append(np.concatenate(gu, 3).reshape(E + 1, C, 2 * HB * P))
    w2.append(np.concatenate([i["L3_ffn_Wd_r"], i["L3_ffn_Wd_s"]], 0))
    wr = [i["L0_ffn_Wg"], i["L1_ffn_Wr"], i["L2_ffn_w_g"].T, i["L3_conv_gate_w"].T, i["L3_ffn_W_router"]]
    for m in range(5):
        a[f"M{m}_w1"], a[f"M{m}_wr"] = (up(w1[m]), rows(wr[m])) if MOE[m]["cap"] else (up_twice(w1[m]), rows_twice(wr[m]))
        a[f"M{m}_w2"] = down(w2[m])
    a["M1_rbias"], a["M4_rbias"] = i["L1_ffn_br"], i["L3_ffn_expert_bias"]
    a["M0_b1"], a["M0_b2"] = cols(i["L0_ffn_b1"]), i["L0_ffn_b2"]
    a["M1_b1"], a["M1_b2"] = cols(i["L1_ffn_bfc"]), i["L1_ffn_bproj"]
    a["M3_b1"] = cols(np.concatenate([i["L3_conv_b1"], i["L3_conv_bs1"][None]], 0))
    a["M3_b2"] = np.concatenate([i["L3_conv_b2"], i["L3_conv_bs2"][None]], 0)
    a["lnw"] = np.ascontiguousarray(np.stack([i["L2_ffn_ln1_w"], i["L2_ffn_ln2_w"]], 0).reshape(2, KC, CH).transpose(2, 0, 1))
    c = np.zeros((P, CONST_W), np.float32)
    c[:, CONST["ident"]] = np.eye(P)
    c[:, CONST["earlier"]] = np.triu(np.ones((P, P)), 1)
    c[:, CONST["ones"]] = 1.0
    c[:, CONST["iota"]] = np.arange(E)
    c[:, CONST["places"]] = np.arange(1, CAP + 1)
    tok = np.arange(T)
    hot = np.zeros((T, 2, SIDE), np.float32)
    hot[tok, 0, SIDE - 1 - tok // SIDE] = 1.0
    hot[tok, 1, SIDE - 1 - tok % SIDE] = 1.0
    c[:, CONST["onehot"]] = hot.reshape(TT, P, 2 * SIDE).transpose(1, 0, 2).reshape(P, -1)
    row = (tok[:, None] // SIDE == np.arange(SIDE)).astype(np.float32)
    c[:, CONST["rowhot"]] = row.reshape(TT, P, SIDE).transpose(1, 0, 2).reshape(P, -1)
    c[:, CONST["causal"]] = np.where(tok[None, :P] > tok[:P, None], np.float32(NEG), np.float32(0.0))
    a["consts"] = c
    return a


def kernel(**inputs):
    import numpy as _np
    import concourse.bacc as _bacc
    from concourse import mybir as _mybir
    from concourse.bass_utils import run_bass_kernel_spmd as _run

    nc = _bacc.Bacc("TRN2", target_bir_lowering=False, num_devices=1)
    arrays, args = {}, {}
    for name, v in _layout({k: _np.asarray(v) for k, v in inputs.items()}).items():
        v = _np.ascontiguousarray(v)
        arrays[f"in_{name}_dram"] = v
        args[name] = nc.dram_tensor(f"in_{name}_dram", v.shape, _mybir.dt.from_np(v.dtype), kind="ExternalInput").ap()
    out = nc.dram_tensor("out_dram", (T, C), F32, kind="ExternalOutput").ap()
    metaformer_kernel(nc, args, out)
    r = _run(nc, [arrays], core_ids=[0])
    return r.results[0]["out_dram"].reshape(1, SIDE, SIDE, C)
```
